# Optimizing a Trainium2 kernel written in Bass

```python
import numpy as np
import jax
import jax.numpy as jnp

def _softmax(x, axis=-1):
    return jax.nn.softmax(x, axis=axis)

def _gelu(x):
    return jax.nn.gelu(x, approximate=True)

def _silu(x):
    return jax.nn.silu(x)

def _sigmoid(x):
    return jax.nn.sigmoid(x)

def _layernorm(x, axis=-1, eps=1e-05):
    m = jnp.mean(x, axis=axis, keepdims=True)
    v = jnp.var(x, axis=axis, keepdims=True)
    return (x - m) / jnp.sqrt(v + eps)

def _scatter_add(tgt, idx, src, axis=0):
    return tgt.at[idx].add(src)

def _segment_sum(src, seg, n):
    return jax.ops.segment_sum(src, seg, n)
kernel_name = 'mk_cond_seq_d4_seqx_r4_e9a80c'

def setup_inputs(seed: int=0):
    np.random.seed(seed)
    _w = jnp.asarray

    def _rec_inputs():
        import jax
        import jax.numpy as jnp
        _rk = jax.random.key(seed)
        x = 1.648e-05 + 1 * jax.random.normal(jax.random.fold_in(_rk, 1), (4, 512, 288), jnp.float32)
        _lenS = 512 - jax.random.randint(jax.random.fold_in(_rk, 7), (4,), 0, max(1, 512 // 4) + 1, jnp.int32)
        _lenS2 = 512 - jax.random.randint(jax.random.fold_in(_rk, 8), (4,), 0, max(1, 512 // 4) + 1, jnp.int32)
        cond_1152 = 0.00914911 + 1.00357 * jax.random.normal(jax.random.fold_in(_rk, 11), (4, 288), jnp.float32)
        return (x, cond_1152)
    x, cond_1152 = _rec_inputs()

    def _L0_cond_setup():
        import jax, jax.numpy as jnp
        import numpy as np
        NUM_HEADS = 16
        NUM_EXPERTS = 4
        TOP_K = 2
        LN_EPS = 1e-06

        def _ln(h):
            mu = jnp.mean(h, axis=-1, keepdims=True)
            var = jnp.var(h, axis=-1, keepdims=True)
            return (h - mu) * jax.lax.rsqrt(var + LN_EPS)

        def _modulate(h, shift, scale):
            return h * (1.0 + scale[:, None, :]) + shift[:, None, :]
        key = jax.random.key(seed)
        ks = jax.random.split(key, 12)
        B, N, C = (8, 256, 288)
        H = 4 * C
        E = NUM_EXPERTS
        s = 0.02
        return {'x': jax.random.normal(ks[0], (B, N, C), jnp.float32), 'c': jax.random.normal(ks[1], (B, C), jnp.float32), 'w_adaln': jax.random.normal(ks[2], (C, 6 * C), jnp.float32) * s, 'b_adaln': jnp.zeros((6 * C,), jnp.float32), 'w_qkv': jax.random.normal(ks[3], (C, 3 * C), jnp.float32) * s, 'b_qkv': jnp.zeros((3 * C,), jnp.float32), 'w_proj': jax.random.normal(ks[4], (C, C), jnp.float32) * s, 'b_proj': jnp.zeros((C,), jnp.float32), 'w_gate': jax.random.normal(ks[5], (C, E), jnp.float32) * s, 'w1': jax.random.normal(ks[6], (E, C, H), jnp.float32) * s, 'b1': jnp.zeros((E, H), jnp.float32), 'w2': jax.random.normal(ks[7], (E, H, C), jnp.float32) * s, 'b2': jnp.zeros((E, C), jnp.float32)}
    _L0_cond_all = _L0_cond_setup()
    _L0_cond_in = {k: v for k, v in _L0_cond_all.items() if k in ('w_adaln', 'b_adaln', 'w_qkv', 'b_qkv', 'w_proj', 'b_proj', 'w_gate', 'w1', 'b1', 'w2', 'b2')}
    del _L0_cond_all

    def _L1_cond_setup():
        import jax, jax.numpy as jnp
        import numpy as np
        B, L, C = (8, 256, 288)
        H = 16
        D = C // H
        FF = int(C * 4.0)
        EPS = 1e-06

        def _layernorm(x):
            mu = jnp.mean(x, axis=-1, keepdims=True)
            var = jnp.mean(jnp.square(x - mu), axis=-1, keepdims=True)
            return (x - mu) * jax.lax.rsqrt(var + EPS)

        def _modulate(x, shift, scale):
            return x * (1.0 + scale) + shift

        def _attention(h, W_qkv, b_qkv, W_proj, b_proj):
            b, l, c = h.shape
            qkv = h @ W_qkv + b_qkv
            qkv = qkv.reshape(b, l, 3, H, D)
            q, k, v = (qkv[:, :, 0], qkv[:, :, 1], qkv[:, :, 2])
            scale = D ** (-0.5)
            scores = jnp.einsum('blhd,bmhd->bhlm', q * scale, k)
            attn = jax.nn.softmax(scores, axis=-1)
            o = jnp.einsum('bhlm,bmhd->blhd', attn, v).reshape(b, l, c)
            return o @ W_proj + b_proj
        key = jax.random.key(seed)
        ks = jax.random.split(key, 12)
        s = 0.02
        return {'x': jax.random.normal(ks[0], (B, L, C), jnp.float32), 'c': jax.random.normal(ks[1], (B, 1, C), jnp.float32), 'W_qkv': jax.random.normal(ks[2], (C, 3 * C), jnp.float32) * s, 'b_qkv': jnp.zeros((3 * C,), jnp.float32), 'W_proj': jax.random.normal(ks[3], (C, C), jnp.float32) * s, 'b_proj': jnp.zeros((C,), jnp.float32), 'W_fc1': jax.random.normal(ks[4], (C, FF), jnp.float32) * s, 'b_fc1': jnp.zeros((FF,), jnp.float32), 'W_fc2': jax.random.normal(ks[5], (FF, C), jnp.float32) * s, 'b_fc2': jnp.zeros((C,), jnp.float32), 'W_ada': jax.random.normal(ks[6], (C, 6 * C), jnp.float32) * s, 'b_ada': jnp.zeros((6 * C,), jnp.float32)}
    _L1_cond_all = _L1_cond_setup()
    _L1_cond_in = {k: v for k, v in _L1_cond_all.items() if k in ('W_qkv', 'b_qkv', 'W_proj', 'b_proj', 'W_fc1', 'b_fc1', 'W_fc2', 'b_fc2', 'W_ada', 'b_ada')}
    del _L1_cond_all

    def _L2_cond_setup():
        import jax, jax.numpy as jnp
        import numpy as np
        from jax.scipy.linalg import expm
        N, D, COND_DIM = (288, 64, 288)
        B, T = (16, 256)

        def _rotation(cond, W, b):
            v = jax.nn.silu(cond) @ W.T + b
            iu, ju = jnp.triu_indices(D, k=1)
            A = jnp.zeros((cond.shape[0], D, D), dtype=v.dtype)
            A = A.at[:, iu, ju].set(v).at[:, ju, iu].set(-v)
            return expm(A)
        key = jax.random.key(seed)
        k1, k2, k3, k4, k5 = jax.random.split(key, 5)
        x = jax.random.normal(k1, (B, T, N), dtype=jnp.float32)
        cond = jax.random.normal(k2, (B, COND_DIM), dtype=jnp.float32)
        P = jax.random.normal(k3, (N, D), dtype=jnp.float32)
        n_skew = D * (D - 1) // 2
        bound = 1.0 / np.sqrt(COND_DIM)
        W = jax.random.uniform(k4, (n_skew, COND_DIM), minval=-bound, maxval=bound, dtype=jnp.float32)
        b = jax.random.uniform(k5, (n_skew,), minval=-bound, maxval=bound, dtype=jnp.float32)
        return {'x': x, 'cond': cond, 'P': P, 'W': W, 'b': b}
    _L2_cond_all = _L2_cond_setup()
    _L2_cond_in = {k: v for k, v in _L2_cond_all.items() if k in ('P', 'W', 'b')}
    del _L2_cond_all

    def _L3_cond_setup():
        import jax, jax.numpy as jnp
        import numpy as np
        B, S, D = (8, 256, 288)
        H = 16
        HD = D // H
        HID = int(D * 4.0)
        LN_EPS = 1e-05

        def layer_norm(x, w, b):
            m = jnp.mean(x, axis=-1, keepdims=True)
            v = jnp.mean(jnp.square(x - m), axis=-1, keepdims=True)
            return (x - m) * jax.lax.rsqrt(v + LN_EPS) * w + b

        def modulate(x, shift, scale):
            return x * (1.0 + scale[:, None, :]) + shift[:, None, :]

        def attention(x, wq, wk, wv, wo, wo_b):
            b, s, d = x.shape
            q = (x @ wq).reshape(b, s, H, HD).transpose(0, 2, 1, 3)
            k = (x @ wk).reshape(b, s, H, HD).transpose(0, 2, 1, 3)
            v = (x @ wv).reshape(b, s, H, HD).transpose(0, 2, 1, 3)
            scale = 1.0 / np.sqrt(HD).astype(np.float32)
            att = jnp.einsum('bhqd,bhkd->bhqk', q, k) * scale
            att = jax.nn.softmax(att, axis=-1)
            out = jnp.einsum('bhqk,bhkd->bhqd', att, v)
            out = out.transpose(0, 2, 1, 3).reshape(b, s, d)
            return out @ wo + wo_b
        key = jax.random.key(seed)
        ks = jax.random.split(key, 16)
        s = 0.02
        return {'x': jax.random.normal(ks[0], (B, S, D), jnp.float32), 'c': jax.random.normal(ks[1], (B, D), jnp.float32), 'ln1_w': jnp.ones((D,), jnp.float32), 'ln1_b': jnp.zeros((D,), jnp.float32), 'wq': jax.random.normal(ks[2], (D, D), jnp.float32) * s, 'wk': jax.random.normal(ks[3], (D, D), jnp.float32) * s, 'wv': jax.random.normal(ks[4], (D, D), jnp.float32) * s, 'wo': jax.random.normal(ks[5], (D, D), jnp.float32) * s, 'wo_b': jnp.zeros((D,), jnp.float32), 'ln2_w': jnp.ones((D,), jnp.float32), 'ln2_b': jnp.zeros((D,), jnp.float32), 'fc1_w': jax.random.normal(ks[6], (D, HID), jnp.float32) * s, 'fc1_b': jnp.zeros((HID,), jnp.float32), 'fc2_w': jax.random.normal(ks[7], (HID, D), jnp.float32) * s, 'fc2_b': jnp.zeros((D,), jnp.float32), 'ada_w': jax.random.normal(ks[8], (D, 6 * D), jnp.float32) * s, 'ada_b': jnp.zeros((6 * D,), jnp.float32)}
    _L3_cond_all = _L3_cond_setup()
    _L3_cond_in = {k: v for k, v in _L3_cond_all.items() if k in ('ln1_w', 'ln1_b', 'wq', 'wk', 'wv', 'wo', 'wo_b', 'ln2_w', 'ln2_b', 'fc1_w', 'fc1_b', 'fc2_w', 'fc2_b', 'ada_w', 'ada_b')}
    del _L3_cond_all
    return {'x': x, 'cond_1152': cond_1152, 'L0_cond_w_adaln': _L0_cond_in['w_adaln'], 'L0_cond_b_adaln': _L0_cond_in['b_adaln'], 'L0_cond_w_qkv': _L0_cond_in['w_qkv'], 'L0_cond_b_qkv': _L0_cond_in['b_qkv'], 'L0_cond_w_proj': _L0_cond_in['w_proj'], 'L0_cond_b_proj': _L0_cond_in['b_proj'], 'L0_cond_w_gate': _L0_cond_in['w_gate'], 'L0_cond_w1': _L0_cond_in['w1'], 'L0_cond_b1': _L0_cond_in['b1'], 'L0_cond_w2': _L0_cond_in['w2'], 'L0_cond_b2': _L0_cond_in['b2'], 'L1_cond_W_qkv': _L1_cond_in['W_qkv'], 'L1_cond_b_qkv': _L1_cond_in['b_qkv'], 'L1_cond_W_proj': _L1_cond_in['W_proj'], 'L1_cond_b_proj': _L1_cond_in['b_proj'], 'L1_cond_W_fc1': _L1_cond_in['W_fc1'], 'L1_cond_b_fc1': _L1_cond_in['b_fc1'], 'L1_cond_W_fc2': _L1_cond_in['W_fc2'], 'L1_cond_b_fc2': _L1_cond_in['b_fc2'], 'L1_cond_W_ada': _L1_cond_in['W_ada'], 'L1_cond_b_ada': _L1_cond_in['b_ada'], 'L2_cond_P': _L2_cond_in['P'], 'L2_cond_W': _L2_cond_in['W'], 'L2_cond_b': _L2_cond_in['b'], 'L3_cond_ln1_w': _L3_cond_in['ln1_w'], 'L3_cond_ln1_b': _L3_cond_in['ln1_b'], 'L3_cond_wq': _L3_cond_in['wq'], 'L3_cond_wk': _L3_cond_in['wk'], 'L3_cond_wv': _L3_cond_in['wv'], 'L3_cond_wo': _L3_cond_in['wo'], 'L3_cond_wo_b': _L3_cond_in['wo_b'], 'L3_cond_ln2_w': _L3_cond_in['ln2_w'], 'L3_cond_ln2_b': _L3_cond_in['ln2_b'], 'L3_cond_fc1_w': _L3_cond_in['fc1_w'], 'L3_cond_fc1_b': _L3_cond_in['fc1_b'], 'L3_cond_fc2_w': _L3_cond_in['fc2_w'], 'L3_cond_fc2_b': _L3_cond_in['fc2_b'], 'L3_cond_ada_w': _L3_cond_in['ada_w'], 'L3_cond_ada_b': _L3_cond_in['ada_b']}

def reference(x, cond_1152, L0_cond_w_adaln, L0_cond_b_adaln, L0_cond_w_qkv, L0_cond_b_qkv, L0_cond_w_proj, L0_cond_b_proj, L0_cond_w_gate, L0_cond_w1, L0_cond_b1, L0_cond_w2, L0_cond_b2, L1_cond_W_qkv, L1_cond_b_qkv, L1_cond_W_proj, L1_cond_b_proj, L1_cond_W_fc1, L1_cond_b_fc1, L1_cond_W_fc2, L1_cond_b_fc2, L1_cond_W_ada, L1_cond_b_ada, L2_cond_P, L2_cond_W, L2_cond_b, L3_cond_ln1_w, L3_cond_ln1_b, L3_cond_wq, L3_cond_wk, L3_cond_wv, L3_cond_wo, L3_cond_wo_b, L3_cond_ln2_w, L3_cond_ln2_b, L3_cond_fc1_w, L3_cond_fc1_b, L3_cond_fc2_w, L3_cond_fc2_b, L3_cond_ada_w, L3_cond_ada_b):
    import jax
    import jax.numpy as jnp

    def _L0_cond_ref(x, c, w_adaln, b_adaln, w_qkv, b_qkv, w_proj, b_proj, w_gate, w1, b1, w2, b2):
        import jax, jax.numpy as jnp
        import numpy as np
        NUM_HEADS = 16
        NUM_EXPERTS = 4
        TOP_K = 2
        LN_EPS = 1e-06

        def _ln(h):
            mu = jnp.mean(h, axis=-1, keepdims=True)
            var = jnp.var(h, axis=-1, keepdims=True)
            return (h - mu) * jax.lax.rsqrt(var + LN_EPS)

        def _modulate(h, shift, scale):
            return h * (1.0 + scale[:, None, :]) + shift[:, None, :]
        B, N, C = x.shape
        nh = NUM_HEADS
        hd = C // nh
        mod = jax.nn.silu(c) @ w_adaln + b_adaln
        sh_msa, sc_msa, g_msa, sh_mlp, sc_mlp, g_mlp = jnp.split(mod, 6, axis=-1)
        h = _modulate(_ln(x), sh_msa, sc_msa)
        qkv = (h @ w_qkv + b_qkv).reshape(B, N, 3, nh, hd).transpose(2, 0, 3, 1, 4)
        q, k, v = (qkv[0], qkv[1], qkv[2])
        attn = jax.nn.softmax(jnp.einsum('bhqd,bhkd->bhqk', q, k) * hd ** (-0.5), axis=-1)
        o = jnp.einsum('bhqk,bhkd->bhqd', attn, v).transpose(0, 2, 1, 3).reshape(B, N, C)
        o = o @ w_proj + b_proj
        x = x + g_msa[:, None, :] * o
        xn = _modulate(_ln(x), sh_mlp, sc_mlp)
        xf = xn.reshape(-1, C)
        gate_logits = xf @ w_gate
        topk_logits, topk_idx = jax.lax.top_k(gate_logits, TOP_K)
        gates = jax.nn.softmax(topk_logits, axis=-1)
        cw = jnp.sum(jax.nn.one_hot(topk_idx, NUM_EXPERTS, dtype=xf.dtype) * gates[..., None], axis=1)
        hmid = jax.nn.gelu(jnp.einsum('tc,ech->eth', xf, w1) + b1[:, None, :], approximate=True)
        eo = jnp.einsum('eth,ehc->etc', hmid, w2) + b2[:, None, :]
        moe = jnp.einsum('te,etc->tc', cw, eo).reshape(B, N, C)
        return x + g_mlp[:, None, :] * moe

    def _L1_cond_ref(x, c, W_qkv, b_qkv, W_proj, b_proj, W_fc1, b_fc1, W_fc2, b_fc2, W_ada, b_ada):
        import jax, jax.numpy as jnp
        import numpy as np
        B, L, C = (8, 256, 288)
        H = 16
        D = C // H
        FF = int(C * 4.0)
        EPS = 1e-06

        def _layernorm(x):
            mu = jnp.mean(x, axis=-1, keepdims=True)
            var = jnp.mean(jnp.square(x - mu), axis=-1, keepdims=True)
            return (x - mu) * jax.lax.rsqrt(var + EPS)

        def _modulate(x, shift, scale):
            return x * (1.0 + scale) + shift

        def _attention(h, W_qkv, b_qkv, W_proj, b_proj):
            b, l, c = h.shape
            qkv = h @ W_qkv + b_qkv
            qkv = qkv.reshape(b, l, 3, H, D)
            q, k, v = (qkv[:, :, 0], qkv[:, :, 1], qkv[:, :, 2])
            scale = D ** (-0.5)
            scores = jnp.einsum('blhd,bmhd->bhlm', q * scale, k)
            attn = jax.nn.softmax(scores, axis=-1)
            o = jnp.einsum('bhlm,bmhd->blhd', attn, v).reshape(b, l, c)
            return o @ W_proj + b_proj
        ada = jax.nn.silu(c) @ W_ada + b_ada
        shift_msa, scale_msa, gate_msa, shift_mlp, scale_mlp, gate_mlp = jnp.split(ada, 6, axis=-1)
        h = _modulate(_layernorm(x), shift_msa, scale_msa)
        x = x + gate_msa * _attention(h, W_qkv, b_qkv, W_proj, b_proj)
        h = _modulate(_layernorm(x), shift_mlp, scale_mlp)
        mlp = jax.nn.gelu(h @ W_fc1 + b_fc1, approximate=True) @ W_fc2 + b_fc2
        x = x + gate_mlp * mlp
        return x

    def _L2_cond_ref(x, cond, P, W, b):
        import jax, jax.numpy as jnp
        import numpy as np
        from jax.scipy.linalg import expm
        N, D, COND_DIM = (288, 64, 288)
        B, T = (16, 256)

        def _rotation(cond, W, b):
            v = jax.nn.silu(cond) @ W.T + b
            iu, ju = jnp.triu_indices(D, k=1)
            A = jnp.zeros((cond.shape[0], D, D), dtype=v.dtype)
            A = A.at[:, iu, ju].set(v).at[:, ju, iu].set(-v)
            return expm(A)
        U, _ = jnp.linalg.qr(P)
        R = _rotation(cond, W, b)
        z = jnp.einsum('btn,nd->btd', x, U)
        z_rot = jnp.einsum('btd,bde->bte', z, R)
        x_rot = x + jnp.einsum('btd,nd->btn', z_rot - z, U)
        return x_rot

    def _L3_cond_ref(x, c, ln1_w, ln1_b, wq, wk, wv, wo, wo_b, ln2_w, ln2_b, fc1_w, fc1_b, fc2_w, fc2_b, ada_w, ada_b):
        import jax, jax.numpy as jnp
        import numpy as np
        B, S, D = (8, 256, 288)
        H = 16
        HD = D // H
        HID = int(D * 4.0)
        LN_EPS = 1e-05

        def layer_norm(x, w, b):
            m = jnp.mean(x, axis=-1, keepdims=True)
            v = jnp.mean(jnp.square(x - m), axis=-1, keepdims=True)
            return (x - m) * jax.lax.rsqrt(v + LN_EPS) * w + b

        def modulate(x, shift, scale):
            return x * (1.0 + scale[:, None, :]) + shift[:, None, :]

        def attention(x, wq, wk, wv, wo, wo_b):
            b, s, d = x.shape
            q = (x @ wq).reshape(b, s, H, HD).transpose(0, 2, 1, 3)
            k = (x @ wk).reshape(b, s, H, HD).transpose(0, 2, 1, 3)
            v = (x @ wv).reshape(b, s, H, HD).transpose(0, 2, 1, 3)
            scale = 1.0 / np.sqrt(HD).astype(np.float32)
            att = jnp.einsum('bhqd,bhkd->bhqk', q, k) * scale
            att = jax.nn.softmax(att, axis=-1)
            out = jnp.einsum('bhqk,bhkd->bhqd', att, v)
            out = out.transpose(0, 2, 1, 3).reshape(b, s, d)
            return out @ wo + wo_b
        mod = jax.nn.silu(c) @ ada_w + ada_b
        sh_msa, sc_msa, g_msa, sh_mlp, sc_mlp, g_mlp = jnp.split(mod, 6, axis=1)
        h = modulate(layer_norm(x, ln1_w, ln1_b), sh_msa, sc_msa)
        x = x + g_msa[:, None, :] * attention(h, wq, wk, wv, wo, wo_b)
        h = modulate(layer_norm(x, ln2_w, ln2_b), sh_mlp, sc_mlp)
        h = jax.nn.gelu(h @ fc1_w + fc1_b, approximate=False) @ fc2_w + fc2_b
        x = x + g_mlp[:, None, :] * h
        return x
    x = _L0_cond_ref(x, cond_1152, L0_cond_w_adaln, L0_cond_b_adaln, L0_cond_w_qkv, L0_cond_b_qkv, L0_cond_w_proj, L0_cond_b_proj, L0_cond_w_gate, L0_cond_w1, L0_cond_b1, L0_cond_w2, L0_cond_b2)
    x = _L1_cond_ref(x, cond_1152[:, None, :], L1_cond_W_qkv, L1_cond_b_qkv, L1_cond_W_proj, L1_cond_b_proj, L1_cond_W_fc1, L1_cond_b_fc1, L1_cond_W_fc2, L1_cond_b_fc2, L1_cond_W_ada, L1_cond_b_ada)
    x = _L2_cond_ref(x, cond_1152, L2_cond_P, L2_cond_W, L2_cond_b)
    x = _L3_cond_ref(x, cond_1152, L3_cond_ln1_w, L3_cond_ln1_b, L3_cond_wq, L3_cond_wk, L3_cond_wv, L3_cond_wo, L3_cond_wo_b, L3_cond_ln2_w, L3_cond_ln2_b, L3_cond_fc1_w, L3_cond_fc1_b, L3_cond_fc2_w, L3_cond_fc2_b, L3_cond_ada_w, L3_cond_ada_b)
    return x

_drawn_inputs = setup_inputs


def setup_inputs(seed=0):
    import zlib

    import numpy as np

    out = dict(_drawn_inputs(seed))
    spreads = {'L0_cond_b_adaln': (0.0, 0.432),
     'L0_cond_b_qkv': (0.0, 0.8),
     'L0_cond_b_proj': (0.0, 0.356),
     'L0_cond_b1': (0.0, 0.8),
     'L0_cond_b2': (0.0, 0.511),
     'L1_cond_b_qkv': (0.0, 0.8),
     'L1_cond_b_proj': (0.0, 0.337),
     'L1_cond_b_fc1': (0.0, 0.8),
     'L1_cond_b_fc2': (0.0, 0.358),
     'L1_cond_b_ada': (0.0, 0.377),
     'L3_cond_ln1_w': (1.0, 0.6),
     'L3_cond_ln1_b': (0.0, 0.8),
     'L3_cond_wo_b': (0.0, 1.26),
     'L3_cond_ln2_w': (1.0, 0.6),
     'L3_cond_ln2_b': (0.0, 2.0),
     'L3_cond_fc1_b': (0.0, 2.0),
     'L3_cond_fc2_b': (0.0, 1.151),
     'L3_cond_ada_b': (0.0, 0.373)}
    factors = {'L0_cond_w_qkv': 8.0,
     'L0_cond_w_proj': 5.52,
     'L0_cond_w_gate': 2.868,
     'L0_cond_w1': 2.708,
     'L1_cond_W_qkv': 8.0,
     'L1_cond_W_proj': 5.444,
     'L3_cond_wq': 8.0,
     'L3_cond_wk': 8.0,
     'L3_cond_wv': 8.0,
     'L3_cond_wo': 8.0,
     'L3_cond_fc1_w': 2.914}
    for name, (base, spread) in spreads.items():
        noise = np.random.default_rng([zlib.crc32(name.encode()), seed]).standard_normal(out[name].shape)
        drawn = base * np.exp(spread * noise) if base else spread * noise
        out[name] = jnp.asarray(drawn.astype(out[name].dtype))
    for name, factor in factors.items():
        out[name] = (out[name] * factor).astype(out[name].dtype)
    return out
```

```python
from contextlib import ExitStack

import numpy as np
import concourse.bass as bass
from concourse import mybir

ALU = mybir.AluOpType
ACT = mybir.ActivationFunctionType
AX = mybir.AxisListType
F32 = mybir.dt.float32
F32R = mybir.dt.float32r
I32 = mybir.dt.int32

B, N, C = 4, 512, 288
NH = 16
HD = C // NH
HID = 4 * C
NE = 4
RD = 64
P = 128
TT = N // P
KC = 3
CW = C // KC
NJ = HID // P
HG = 4
NG = NH // HG
QK_TILES = [(0, 6), (6, 6), (12, 4)]
SCALE = float(HD) ** -0.5
DOUBLINGS = 14
TAYLOR = 6
EPS = [1e-6, 1e-6, 1e-5]
NL = 3
MOD = 6 * C
NCOL = 18 + NE * NJ
LN_STEPS = 20
HH_START, HH_FWD, HH_BWD = 4, 27, 7
RSQRT_MAGIC = 0x5F3759DF


def wait_alone(eng, sem, value, passed):
    eng.wait_ge(sem, value)
    eng.sem_inc(passed, 1)


def bass_cond_seq_kernel(nc, a, out):
    modd = nc.dram_tensor("mod_rows", [NL, B, MOD], F32).ap()
    vd = nc.dram_tensor("skew_rows", [B, RD * RD], F32).ap()

    with ExitStack() as ctx:
        base = [nc.sbuf_base + 31 & ~31]

        def put(name, shape, dt, at):
            size = 4 * int(np.prod(shape[1:]))
            assert at + size <= nc.sbuf_usable_end, (name, at + size)
            return nc.alloc_sbuf_tensor_at(name, shape, dt, offset=at), at + (size + 31 & ~31)

        def keep(name, shape, dt=F32):
            t, base[0] = put(name, shape, dt, base[0])
            return t

        xres = keep("xres", [P, B * TT, C])
        gates = keep("gates", [P, 2, B, C])
        h2T = keep("h2T", [CW, KC, B * N])
        wqkv = keep("wqkv", [CW, KC, 3 * C])
        wproj = keep("wproj", [P, NG, C])
        rows_b = keep("rows_b", [P, 2, C])
        cols = keep("cols", [P, NL, NCOL])
        modcol = keep("modcol", [CW, NL, 4, KC, B])
        ident = keep("ident", [P, P])
        lowmask = keep("lowmask", [P, TT, NE, NE])
        onesr = keep("onesr", [2, N], F32R)
        wgate = keep("wgate", [CW, KC, NE])
        silu = keep("silu", [CW + 1, KC, B])
        stats = keep("stats", [P, TT, 6])
        mv = keep("mv", [P, TT, 2])
        nwt = keep("nwt", [P, 4, TT])
        qf = keep("qf", [108, 2, N])
        qhi = keep("qhi", [108, 2, N], F32R)
        qlo = keep("qlo", [108, 2, N], F32R)
        vaug = keep("vaug", [P, TT, NH, 32])
        mx = keep("mx", [P, NG, TT, HG])
        nm = keep("nm", [P, NG, TT, 2 * HG], F32R)
        nmT = keep("nmT", [2 * HG, 2, N], F32R)
        cw = keep("cw", [P, B * TT, NE])
        tk = keep("tk", [P, 4, TT, NE])
        tkm = keep("tkm", [P, 2, TT])
        tkc = keep("tkc", [P, 2, TT, NE, NE])
        lgT = keep("lgT", [NE, N])
        U = keep("U", [CW, KC, RD])
        EUt = keep("EUt", [RD, B, C])
        GE = keep("GE", [RD, B, RD])
        hA = keep("hA", [CW, KC, RD])
        hV = keep("hV", [CW, KC, RD])
        hp = keep("hp", [CW, KC, RD])
        hr = keep("hr", [CW, 2 * RD])
        hR = keep("hR", [CW, 2 * RD])
        hC = keep("hC", [CW, RD])
        hs = keep("hs", [CW, 16])
        hU = keep("hU", [RD, C])
        oc, s_a = put("oc", [P, N], F32, base[0])
        osh, s_a = put("osh", [P, N], F32, s_a)
        orc, s_a = put("orc", [P, N], F32, s_a)
        region = s_a
        qs, at = put("qs", [P, NH, N], F32R, region)
        ks, at = put("ks", [P, NH, N], F32R, at)
        oT, at = put("oT", [P, NG, N], F32, at)
        shared = at
        pT, _ = put("pT", [P, 4, 2, N], F32, shared)
        xn, at = put("xn", [P, TT, C], F32, shared)
        hT, _ = put("hT", [CW, KC, N], F32, at)
        acc, at = put("acc", [P, B * TT, C], F32, region)
        w1, at = put("w1", [CW, KC, HID], F32, at)
        w2, at = put("w2", [P, NJ, C], F32, at)
        gT, at = put("gT", [P, NJ, N], F32, at)
        b2b, at = put("b2b", [P, C], F32, at)
        tmp, at = put("tmp", [P, TT, C], F32, at)
        zT, at = put("zT", [RD, N], F32, at)
        assert at <= shared
        ada, at = put("ada", [CW + 1, 2, KC, MOD], F32, region)
        wf, at = put("wf", [CW + 1, 2, KC, 1024], F32, at)
        vsb, at = put("vsb", [B, 2, 512], F32, at)
        modsb, at = put("modsb", [B, MOD], F32, at)
        skew, at = put("skew", [RD, B, RD], F32, at)
        sx, at = put("sx", [RD, 2, B, RD], F32, at)
        ey, at = put("ey", [RD, 2, 2, B, RD], F32, at)
        eye8, at = put("eye8", [RD, 2, B, RD], F32, at)
        assert at <= nc.sbuf_usable_end

        ps = ctx.enter_context(nc.psum_tensor("ps", [P, 8, N], F32))

        def bank(i):
            return ps[:, i, :]

        names = """ld_const ld_x ld_cond ld_wf0 ld_wf1 ld_ada0 ld_ada1 ld_skew ld_gate ld_w ld_mlp ld_p silu_done
            skew_mm skew_out skew_stored0 skew_stored1 sk_tr sk_dve ex_mm ex_ev mod_mm mod_cp mod_stored mod_tr md_step hh_z tk_r cw_ready
            ln_step xn_ready tr_done h_ready qk_mm qf_ready hi_done split_done stack_ld0 stack_ld1 ones_ld
            v_mm v_ready max_mm mx_done nh_done nm_ready nm_tr nmT_ready nm_ld0 nm_ld1 st_mm exp_done pv_done
            oc_done o_step oT_ready pj_mm xa_t xa_g xa_done lg_mm lg_cp lg_tr tk_step tk_in tk_exp
            fc1_mm gelu_done fc2_mm evac_done acc_done gm_done xm_done
            hh_step hh_ld hh_st u_done u_tr u_cp eu_mm eu_cp xc_done xt_tr xt_cp z_mm z_cp r_mm xr_done
            out_done setup_done pool_passed dve_passed pe_passed""".split()
        S = {n: ctx.enter_context(nc.semaphore(n)) for n in names}
        block = ctx.enter_context(nc.Block())

        @block.sync
        def _(sp):
            for dst, src in ((ident[:, :], a["ident"]), (cols[:, :, :], a["cols"]),
                             (lowmask[:, :, :, :], a["lowmask"]),
                             (wgate[:, :, :], a["w_gate"].rearrange("(c p) e -> p c e", p=CW)),
                             (onesr[:, :].bitcast(F32), a["ones"]), (eye8[:, :, :, :], a["eye8"])):
                sp.dma_start(dst, src).then_inc(S["ld_const"], 16)
            sp.dma_start(silu[0:CW, :, :], a["condT"].rearrange("(c p) b -> p c b", p=CW)).then_inc(S["ld_cond"], 16)

            def load_wf(k):
                src = a["w_skew"][:, k * 1024:(k + 1) * 1024]
                sp.dma_start(wf[0:CW, k % 2, 0:2, :], src[0:2 * CW].rearrange("(c p) n -> p c n", p=CW)).then_inc(S[f"ld_wf{k % 2}"], 16)
                sp.dma_start(wf[:, k % 2, 2, :], src[2 * CW:C + 1]).then_inc(S[f"ld_wf{k % 2}"], 16)

            def load_ada(l):
                src = a["w_ada"][l]
                sp.dma_start(ada[0:CW, l % 2, 0:2, :], src[0:2 * CW].rearrange("(c p) n -> p c n", p=CW)).then_inc(S[f"ld_ada{l % 2}"], 16)
                sp.dma_start(ada[:, l % 2, 2, :], src[2 * CW:C + 1]).then_inc(S[f"ld_ada{l % 2}"], 16)

            load_wf(0)
            load_wf(1)
            load_ada(0)
            load_ada(1)
            for k in (2, 3):
                sp.wait_ge(S["skew_mm"], 2 * (k - 1))
                load_wf(k)
            sp.wait_ge(S["mod_mm"], 4)
            load_ada(2)
            for u in range(2):
                sp.wait_ge(S[f"skew_stored{u}"], 4 * 16)
            sp.dma_start(skew[:, :, :], vd.rearrange("b (i j) -> i b j", i=RD)).then_inc(S["ld_skew"], 16)

            for l in range(NL):
                if l == 2:
                    sp.wait_ge(S["xr_done"], TT * B)
                sp.wait_ge(S["mod_stored"], 16 * NL)
                if l == 0:
                    sp.wait_ge(S["setup_done"], 1)
                else:
                    sp.wait_ge(S["fc2_mm"], 16 * (NE + l - 1) + TT)
                for s, sec in enumerate((2, 5)):
                    if l:
                        sp.wait_ge(S["xm_done"], 16 * l)
                    sp.dma_start(gates[:, s, :, :], modd[l, :, sec * C:(sec + 1) * C].partition_broadcast(P)).then_inc(S["ld_gate"], 16)
                sp.dma_start(wqkv[:, :, :], a["wqkv"][l].rearrange("(c p) n -> p c n", p=CW)).then_inc(S["ld_w"], 16)
                sp.dma_start(wproj[:, :, :], a["wproj"][l].rearrange("g p n -> p g n")).then_inc(S["ld_w"], 16)
                sp.dma_start(rows_b[:, :, :], a["rows_b"][l].partition_broadcast(P)).then_inc(S["ld_w"], 16)
                for h in range(NH):
                    sp.dma_start(ks[72:74, h, :].bitcast(F32), onesr[:, :].bitcast(F32)).then_inc(S["ones_ld"], 16)
                with sp.Fori(0, B) as b:
                    it = b + B * l
                    for m, (h0, nh) in enumerate(QK_TILES + QK_TILES):
                        sp.wait_ge(S["split_done"], it * 6 + (m + 1))
                        is_q, dst = m < 3, qs if m < 3 else ks
                        if m == 0:
                            sp.wait_ge(S["pv_done"], it * 16 + 16)
                        for h in range(nh):
                            for r, part in enumerate((qhi, qhi, qlo, qlo) if is_q else (qhi, qlo, qhi, qlo)):
                                sp.dma_start(dst[HD * r:HD * r + HD, h0 + h, :].bitcast(F32),
                                             part[HD * h:HD * h + HD, m % 2, :].bitcast(F32)).then_inc(S[f"stack_ld{m % 2}"], 16)
                    for g in range(NG):
                        sp.wait_ge(S["nmT_ready"], it * NG + (g + 1))
                        for r in range(2):
                            sp.dma_start(qs[72 + r:73 + r, HG * g:HG * g + HG, :].bitcast(F32),
                                         nmT[HG * r:HG * r + HG, g % 2, :].bitcast(F32)).then_inc(S[f"nm_ld{g % 2}"], 16)
                sp.wait_ge(S["h_ready"], 6 * B * (l + 1) + 6)
                sp.wait_ge(S["pv_done"], 16 * B * (l + 1) + 16)
                for e in range(NE if l == 0 else 1):
                    p = e if l == 0 else NE + l - 1
                    if e:
                        sp.wait_ge(S["fc2_mm"], 16 * p + TT)
                        sp.wait_ge(S["evac_done"], 16 * p + TT)
                    sp.dma_start(w1[:, :, :], a["w1"][p].rearrange("(c p) n -> p c n", p=CW)).then_inc(S["ld_mlp"], 16)
                    sp.dma_start(w2[:, :, :], a["w2"][p].rearrange("(j p) n -> p j n", p=P)).then_inc(S["ld_mlp"], 16)
                    sp.dma_start(b2b[:, :], a["b2"][p].partition_broadcast(P)).then_inc(S["ld_mlp"], 16)
            with sp.Fori(0, B) as b:
                sp.wait_ge(S["xm_done"], b * TT + (2 * TT * B + TT))
                sp.dma_start(out.rearrange("b (t p) c -> p (b t) c", p=P)[:, bass.ds(b * TT, TT), :],
                             xres[:, bass.ds(b * TT, TT), :]).then_inc(S["out_done"], 16)
            sp.wait_ge(S["out_done"], 16 * B)

        @block.gpsimd
        def _(pool):
            g = nc.gpsimd
            RED = bass.bass_isa.ReduceOp.add
            pool.dma_start(hA[:, :, :], a["P"].rearrange("(c p) d -> p c d", p=CW)).then_inc(S["ld_p"], 16)
            pool.wait_ge(S["ld_const"], 16 * 6)
            g.memset(hs[:, :], 0.5).then_inc(S["hh_step"], 1)
            g.memset(U[:, :, :], 0.0).then_inc(S["hh_step"], 1)
            pool.wait_ge(S["hh_step"], 2)
            g.tensor_copy(U[0:RD, 0, :], ident[0:RD, 0:RD]).then_inc(S["hh_step"], 1)
            g.memset(hs[:, 1:2], -1.0).then_inc(S["hh_step"], 1)
            pool.wait_ge(S["hh_step"], HH_START)
            pool.wait_ge(S["ld_p"], 16)
            half, neg, sig, nrm, al, sg, sn, den, c, idj, keepj = (hs[:, i:i + 1] for i in range(11))
            wide = [CW, KC, RD]

            with pool.Fori(0, RD) as j:
                n = [0]

                def step(ins):
                    n[0] += 1
                    ins.then_inc(S["hh_step"], 1)
                    wait_alone(pool, S["hh_step"], j * HH_FWD + (HH_START + n[0]), S["pool_passed"])

                vj = hV[:, :, bass.ds(j, 1)]
                step(g.tensor_copy(vj, hA[:, :, bass.ds(j, 1)]))
                step(g.tensor_copy(idj, ident[0:CW, bass.ds(j, 1)]))
                step(g.tensor_tensor(hp[:, :, :], hA[:, :, :], vj.to_broadcast(wide), ALU.mult))
                step(g.tensor_tensor(hp[:, 0, :], hp[:, 0, :], hp[:, 1, :], ALU.add))
                step(g.tensor_tensor(hr[:, 0:RD], hp[:, 0, :], hp[:, 2, :], ALU.add))
                step(g.tensor_scalar(hr[:, RD:2 * RD], hA[:, 0, :], idj, 1.0, ALU.mult, ALU.mult))
                step(g.partition_all_reduce(hR[:, :], hr[:, :], CW, RED))
                step(g.tensor_copy(sig, hR[:, bass.ds(j, 1)]))
                step(g.tensor_copy(al, hR[:, bass.ds(j + RD, 1)]))
                step(g.tensor_tensor(nrm, sig, half, ALU.pow))
                step(g.tensor_scalar(sg, al, 0.0, 2.0, ALU.is_ge, ALU.mult))
                step(g.tensor_scalar(sg, sg, 1.0, -1.0, ALU.mult, ALU.add))
                step(g.tensor_tensor(sn, nrm, sg, ALU.mult))
                step(g.tensor_tensor(den, al, sn, ALU.mult))
                step(g.tensor_tensor(den, den, sig, ALU.add))
                step(g.tensor_scalar(den, den, 1e-37, 1e38, ALU.max, ALU.min))
                step(g.tensor_tensor(c, den, neg, ALU.pow))
                step(g.tensor_copy(hC[:, bass.ds(j, 1)], c))
                step(g.tensor_tensor(sig, idj, sn, ALU.mult))
                step(g.tensor_tensor(hV[:, 0, bass.ds(j, 1)], hV[:, 0, bass.ds(j, 1)], sig, ALU.add))
                step(g.tensor_scalar(hr[:, 0:RD], hR[:, RD:2 * RD], sn, 1.0, ALU.mult, ALU.mult))
                step(g.tensor_tensor(hr[:, 0:RD], hr[:, 0:RD], hR[:, 0:RD], ALU.add))
                step(g.tensor_scalar(hr[:, 0:RD], hr[:, 0:RD], c, 1.0, ALU.mult, ALU.mult))
                step(g.tensor_tensor(hp[:, :, :], hr[:, 0:RD].unsqueeze(1).to_broadcast(wide), vj.to_broadcast(wide), ALU.mult))
                step(g.tensor_tensor(hA[:, :, :], hA[:, :, :], hp[:, :, :], ALU.subtract))
                step(g.tensor_scalar(keepj, idj, -1.0, 1.0, ALU.mult, ALU.add))
                step(g.tensor_scalar(hA[:, 0, :], hA[:, 0, :], keepj, 1.0, ALU.mult, ALU.mult))
                assert n[0] == HH_FWD, n
            with pool.Fori(0, RD) as i:
                j = (RD - 1) - i
                n = [0]

                def step(ins):
                    n[0] += 1
                    ins.then_inc(S["hh_step"], 1)
                    wait_alone(pool, S["hh_step"], i * HH_BWD + (HH_START + RD * HH_FWD + n[0]), S["pool_passed"])

                vj = hV[:, :, bass.ds(j, 1)]
                step(g.tensor_tensor(hp[:, :, :], U[:, :, :], vj.to_broadcast(wide), ALU.mult))
                step(g.tensor_tensor(hp[:, 0, :], hp[:, 0, :], hp[:, 1, :], ALU.add))
                step(g.tensor_tensor(hr[:, 0:RD], hp[:, 0, :], hp[:, 2, :], ALU.add))
                step(g.partition_all_reduce(hR[:, 0:RD], hr[:, 0:RD], CW, RED))
                step(g.tensor_tensor(hr[:, 0:RD], hR[:, 0:RD], hC[:, bass.ds(j, 1)].to_broadcast([CW, RD]), ALU.mult))
                step(g.tensor_tensor(hp[:, :, :], hr[:, 0:RD].unsqueeze(1).to_broadcast(wide), vj.to_broadcast(wide), ALU.mult))
                step(g.tensor_tensor(U[:, :, :], U[:, :, :], hp[:, :, :], ALU.subtract))
                assert n[0] == HH_BWD, n

        @block.tensor
        def _(pe):
            mm, tr = nc.tensor.matmul, nc.tensor.transpose
            pe.sem_inc(S["tr_done"], 3)
            pe.sem_inc(S["pv_done"], 16)
            pe.sem_inc(S["fc2_mm"], TT)
            pe.sem_inc(S["xt_tr"], KC)
            pe.wait_ge(S["silu_done"], 2)

            for n in range(8):
                if n % 2 == 0:
                    pe.wait_ge(S[f"ld_wf{n // 2 % 2}"], 32 * (n // 4 + 1))
                if n >= 4:
                    pe.wait_ge(S["skew_out"], n - 3)
                for c in range(KC):
                    k = CW + (c == KC - 1)
                    ins = mm(ps[0:B, n % 4, :], silu[0:k, c, :], wf[0:k, (n // 2) % 2, c, (n % 2) * 512:(n % 2) * 512 + 512],
                             start=(c == 0), stop=(c == KC - 1))
                ins.then_inc(S["skew_mm"], 1)
            pe.wait_ge(S["ld_const"], 16 * 6)
            MC = MOD // 4
            for l in range(NL):
                pe.wait_ge(S[f"ld_ada{l % 2}"], 32 * (l // 2 + 1))
                if l:
                    pe.wait_ge(S["mod_cp"], 4 * l)
                for n in range(4):
                    for c in range(KC):
                        k = CW + (c == KC - 1)
                        ins = mm(ps[0:B, 4 + n, 0:MC], silu[0:k, c, :], ada[0:k, l % 2, c, n * MC:(n + 1) * MC],
                                 start=(c == 0), stop=(c == KC - 1))
                    ins.then_inc(S["mod_mm"], 1)
                if l:
                    pe.wait_ge(S["md_step"], 18 * l)
                else:
                    pe.wait_ge(S["skew_out"], 8)
                pe.wait_ge(S["mod_cp"], 4 * (l + 1))
                for s, sec in enumerate((0, 1, 3, 4)):
                    for c in range(KC):
                        q = (s * KC + c) * B
                        ins = tr(ps[0:CW, 0, q:q + B], modsb[:, sec * C + c * CW:sec * C + (c + 1) * CW], ident[0:B, 0:B])
                ins.then_inc(S["mod_tr"], 1)
            pe.wait_ge(S["ld_skew"], 16)
            for b in range(B):
                ins = tr(ps[0:RD, 1, b * RD:(b + 1) * RD], skew[:, b, :], ident[0:RD, 0:RD])
            ins.then_inc(S["sk_tr"], 1)

            def pair_products(to, left, right):
                for h in range(2):
                    for b in range(B):
                        q = (h * B + b) * RD
                        ins = mm(ps[0:RD, to, q:q + RD], left[:, 1 - h, b, :], right[:, h, b, :], start=True, stop=True)
                ins.then_inc(S["ex_mm"], 1)

            for i in range(TAYLOR - 1):
                pe.wait_ge(S["ex_ev"], i + 1)
                pair_products(2 + i % 2, sx, ey[:, i % 2])
            with pe.Fori(0, DOUBLINGS // 2) as i:
                for u in range(2):
                    wait_alone(pe, S["ex_ev"], i * 2 + (TAYLOR + u), S["pe_passed"])
                    e = ey[:, (TAYLOR - 1 + u) % 2]
                    pair_products(2 + (TAYLOR - 1 + u) % 2, e, e)

            def transposes(src, n_ready, banks, done):
                for t in range(TT):
                    pe.wait_ge(S["xn_ready"], n_ready + (t + 1))
                for c in range(KC):
                    for t in range(TT):
                        ins = tr(ps[0:CW, banks[c], t * P:(t + 1) * P], src[:, t, c * CW:(c + 1) * CW], ident[:, :])
                    ins.then_inc(S["tr_done"], 1)

            def attention(l, b):
                it = b + B * l
                if l == 0:
                    pe.wait_ge(S["ld_w"], 48)
                pe.wait_ge(S["h_ready"], it * 6 + 6)
                transposes(xn, it * 8, (4, 5, 7), None)
                for m, (h0, nh) in enumerate(QK_TILES + QK_TILES):
                    if m >= 2:
                        pe.wait_ge(S["qf_ready"], it * 6 + (m - 1))
                    o = (m // 3) * C + h0 * HD
                    for c in range(KC):
                        if m == 0:
                            pe.wait_ge(S["h_ready"], it * 6 + (6 + c + 1))
                        ins = mm(ps[0:nh * HD, m % 2, :], wqkv[:, c, o:o + nh * HD], hT[:, c, :], start=(c == 0), stop=(c == KC - 1))
                    ins.then_inc(S["qk_mm"], 1)

                def max_unit(g, qt):
                    for i in range(HG):
                        h, u = g * HG + i, (g * TT + qt) * HG + i
                        if u >= 2:
                            pe.wait_ge(S["mx_done"], it * 64 + (u - 1))
                        ins = mm(bank(u % 2), qs[0:72, h, qt * P:(qt + 1) * P], ks[0:72, h, :], start=True, stop=True)
                        ins.then_inc(S["max_mm"], 1)

                def max_rows(g):
                    pe.wait_ge(S["nm_ready"], it * NG + (g + 1))
                    if g:
                        pe.wait_ge(S["nmT_ready"], it * NG + g)
                    for qt in range(TT):
                        ins = tr(ps[0:2 * HG, 7, qt * P:(qt + 1) * P], nm[:, g, qt, :].bitcast(F32), ident[:, :])
                    ins.then_inc(S["nm_tr"], 1)

                pe.wait_ge(S["qf_ready"], it * 6 + 6)
                for u in range(2):
                    pe.wait_ge(S[f"stack_ld{u}"], it * (16 * 4 * NH) + 16 * 4 * NH)
                pe.wait_ge(S["ones_ld"], 16 * NH * (l + 1))
                for qt in range(TT):
                    max_unit(0, qt)
                for t in range(TT):
                    if t >= 2:
                        pe.wait_ge(S["v_ready"], it * TT + (t - 1))
                    for c in range(KC):
                        ins = mm(ps[:, 2 + t % 2, 0:C], hT[:, c, t * P:(t + 1) * P], wqkv[:, c, 2 * C:3 * C], start=(c == 0), stop=(c == KC - 1))
                    ins.then_inc(S["v_mm"], 1)
                max_rows(0)
                for qt in range(TT):
                    max_unit(1, qt)

                def scores(k):
                    g, kt = divmod(k, TT)
                    if kt == 0:
                        pe.wait_ge(S[f"nm_ld{g % 2}"], it * (16 * NG) + 32 * (g // 2 + 1))
                    if k == 0:
                        pe.wait_ge(S["v_ready"], it * TT + TT)
                    for r in range(2):
                        if k:
                            pe.wait_ge(S["exp_done"], it * 32 + (2 * k - 1 + r))
                        for i in range(2):
                            h = g * HG + 2 * r + i
                            ins = mm(bank(2 + 2 * r + i), ks[0:74, h, kt * P:(kt + 1) * P], qs[0:74, h, :], start=True, stop=True)
                        ins.then_inc(S["st_mm"], 1)

                scores(0)
                for k in range(NG * TT):
                    g, kt = divmod(k, TT)
                    if k + 1 < NG * TT:
                        scores(k + 1)
                    if g + 2 < NG:
                        max_unit(g + 2, kt)
                    pe.wait_ge(S["exp_done"], it * 32 + (2 * k + 2))
                    if kt == 0 and g:
                        pe.wait_ge(S["oc_done"], it * NG + g)
                    for i in range(HG):
                        ins = mm(ps[32 * i:32 * i + 32, 6, :], vaug[:, kt, g * HG + i, :], pT[:, (2 * k + i // 2) % 4, i % 2, :],
                                 start=(kt == 0), stop=(kt == TT - 1), tile_position=(0, 32 * i))
                    ins.then_inc(S["pv_done"], 1)
                    if kt == 1 and g + 1 < NG:
                        max_rows(g + 1)
                pe.wait_ge(S["mx_done"], it * 64 + 64)
                pe.wait_ge(S["oT_ready"], it * NG + NG)
                for t in range(TT):
                    for g in range(NG):
                        ins = mm(ps[:, t, 0:C], oT[:, g, t * P:(t + 1) * P], wproj[:, g, :], start=(g == 0), stop=(g == NG - 1))
                    ins.then_inc(S["pj_mm"], 1)
                transposes(xn, it * 8 + 4, (4, 5, 7), None)
                if l == 0:
                    pe.wait_ge(S["h_ready"], it * 6 + 12)
                    for c in range(KC):
                        ins = mm(ps[0:NE, 6, :], wgate[:, c, :], h2T[:, c, bass.ds(b * N, N)], start=(c == 0), stop=(c == KC - 1))
                    ins.then_inc(S["lg_mm"], 1)
                    wait_alone(pe, S["lg_cp"], b + 1, S["pe_passed"])
                    for t in range(TT):
                        ins = tr(ps[:, 6, t * NE:(t + 1) * NE], lgT[:, t * P:(t + 1) * P], ident[0:NE, 0:NE])
                    ins.then_inc(S["lg_tr"], 1)

            def mlp(p, b):
                it = b + B * p
                for j in range(NJ):
                    if j >= 3:
                        pe.wait_ge(S["gelu_done"], it * NJ + (j - 2))
                    for c in range(KC):
                        ins = mm(bank(j % 3), w1[:, c, j * P:(j + 1) * P], h2T[:, c, bass.ds(b * N, N)], start=(c == 0), stop=(c == KC - 1))
                    ins.then_inc(S["fc1_mm"], 1)
                pe.wait_ge(S["evac_done"], it * TT + TT)
                for t in range(TT):
                    for j in range(NJ):
                        if t == 0:
                            pe.wait_ge(S["gelu_done"], it * NJ + (j + 1))
                        ins = mm(ps[:, 4 + t, 0:C], gT[:, j, t * P:(t + 1) * P], w2[:, j, :], start=(j == 0), stop=(j == NJ - 1))
                    ins.then_inc(S["fc2_mm"], 1)

            def rotation():
                pe.wait_ge(S["hh_step"], HH_START + RD * (HH_FWD + HH_BWD))
                for c in range(KC):
                    ins = tr(ps[0:RD, 3, c * CW:(c + 1) * CW], U[:, c, :], ident[0:CW, 0:CW])
                ins.then_inc(S["u_tr"], 1)
                pe.wait_ge(S["u_cp"], 1)
                for b in range(B):
                    pe.wait_ge(S["evac_done"], 16 * (NE + 1) + TT)
                    ins = mm(ps[0:RD, 4 + b, 0:C], GE[:, b, :], hU[:, :], start=True, stop=True)
                ins.then_inc(S["eu_mm"], 1)
                pe.wait_ge(S["eu_cp"], 1)
                with pe.Fori(0, B) as b:
                    pe.wait_ge(S["xc_done"], b * TT + TT)
                    for c in range(KC):
                        for t in range(TT):
                            ins = tr(ps[0:CW, c, t * P:(t + 1) * P], xn[:, t, c * CW:(c + 1) * CW], ident[:, :])
                        ins.then_inc(S["xt_tr"], 1)
                    for c in range(KC):
                        pe.wait_ge(S["xt_cp"], b * KC + (c + 1))
                        ins = mm(ps[0:RD, 3, :], U[:, c, :], hT[:, c, :], start=(c == 0), stop=(c == KC - 1))
                    ins.then_inc(S["z_mm"], 1)
                    pe.wait_ge(S["z_cp"], b + 1)
                    for t in range(TT):
                        ins = mm(ps[:, 4 + t, 0:C], zT[:, t * P:(t + 1) * P], EUt[:, bass.ds(b, 1), :].rearrange("p a n -> p (a n)"), start=True, stop=True)
                        ins.then_inc(S["r_mm"], 1)

            for l in range(NL):
                if l == 2:
                    rotation()
                if l:
                    pe.wait_ge(S["ld_w"], 48 * (l + 1))
                with pe.Fori(0, B) as b:
                    attention(l, b)
                for e in range(NE if l == 0 else 1):
                    p = e if l == 0 else NE + l - 1
                    pe.wait_ge(S["ld_mlp"], 48 * (p + 1))
                    pe.wait_ge(S["h_ready"], 6 * B * (l + 1) + 6)
                    with pe.Fori(0, B) as b:
                        mlp(p, b)

        @block.scalar
        def _(act):
            A = nc.scalar.activation
            act.sem_inc(S["h_ready"], 6)
            act.dma_start(xres[:, :, :], a["x"].rearrange("b (t p) c -> p (b t) c", p=P)).then_inc(S["ld_x"], 16)
            act.wait_ge(S["ld_cond"], 16)
            A(silu[0:CW, :, :], silu[0:CW, :, :], ACT.Silu).then_inc(S["silu_done"], 1)
            for n in range(8):
                act.wait_ge(S["skew_mm"], n + 1)
                if n >= 2:
                    act.wait_ge(S[f"skew_stored{n % 2}"], 16 * (n // 2))
                A(vsb[:, n % 2, :], ps[0:B, n % 4, :], ACT.Copy).then_inc(S["skew_out"], 1)
                act.wait_ge(S["skew_out"], n + 1)
                act.dma_start(vd[:, n * 512:(n + 1) * 512], vsb[:, n % 2, :]).then_inc(S[f"skew_stored{n % 2}"], 16)
            for l in range(NL):
                if l:
                    act.wait_ge(S["mod_stored"], 16 * l)
                    act.wait_ge(S["mod_tr"], l)
                for n in range(4):
                    act.wait_ge(S["mod_mm"], 4 * l + n + 1)
                    A(modsb[:, n * (MOD // 4):(n + 1) * (MOD // 4)], ps[0:B, 4 + n, 0:MOD // 4], ACT.Copy).then_inc(S["mod_cp"], 1)
                act.wait_ge(S["mod_cp"], 4 * l + 4)
                act.dma_start(modd[l], modsb[:, :]).then_inc(S["mod_stored"], 16)

            def attention(l, b):
                it = b + B * l
                act.wait_ge(S["md_step"], 18 * (l + 1))
                for c in range(KC):
                    act.wait_ge(S["tr_done"], it * 6 + (3 + c + 1))
                    A(hT[:, c, :], ps[0:CW, (4, 5, 7)[c], :], ACT.Identity, bias=modcol[:, l, 0, c, bass.ds(b, 1)],
                      scale=modcol[:, l, 1, c, bass.ds(b, 1)]).then_inc(S["h_ready"], 1)
                for m, (h0, nh) in enumerate(QK_TILES + QK_TILES):
                    act.wait_ge(S["qk_mm"], it * 6 + (m + 1))
                    if m >= 2:
                        act.wait_ge(S["split_done"], it * 6 + (m - 1))
                    A(qf[0:nh * HD, m % 2, :], ps[0:nh * HD, m % 2, :], ACT.Identity, bias=cols[0:nh * HD, l, m:m + 1]).then_inc(S["qf_ready"], 1)

                def max_rows(g):
                    act.wait_ge(S["nm_tr"], it * NG + (g + 1))
                    if g >= 2:
                        act.wait_ge(S[f"nm_ld{g % 2}"], it * (16 * NG) + 32 * (g // 2))
                    A(nmT[:, g % 2, :], ps[0:2 * HG, 7, :], ACT.Copy).then_inc(S["nmT_ready"], 1)

                max_rows(0)
                for k in range(NG * TT):
                    g, kt = divmod(k, TT)
                    for r in range(2):
                        act.wait_ge(S["st_mm"], it * 32 + (2 * k + r + 1))
                        if k >= 2:
                            act.wait_ge(S["pv_done"], it * 16 + (16 + k - 1))
                        A(pT[:, (2 * k + r) % 4, :, :], ps[:, 2 + 2 * r:4 + 2 * r, :], ACT.Exp, scale=SCALE).then_inc(S["exp_done"], 1)
                    if kt == 1 and g + 1 < NG:
                        max_rows(g + 1)
                for c in range(KC):
                    act.wait_ge(S["tr_done"], it * 6 + (6 + c + 1))
                    A(h2T[:, c, bass.ds(b * N, N)], ps[0:CW, (4, 5, 7)[c], :], ACT.Identity, bias=modcol[:, l, 2, c, bass.ds(b, 1)],
                      scale=modcol[:, l, 3, c, bass.ds(b, 1)]).then_inc(S["h_ready"], 1)
                if l == 0:
                    act.wait_ge(S["lg_mm"], b + 1)
                    A(lgT[:, :], ps[0:NE, 6, :], ACT.Copy).then_inc(S["lg_cp"], 1)
                    act.wait_ge(S["tk_in"], b + 1)
                    A(tk[:, 1, :, :], tk[:, 1, :, :], ACT.Exp).then_inc(S["tk_exp"], 1)

            def mlp(l, e, p, b):
                it = b + B * p
                act.wait_ge(S["fc2_mm"], it * TT + TT)
                for j in range(NJ):
                    act.wait_ge(S["fc1_mm"], it * NJ + (j + 1))
                    A(gT[:, j, :], bank(j % 3), ACT.Gelu if l == 2 else ACT.Gelu_apprx_tanh,
                      bias=cols[:, l, 18 + NJ * e + j:19 + NJ * e + j]).then_inc(S["gelu_done"], 1)

            for l in range(NL):
                if l == 2:
                    act.wait_ge(S["u_tr"], 1)
                    A(hU[:, :], ps[0:RD, 3, 0:C], ACT.Copy).then_inc(S["u_cp"], 1)
                    act.wait_ge(S["eu_mm"], 1)
                    A(EUt[:, :, :], ps[0:RD, 4:8, 0:C], ACT.Copy).then_inc(S["eu_cp"], 1)
                    with act.Fori(0, B) as b:
                        for c in range(KC):
                            act.wait_ge(S["xt_tr"], b * KC + (KC + c + 1))
                            A(hT[:, c, :], ps[0:CW, c, :], ACT.Copy).then_inc(S["xt_cp"], 1)
                        act.wait_ge(S["z_mm"], b + 1)
                        A(zT[:, :], ps[0:RD, 3, :], ACT.Copy).then_inc(S["z_cp"], 1)
                with act.Fori(0, B) as b:
                    attention(l, b)
                for e in range(NE if l == 0 else 1):
                    p = e if l == 0 else NE + l - 1
                    with act.Fori(0, B) as b:
                        mlp(l, e, p, b)

        @block.vector
        def _(dve):
            V = nc.vector
            dve.sem_inc(S["evac_done"], TT)
            V.memset(silu[CW:CW + 1, :, :], 1.0).then_inc(S["silu_done"], 1)
            V.memset(vaug[:, :, :, :], 1.0)
            dve.wait_ge(S["ld_const"], 16 * 6)
            for l in range(NL):
                dve.wait_ge(S["mod_tr"], l + 1)
                tp = ps[0:CW, 0, 0:4 * KC * B].rearrange("p (s c b) -> p s c b", s=4, c=KC)
                for s in (0, 2):
                    for c in range(KC):
                        lnw = cols[0:CW, l, 6 + 3 * s + c:7 + 3 * s + c]
                        lnb = cols[0:CW, l, 9 + 3 * s + c:10 + 3 * s + c]
                        V.tensor_scalar(modcol[:, l, s + 1, c, :], tp[:, s + 1, c, :], 1.0, lnw, ALU.add, ALU.mult).then_inc(S["md_step"], 1)
                        V.tensor_scalar(stats[0:CW, 0, 0:B], tp[:, s + 1, c, :], 1.0, lnb, ALU.add, ALU.mult).then_inc(S["md_step"], 1)
                        k = (l * 2 + s // 2) * KC + c
                        dve.wait_ge(S["md_step"], 3 * k + 2)
                        V.tensor_tensor(modcol[:, l, s, c, :], stats[0:CW, 0, 0:B], tp[:, s, c, :], ALU.add).then_inc(S["md_step"], 1)
                        dve.wait_ge(S["md_step"], 3 * k + 3)
            dve.wait_ge(S["ld_skew"], 16)
            dve.wait_ge(S["sk_tr"], 1)
            vt = ps[0:RD, 1, 0:B * RD].rearrange("p (b j) -> p b j", b=B)
            V.tensor_tensor(skew[:, :, :], skew[:, :, :], vt, ALU.subtract).then_inc(S["sk_dve"], 1)
            dve.wait_ge(S["sk_dve"], 1)
            for h in range(2):
                V.tensor_scalar(sx[:, h, :, :], skew[:, :, :], (1 - 2 * h) * 2.0 ** -DOUBLINGS, None, ALU.mult).then_inc(S["sk_dve"], 1)
            dve.wait_ge(S["sk_dve"], 3)

            def flat(t):
                return t.rearrange("p h b j -> p (h b j)")

            V.scalar_tensor_tensor(out=flat(ey[:, 0]), in0=flat(sx[:, :, :, :]), scalar=1.0 / TAYLOR, in1=flat(eye8[:, :, :, :]),
                                   op0=ALU.mult, op1=ALU.add).then_inc(S["ex_ev"], 1)
            for i in range(TAYLOR - 1):
                k = TAYLOR - 1 - i
                dve.wait_ge(S["ex_mm"], i + 1)
                if k > 1:
                    V.scalar_tensor_tensor(out=flat(ey[:, (i + 1) % 2]), in0=ps[0:RD, 2 + i % 2, :], scalar=1.0 / k,
                                           in1=flat(eye8[:, :, :, :]), op0=ALU.mult, op1=ALU.add).then_inc(S["ex_ev"], 1)
                else:
                    V.tensor_copy(flat(ey[:, (i + 1) % 2]), ps[0:RD, 2 + i % 2, :]).then_inc(S["ex_ev"], 1)
            with dve.Fori(0, DOUBLINGS // 2) as i:
                for u in range(2):
                    dve.wait_ge(S["ex_mm"], i * 2 + (TAYLOR + u))
                    dve.wait_ge(S["ex_ev"], i * 2 + (TAYLOR + u))
                    q = (TAYLOR - 1 + u) % 2
                    V.scalar_tensor_tensor(out=flat(ey[:, 1 - q]), in0=flat(ey[:, q]), scalar=2.0, in1=ps[0:RD, 2 + q, :],
                                           op0=ALU.mult, op1=ALU.add).then_inc(S["ex_ev"], 1)
            dve.wait_ge(S["ex_ev"], TAYLOR + DOUBLINGS)
            V.tensor_copy(GE[:, :, :], ey[:, (TAYLOR - 1) % 2, 1, :, :]).then_inc(S["setup_done"], 1)

            def layernorm(n, b, eps):
                ln, at0 = S["ln_step"], n * LN_STEPS
                k = [0]

                def step(ins, wait=True):
                    k[0] += 1
                    ins.then_inc(ln, 1)
                    if wait:
                        wait_alone(dve, ln, at0 + k[0], S["dve_passed"])

                x = xres[:, bass.ds(b * TT, TT), :]
                for t in range(TT):
                    step(V.bn_stats(stats[:, t, :], xres[:, bass.ds(b * TT + t, 1), :].rearrange("p a n -> p (a n)")), t == TT - 1)
                for t in range(TT):
                    step(V.bn_aggr(mv[:, t, :], stats[:, t, :]), t == TT - 1)
                var, y, u, w = (nwt[:, i, :] for i in range(4))
                step(V.tensor_scalar(var, mv[:, :, 1], eps, None, ALU.add))
                step(V.tensor_scalar(u.bitcast(I32), var.bitcast(I32), 1, None, ALU.logical_shift_right))
                step(V.tensor_scalar(y.bitcast(I32), u.bitcast(I32), -1.0, float(RSQRT_MAGIC), ALU.mult, ALU.add))
                for _ in range(3):
                    step(V.tensor_tensor(u, y, y, ALU.mult))
                    step(V.scalar_tensor_tensor(out=w, in0=u, scalar=-0.5, in1=var, op0=ALU.mult, op1=ALU.mult))
                    step(V.scalar_tensor_tensor(out=y, in0=w, scalar=1.5, in1=y, op0=ALU.add, op1=ALU.mult))
                assert k[0] == LN_STEPS, k
                dve.wait_ge(S["tr_done"], n * 3 + 3)
                for t in range(TT):
                    V.tensor_scalar(xn[:, t, :], xres[:, bass.ds(b * TT + t, 1), :].rearrange("p a n -> p (a n)"),
                                    mv[:, t, 0:1], y[:, t:t + 1], ALU.subtract, ALU.mult).then_inc(S["xn_ready"], 1)

            def xrow(b, t):
                return xres[:, bass.ds(b * TT + t, 1), :].rearrange("p a n -> p (a n)")

            def gate_row(s, b):
                return gates[:, s, bass.ds(b, 1), :].rearrange("p a n -> p (a n)")

            def attention(l, b):
                it = b + B * l
                layernorm(it * 2, b, EPS[l])
                for m in range(6):
                    rows = QK_TILES[m % 3][1] * HD
                    dve.wait_ge(S["qf_ready"], it * 6 + (m + 1))
                    if m >= 2:
                        heads = sum(QK_TILES[i % 3][1] for i in range(m % 2, m, 2))
                        dve.wait_ge(S[f"stack_ld{m % 2}"], it * (16 * 4 * NH) + 64 * heads)
                    V.tensor_copy(qhi[0:rows, m % 2, :], qf[0:rows, m % 2, :]).then_inc(S["hi_done"], 1)
                    dve.wait_ge(S["hi_done"], it * 6 + (m + 1))
                    V.tensor_tensor(qlo[0:rows, m % 2, :], qf[0:rows, m % 2, :], qhi[0:rows, m % 2, :].bitcast(F32),
                                    ALU.subtract).then_inc(S["split_done"], 1)

                def maxima(g, qt):
                    for i in range(HG):
                        u = (g * TT + qt) * HG + i
                        dve.wait_ge(S["max_mm"], it * 64 + (u + 1))
                        V.tensor_reduce(mx[:, g, qt, i:i + 1], bank(u % 2), AX.X, ALU.max).then_inc(S["mx_done"], 1)

                def negate(g):
                    dve.wait_ge(S["mx_done"], it * 64 + 16 * (g + 1))
                    V.tensor_scalar(nm[:, g, :, 0:HG], mx[:, g, :, :], -1.0, None, ALU.mult).then_inc(S["nh_done"], 1)
                    dve.wait_ge(S["nh_done"], it * NG + (g + 1))
                    V.scalar_tensor_tensor(out=nm[:, g, :, HG:2 * HG], in0=mx[:, g, :, :], scalar=-1.0, in1=nm[:, g, :, 0:HG].bitcast(F32),
                                           op0=ALU.mult, op1=ALU.subtract).then_inc(S["nm_ready"], 1)

                def normalise(g):
                    dve.wait_ge(S["pv_done"], it * 16 + (16 + 4 * g + 4))
                    V.tensor_copy(oc[:, :], bank(6)).then_inc(S["oc_done"], 1)
                    wait_alone(dve, S["oc_done"], it * NG + (g + 1), S["dve_passed"])
                    V.stream_shuffle(osh[:, :], oc[:, :], [HD] * 32).then_inc(S["o_step"], 1)
                    dve.wait_ge(S["o_step"], it * (2 * NG) + (2 * g + 1))
                    V.reciprocal(orc[:, :], osh[:, :]).then_inc(S["o_step"], 1)
                    dve.wait_ge(S["o_step"], it * (2 * NG) + (2 * g + 2))
                    V.tensor_tensor(oT[:, g, :], oc[:, :], orc[:, :], ALU.mult).then_inc(S["oT_ready"], 1)
                    dve.wait_ge(S["oT_ready"], it * NG + (g + 1))

                for qt in range(TT):
                    maxima(0, qt)
                negate(0)
                for t in range(TT):
                    dve.wait_ge(S["v_mm"], it * TT + (t + 1))
                    V.tensor_tensor(vaug[:, t, :, 0:HD], ps[:, 2 + t % 2, 0:C].rearrange("p (h d) -> p h d", h=NH),
                                    rows_b[:, 0, :].rearrange("p (h d) -> p h d", h=NH), ALU.add).then_inc(S["v_ready"], 1)
                for qt in range(TT):
                    maxima(1, qt)
                negate(1)
                for g in range(NG):
                    if g + 2 < NG:
                        maxima(g + 2, 0)
                    if g:
                        normalise(g - 1)
                    if g + 2 < NG:
                        for qt in range(1, TT):
                            maxima(g + 2, qt)
                        negate(g + 2)
                normalise(NG - 1)
                for t in range(TT):
                    dve.wait_ge(S["pj_mm"], it * TT + (t + 1))
                    V.tensor_tensor(orc[:, 0:C], ps[:, t, 0:C], rows_b[:, 1, :], ALU.add).then_inc(S["xa_t"], 1)
                    dve.wait_ge(S["xa_t"], it * TT + (t + 1))
                    V.tensor_tensor(osh[:, 0:C], orc[:, 0:C], gate_row(0, b), ALU.mult).then_inc(S["xa_g"], 1)
                    dve.wait_ge(S["xa_g"], it * TT + (t + 1))
                    V.tensor_tensor(xrow(b, t), xrow(b, t), osh[:, 0:C], ALU.add).then_inc(S["xa_done"], 1)
                wait_alone(dve, S["xa_done"], it * TT + TT, S["dve_passed"])
                layernorm(it * 2 + 1, b, EPS[l])
                if l == 0:
                    top2(b)

            def top2(b):
                k = [0]

                def step(ins, wait=True):
                    k[0] += 1
                    ins.then_inc(S["tk_step"], 1)
                    if wait:
                        dve.wait_ge(S["tk_step"], b * 9 + k[0])

                dve.wait_ge(S["lg_tr"], b + 1)
                lg, e1, rank, sel = (tk[:, i, :, :] for i in range(4))
                gt, eq = tkc[:, 0, :, :, :], tkc[:, 1, :, :, :]
                step(V.tensor_copy(lg, ps[:, 6, 0:TT * NE].rearrange("p (t e) -> p t e", t=TT)))
                step(V.tensor_reduce(tkm[:, 0, :], lg, AX.X, ALU.max))
                V.tensor_tensor(e1, lg, tkm[:, 0, :].unsqueeze(2).to_broadcast([P, TT, NE]), ALU.subtract).then_inc(S["tk_in"], 1)
                me = lg.unsqueeze(3).to_broadcast([P, TT, NE, NE])
                other = lg.unsqueeze(2).to_broadcast([P, TT, NE, NE])
                step(V.tensor_tensor(gt, other, me, ALU.is_gt), False)
                step(V.tensor_tensor(eq, other, me, ALU.is_equal))
                step(V.tensor_tensor(eq, eq, lowmask[:, :, :, :], ALU.mult))
                step(V.tensor_tensor(gt, gt, eq, ALU.add))
                step(V.tensor_reduce(rank, gt, AX.X, ALU.add))
                dve.wait_ge(S["tk_exp"], b + 1)
                step(V.scalar_tensor_tensor(out=sel.rearrange("p t e -> p (t e)"), in0=rank.rearrange("p t e -> p (t e)"), scalar=1.5,
                                            in1=e1.rearrange("p t e -> p (t e)"), op0=ALU.is_lt, op1=ALU.mult))
                step(V.tensor_reduce(tkm[:, 1, :], sel, AX.X, ALU.add))
                V.reciprocal(tkm[:, 0, :], tkm[:, 1, :]).then_inc(S["tk_r"], 1)
                dve.wait_ge(S["tk_r"], b + 1)
                V.tensor_tensor(cw[:, bass.ds(b * TT, TT), :], sel, tkm[:, 0, :].unsqueeze(2).to_broadcast([P, TT, NE]),
                                ALU.mult).then_inc(S["cw_ready"], 1)
                assert k[0] == 9, k

            def mlp(l, e, p, b):
                it = b + B * p
                fin = (e == NE - 1) or l > 0
                fi = b + B * l
                for t in range(TT):
                    dve.wait_ge(S["fc2_mm"], it * TT + (TT + t + 1))
                    V.tensor_tensor(tmp[:, t, :], ps[:, 4 + t, 0:C], b2b[:, :], ALU.add).then_inc(S["evac_done"], 1)
                    dve.wait_ge(S["evac_done"], it * TT + (TT + t + 1))
                    src = tmp[:, t, :]
                    if l == 0:
                        row = acc[:, bass.ds(b * TT + t, 1), :].rearrange("p a n -> p (a n)")
                        wgt = cw[:, bass.ds(b * TT + t, 1), e:e + 1].rearrange("p a n -> p (a n)")
                        if e == 0:
                            V.tensor_scalar(row, src, wgt, None, ALU.mult).then_inc(S["acc_done"], 1)
                        else:
                            V.scalar_tensor_tensor(out=row, in0=src, scalar=wgt, in1=row, op0=ALU.mult, op1=ALU.add).then_inc(S["acc_done"], 1)
                        dve.wait_ge(S["acc_done"], it * TT + (t + 1))
                        src = row
                    if fin:
                        V.tensor_tensor(tmp[:, t, :], src, gate_row(1, b), ALU.mult).then_inc(S["gm_done"], 1)
                        dve.wait_ge(S["gm_done"], fi * TT + (t + 1))
                        V.tensor_tensor(xrow(b, t), xrow(b, t), tmp[:, t, :], ALU.add).then_inc(S["xm_done"], 1)

            dve.wait_ge(S["ld_x"], 16)
            dve.wait_ge(S["mod_stored"], 16 * NL)
            for l in range(NL):
                if l == 1:
                    dve.wait_ge(S["xm_done"], 16)
                if l == 2:
                    with dve.Fori(0, B) as b:
                        for t in range(TT):
                            dve.wait_ge(S["xm_done"], 32)
                            if t == 0:
                                dve.wait_ge(S["xt_tr"], b * KC + KC)
                            V.tensor_copy(xn[:, t, :], xrow(b, t)).then_inc(S["xc_done"], 1)
                        for t in range(TT):
                            dve.wait_ge(S["r_mm"], b * TT + (t + 1))
                            V.tensor_tensor(xrow(b, t), xrow(b, t), ps[:, 4 + t, 0:C], ALU.add).then_inc(S["xr_done"], 1)
                    dve.wait_ge(S["xr_done"], 16)
                dve.wait_ge(S["ld_gate"], 32 * (l + 1))
                dve.wait_ge(S["ld_w"], 48 * (l + 1))
                with dve.Fori(0, B) as b:
                    attention(l, b)
                for e in range(NE if l == 0 else 1):
                    p = e if l == 0 else NE + l - 1
                    dve.wait_ge(S["ld_mlp"], 48 * (p + 1))
                    with dve.Fori(0, B) as b:
                        mlp(l, e, p, b)


def kernel(**inputs):
    import concourse.bacc as bacc
    from concourse.bass_utils import run_bass_kernel_spmd

    x = {k: np.asarray(v) for k, v in inputs.items()}
    f = np.float32

    def split_heads(w):
        o = np.zeros((NH, 32, C), f)
        o[:, :HD] = w.reshape(NH, HD, C)
        return o.reshape(NG, P, C)

    qkv_w = [x["L0_cond_w_qkv"], x["L1_cond_W_qkv"], np.concatenate([x["L3_cond_wq"], x["L3_cond_wk"], x["L3_cond_wv"]], 1)]
    qkv_b = [x["L0_cond_b_qkv"], x["L1_cond_b_qkv"], np.zeros(3 * C, f)]
    proj_w = [x["L0_cond_w_proj"], x["L1_cond_W_proj"], x["L3_cond_wo"]]
    proj_b = [x["L0_cond_b_proj"], x["L1_cond_b_proj"], x["L3_cond_wo_b"]]
    ada_w = [x["L0_cond_w_adaln"], x["L1_cond_W_ada"], x["L3_cond_ada_w"]]
    ada_b = [x["L0_cond_b_adaln"], x["L1_cond_b_ada"], x["L3_cond_ada_b"]]
    fc1_b = [x["L0_cond_b1"], x["L1_cond_b_fc1"][None], x["L3_cond_fc1_b"][None]]
    one, zero = np.ones(C, f), np.zeros(C, f)
    ln = [(one, zero, one, zero)] * 2 + [(x["L3_cond_ln1_w"], x["L3_cond_ln1_b"], x["L3_cond_ln2_w"], x["L3_cond_ln2_b"])]
    cols = np.zeros((P, NL, NCOL), f)
    for l in range(NL):
        for m, (h0, nh) in enumerate(QK_TILES + QK_TILES):
            o = (m // 3) * C + h0 * HD
            cols[:nh * HD, l, m] = qkv_b[l][o:o + nh * HD]
        for i, v in enumerate(ln[l]):
            cols[:CW, l, 6 + 3 * i:9 + 3 * i] = v.reshape(KC, CW).T
        for e, v in enumerate(fc1_b[l]):
            cols[:, l, 18 + NJ * e:18 + NJ * (e + 1)] = v.reshape(NJ, P).T
    iu, ju = np.triu_indices(RD, k=1)
    w_skew = np.zeros((C + 1, RD * RD), f)
    w_skew[:C, iu * RD + ju] = x["L2_cond_W"].T
    w_skew[C, iu * RD + ju] = x["L2_cond_b"]
    low = np.zeros((P, TT, NE, NE), f)
    low[:, :] = np.tril(np.ones((NE, NE), f), -1)
    eye8 = np.zeros((RD, 2, B, RD), f)
    eye8[np.arange(RD), :, :, np.arange(RD)] = 1
    arrays = {
        "x": x["x"], "condT": x["cond_1152"].T, "w_gate": x["L0_cond_w_gate"],
        "w_ada": np.stack([np.concatenate([w, b[None]], 0) for w, b in zip(ada_w, ada_b)]),
        "w_skew": w_skew, "P": x["L2_cond_P"], "cols": cols,
        "wqkv": np.stack(qkv_w), "wproj": np.stack([split_heads(w) for w in proj_w]),
        "rows_b": np.stack([np.stack([qb[2 * C:], pb]) for qb, pb in zip(qkv_b, proj_b)]),
        "w1": np.concatenate([x["L0_cond_w1"], x["L1_cond_W_fc1"][None], x["L3_cond_fc1_w"][None]]),
        "w2": np.concatenate([x["L0_cond_w2"], x["L1_cond_W_fc2"][None], x["L3_cond_fc2_w"][None]]),
        "b2": np.concatenate([x["L0_cond_b2"], x["L1_cond_b_fc2"][None], x["L3_cond_fc2_b"][None]]),
        "ident": np.eye(P, dtype=f), "lowmask": low, "ones": np.ones((2, N), f), "eye8": eye8,
    }
    arrays = {k: np.ascontiguousarray(v) for k, v in arrays.items()}
    nc = bacc.Bacc("TRN2", target_bir_lowering=False, num_devices=1)
    aps = {k: nc.dram_tensor(f"in_{k}", v.shape, mybir.dt.from_np(v.dtype), kind="ExternalInput").ap() for k, v in arrays.items()}
    out = nc.dram_tensor("out", (B, N, C), F32, kind="ExternalOutput").ap()
    bass_cond_seq_kernel(nc, aps, out)
    r = run_bass_kernel_spmd(nc, [{f"in_{k}": v for k, v in arrays.items()}], core_ids=[0])
    return r.results[0]["out"]
```

```python
from contextlib import ExitStack

import numpy as np
import concourse.bass as bass
from concourse import mybir

ALU = mybir.AluOpType
ACT = mybir.ActivationFunctionType
AX = mybir.AxisListType
F32 = mybir.dt.float32
F32R = mybir.dt.float32r
I32 = mybir.dt.int32

B, N, C = 4, 512, 288
NH = 16
HD = C // NH
HID = 4 * C
NE = 4
RD = 64
P = 128
TT = N // P
KC = 3
CW = C // KC
NJ = HID // P
HG = 4
NG = NH // HG
GR = HG * HD
NU = TT * HG
SCALE = float(HD) ** -0.5
DOUBLINGS = 14
TAYLOR = 6
EPS = [1e-6, 1e-6, 1e-5]
NL = 3
MOD = 6 * C
COL_LN = 8
COL_FC = COL_LN + 4 * KC
NCOL = COL_FC + NE * NJ
LN_STEPS = 20
HH_START, HH_FWD, HH_BWD = 4, 27, 7
RSQRT_MAGIC = 0x5F3759DF


def other_work(g, kt, place, prev, nxt, moe):
    work = {(kt_, p): list(w) for kt_, p, w in (
        (0, "A", [("Pq", 3)]), (0, "B", [("Pk", 3)]), (1, "A", [("R", 1)]), (1, "C", [("on", -1)]), (2, "B", [("ob", -1)]))}
    own = {
        0: [(0, "C", [("V", 0), ("V", 1), ("LN1a", 0)]), (1, "B", [("V", 2), ("LN1b", 0)]), (1, "C", [("V", 3)]), (2, "A", [("LN1c", 0)]),
            (2, "C", [("T1", 0)]), (3, "A", [("T1", 1)]), (3, "B", [("T1", 2)])],
        1: [(0, "C", [("pj", 0), ("pj", 1)]), (1, "B", [("pj", 2)]), (1, "C", [("pj", 3)]), (2, "C", [("LN2a", 0)]), (3, "A", [("LN2b", 0)]),
            (3, "B", [("LN2c", 0)])],
        2: [(0, "C", [("T2", 0)]), (1, "B", [("T2", 1)]), (1, "C", [("T2", 2)]), (3, "A", [("lg", 0)])],
        3: [(2, "C", [("lt", 0)]), (3, "A", [("top2", 0)])],
    }[g]
    for kt_, p, w in own:
        work.setdefault((kt_, p), []).extend(w)
    out = []
    for kind, arg in work.get((kt, place), []):
        if kind in ("Pq", "Pk") and g + arg >= NG and not nxt:
            continue
        if kind == "R" and g + arg >= NG and not nxt:
            continue
        if kind in ("on", "ob") and g == 0 and not prev:
            continue
        if kind[:3] in ("T1", "LN1") and not nxt:
            continue
        if kind[:3] in ("pj", "T2", "LN2", "lg", "lt", "top") and not prev:
            continue
        if kind in ("lg", "lt", "top2") and not moe:
            continue
        out.append((kind, arg))
    return out


def walk(tile, others, pv):
    for g in range(NG):
        for kt in range(TT):
            tile(g, kt, (0, 1))
            others(g, kt, "A")
            tile(g, kt, (2, 3))
            others(g, kt, "B")
            pv(g, kt)
            others(g, kt, "C")


def banks_of_other_work():
    table = {}
    n = 0
    for g in range(NG):
        for kt in range(TT):
            for place in "ABC":
                for kind, arg in other_work(g, kt, place, True, True, True):
                    if kind[:2] in ("LN", "to"):
                        continue
                    table[kind, (g + arg) % NG if kind in ("Pq", "Pk", "R", "on", "ob") else arg] = 5 + n % 3
                    n += 1
    return table


BANK = banks_of_other_work()


def wait_alone(eng, sem, value, passed):
    eng.wait_ge(sem, value)
    eng.sem_inc(passed, 1)


def bass_cond_seq_kernel(nc, a, out):
    modd = nc.dram_tensor("mod_rows", [NL, B, MOD], F32).ap()
    qkd = nc.dram_tensor("qk_rows", [2, HG, HD, 4, N], F32).ap()
    vd = nc.dram_tensor("skew_rows", [B, RD * RD], F32).ap()

    with ExitStack() as ctx:
        base = [nc.sbuf_base + 31 & ~31]

        def put(name, shape, dt, at):
            size = 4 * int(np.prod(shape[1:]))
            assert at + size <= nc.sbuf_usable_end, (name, at + size)
            return nc.alloc_sbuf_tensor_at(name, shape, dt, offset=at), at + (size + 31 & ~31)

        def keep(name, shape, dt=F32):
            t, base[0] = put(name, shape, dt, base[0])
            return t

        xres = keep("xres", [P, B * TT, C])
        gates = keep("gates", [P, B, C])
        h2T = keep("h2T", [CW, KC, B * N])
        wqkv = keep("wqkv", [CW, KC, 3 * C])
        wproj = keep("wproj", [P, NG, C])
        rows_b = keep("rows_b", [P, 2, C])
        cols = keep("cols", [P, NL, NCOL])
        modcol = keep("modcol", [CW, NL, 4, KC, B])
        ident = keep("ident", [P, P])
        lowmask = keep("lowmask", [P, TT, NE, NE])
        onesr = keep("onesr", [2, P], F32R)
        wgate = keep("wgate", [CW, KC, NE])
        silu = keep("silu", [CW + 1, KC, B])
        xn = keep("xn", [P, TT, C])
        hT = keep("hT", [CW, KC, N])
        stats = keep("stats", [P, TT, 6])
        mv = keep("mv", [P, TT, 2])
        nwt = keep("nwt", [P, 4, TT])
        qk = keep("qk", [GR, 2, 4, N], F32R)
        vaug = keep("vaug", [P, TT, NH, 32])
        mx = keep("mx", [P, NG, TT, HG])
        nm = keep("nm", [P, NG, TT, 2 * HG], F32R)
        oc = keep("oc", [P, N])
        rsm = keep("rsm", [P, TT, HG])
        rbc = keep("rbc", [P, TT, HG, 32])
        selden = keep("selden", [P, HG])
        tmpx = keep("tmpx", [P, C])
        nmT = keep("nmT", [2 * HG, 2, N], F32R)
        cw = keep("cw", [P, B * TT, NE])
        tk = keep("tk", [P, 4, TT, NE])
        tkm = keep("tkm", [P, 2, TT])
        tkc = keep("tkc", [P, 2, TT, NE, NE])
        U = keep("U", [CW, KC, RD])
        GE = keep("GE", [RD, B, RD])
        hA = keep("hA", [CW, KC, RD])
        hV = keep("hV", [CW, KC, RD])
        hp = keep("hp", [CW, KC, RD])
        hr = keep("hr", [CW, 2 * RD])
        hR = keep("hR", [CW, 2 * RD])
        hC = keep("hC", [CW, RD])
        hs = keep("hs", [CW, 16])
        region = base[0]
        qs, at = put("qs", [P, NH, N], F32R, region)
        ks, at = put("ks", [P, NH, N], F32R, at)
        oT, at = put("oT", [P, NG, N], F32, at)
        pT, at = put("pT", [P, 2 * HG, N], F32, at)
        lgT, at = put("lgT", [NE, N], F32, at)
        shared = at
        acc, at = put("acc", [P, B * TT, C], F32, region)
        w1, at = put("w1", [CW, KC, HID], F32, at)
        w2, at = put("w2", [P, NJ, C], F32, at)
        gT, at = put("gT", [P, NJ, N], F32, at)
        b2b, at = put("b2b", [P, C], F32, at)
        tmp, at = put("tmp", [P, TT, C], F32, at)
        assert at <= shared
        zT, at = put("zT", [RD, N], F32, region)
        EUt, at = put("EUt", [RD, B, C], F32, at)
        hU, at = put("hU", [RD, C], F32, at)
        assert at <= region + 4 * B * TT * C
        ada, at = put("ada", [CW + 1, 2, KC, MOD], F32, region)
        wf, at = put("wf", [CW + 1, 2, KC, 1024], F32, at)
        vsb, at = put("vsb", [B, 2, 512], F32, at)
        modsb, at = put("modsb", [B, MOD], F32, at)
        skew, at = put("skew", [RD, B, RD], F32, at)
        sx, at = put("sx", [RD, 2, B, RD], F32, at)
        ey, at = put("ey", [RD, 2, 2, B, RD], F32, at)
        eye8, at = put("eye8", [RD, 2, B, RD], F32, at)
        assert at <= nc.sbuf_usable_end

        ps = ctx.enter_context(nc.psum_tensor("ps", [P, 8, N], F32))

        def bank(i):
            return ps[:, i, :]

        names = """ld_const ld_x ld_cond ld_wf0 ld_wf1 ld_ada0 ld_ada1 ld_skew ld_gate ld_w ld_mlp ld_p silu_done
            skew_mm skew_out skew_stored0 skew_stored1 sk_tr sk_dve ex_mm ex_ev mod_mm mod_cp mod_stored mod_tr md_step
            ln1_step ln2_step xn1_ready xn2_ready tr1_done tr2_done h1_ready h2_ready
            qk_mm hi_done lo_done qk_st stack_ld0 stack_ld1 stack_ld2 stack_ld3 ones_ld
            v_mm v_ready max_mm mx_done nh_done nm_ready nm_tr nmT_ready nm_ld0 nm_ld1 st_mm exp_done pv_done
            oc_done on_mm rec_done rbc_ready ob_tr oT_ready pj_mm xa_t xa_g xa_done
            lg_mm lg_cp lg_tr tk_step tk_in tk_exp tk_r cw_ready
            fc1_mm gelu_done fc2_mm evac_done acc_done gm_done xm_done
            hh_step u_tr u_cp eu_mm eu_cp xc_done xt_tr xt_cp z_mm z_cp r_mm xr_done
            out_done setup_done pool_passed dve_passed pe_passed""".split()
        S = {n: ctx.enter_context(nc.semaphore(n)) for n in names}
        block = ctx.enter_context(nc.Block())

        @block.sync
        def _(sp):
            for dst, src in ((ident[:, :], a["ident"]), (cols[:, :, :], a["cols"]),
                             (lowmask[:, :, :, :], a["lowmask"]),
                             (wgate[:, :, :], a["w_gate"].rearrange("(c p) e -> p c e", p=CW)),
                             (onesr[:, :].bitcast(F32), a["ones"]), (selden[:, :], a["selden"]), (eye8[:, :, :, :], a["eye8"])):
                sp.dma_start(dst, src).then_inc(S["ld_const"], 16)
            sp.dma_start(silu[0:CW, :, :], a["condT"].rearrange("(c p) b -> p c b", p=CW)).then_inc(S["ld_cond"], 16)

            def load_wf(k):
                src = a["w_skew"][:, k * 1024:(k + 1) * 1024]
                sp.dma_start(wf[0:CW, k % 2, 0:2, :], src[0:2 * CW].rearrange("(c p) n -> p c n", p=CW)).then_inc(S[f"ld_wf{k % 2}"], 16)
                sp.dma_start(wf[:, k % 2, 2, :], src[2 * CW:C + 1]).then_inc(S[f"ld_wf{k % 2}"], 16)

            def load_ada(l):
                src = a["w_ada"][l]
                sp.dma_start(ada[0:CW, l % 2, 0:2, :], src[0:2 * CW].rearrange("(c p) n -> p c n", p=CW)).then_inc(S[f"ld_ada{l % 2}"], 16)
                sp.dma_start(ada[:, l % 2, 2, :], src[2 * CW:C + 1]).then_inc(S[f"ld_ada{l % 2}"], 16)

            load_wf(0)
            load_wf(1)
            load_ada(0)
            load_ada(1)
            for k in (2, 3):
                sp.wait_ge(S["skew_mm"], 2 * (k - 1))
                load_wf(k)
            sp.wait_ge(S["mod_mm"], 4)
            load_ada(2)
            for u in range(2):
                sp.wait_ge(S[f"skew_stored{u}"], 4 * 16)
            sp.dma_start(skew[:, :, :], vd.rearrange("b (i j) -> i b j", i=RD)).then_inc(S["ld_skew"], 16)

            for l in range(NL):
                if l == 2:
                    sp.wait_ge(S["xr_done"], TT * B)
                sp.wait_ge(S["mod_stored"], 16 * NL)
                if l == 0:
                    sp.wait_ge(S["setup_done"], 1)
                else:
                    sp.wait_ge(S["fc2_mm"], 16 * (NE + l - 1) + TT)
                if l:
                    sp.wait_ge(S["xm_done"], 16 * l)
                sp.dma_start(gates[:, :, :], modd[l, :, 2 * C:3 * C].partition_broadcast(P)).then_inc(S["ld_gate"], 16)
                sp.dma_start(wqkv[:, :, :], a["wqkv"][l].rearrange("(c p) n -> p c n", p=CW)).then_inc(S["ld_w"], 16)
                sp.dma_start(wproj[:, :, :], a["wproj"][l].rearrange("g p n -> p g n")).then_inc(S["ld_w"], 16)
                sp.dma_start(rows_b[:, :, :], a["rows_b"][l].partition_broadcast(P)).then_inc(S["ld_w"], 16)
                sp.dma_start(ks[4 * HD:4 * HD + 2, :, :].rearrange("r h (t n) -> r (h t) n", n=P).bitcast(F32),
                             onesr[:, :].bitcast(F32).unsqueeze(1).to_broadcast([2, NH * TT, P])).then_inc(S["ones_ld"], 16)

                def stack(G, g):
                    sp.wait_ge(S["lo_done"], G * 2 + 2)
                    sp.wait_ge(S["pv_done"], G * TT + TT)
                    sp.dma_start(qkd[g % 2].rearrange("h d a n -> (h d) a n"), qk[:, g % 2, :, :].bitcast(F32)).then_inc(S["qk_st"], 16)
                    sp.wait_ge(S["qk_st"], G * 16 + 16)
                    for to, parts in ((qs, (0, 0, 1, 1)), (ks, (2, 3, 2, 3))):
                        for row, part in enumerate(parts):
                            sp.dma_start(to[HD * row:HD * row + HD, HG * g:HG * g + HG, :].bitcast(F32),
                                         qkd[g % 2, :, :, part, :].rearrange("h d n -> d h n")).then_inc(S[f"stack_ld{g}"], 16)

                def maxima(G, g):
                    sp.wait_ge(S["nmT_ready"], G + 1)
                    for row in range(2):
                        sp.dma_start(qs[4 * HD + row:4 * HD + row + 1, HG * g:HG * g + HG, :].bitcast(F32),
                                     nmT[HG * row:HG * row + HG, g % 2, :].bitcast(F32)).then_inc(S[f"nm_ld{g % 2}"], 16)

                G0 = NG * B * l
                for g in range(3):
                    stack(G0 + g, g)
                maxima(G0, 0)
                with sp.Fori(0, B - 1) as b:
                    for g in range(NG):
                        stack(b * NG + (G0 + g + 3), (g + 3) % NG)
                        maxima(b * NG + (G0 + g + 1), (g + 1) % NG)
                for g in range(NG - 1):
                    if g == 0:
                        stack(G0 + NG * B - 1, NG - 1)
                    maxima(G0 + NG * (B - 1) + g + 1, g + 1)
                sp.wait_ge(S["h2_ready"], KC * B * (l + 1))
                if l == 0:
                    sp.wait_ge(S["cw_ready"], B)
                sp.wait_ge(S["xa_done"], 16 * (l + 1))
                sp.dma_start(gates[:, :, :], modd[l, :, 5 * C:6 * C].partition_broadcast(P)).then_inc(S["ld_gate"], 16)
                for e in range(NE if l == 0 else 1):
                    p = e if l == 0 else NE + l - 1
                    if e:
                        sp.wait_ge(S["fc2_mm"], 16 * p + TT)
                        sp.wait_ge(S["evac_done"], 16 * p + TT)
                    sp.dma_start(w1[:, :, :], a["w1"][p].rearrange("(c p) n -> p c n", p=CW)).then_inc(S["ld_mlp"], 16)
                    sp.dma_start(w2[:, :, :], a["w2"][p].rearrange("(j p) n -> p j n", p=P)).then_inc(S["ld_mlp"], 16)
                    sp.dma_start(b2b[:, :], a["b2"][p].partition_broadcast(P)).then_inc(S["ld_mlp"], 16)
            with sp.Fori(0, B) as b:
                sp.wait_ge(S["xm_done"], b * TT + (2 * TT * B + TT))
                sp.dma_start(out.rearrange("b (t p) c -> p (b t) c", p=P)[:, bass.ds(b * TT, TT), :],
                             xres[:, bass.ds(b * TT, TT), :]).then_inc(S["out_done"], 16)
            sp.wait_ge(S["out_done"], 16 * B)

        @block.gpsimd
        def _(pool):
            g = nc.gpsimd
            RED = bass.bass_isa.ReduceOp.add
            pool.dma_start(hA[:, :, :], a["P"].rearrange("(c p) d -> p c d", p=CW)).then_inc(S["ld_p"], 16)
            pool.wait_ge(S["ld_const"], 16 * 7)
            g.memset(hs[:, :], 0.5).then_inc(S["hh_step"], 1)
            g.memset(U[:, :, :], 0.0).then_inc(S["hh_step"], 1)
            pool.wait_ge(S["hh_step"], 2)
            g.tensor_copy(U[0:RD, 0, :], ident[0:RD, 0:RD]).then_inc(S["hh_step"], 1)
            g.memset(hs[:, 1:2], -1.0).then_inc(S["hh_step"], 1)
            pool.wait_ge(S["hh_step"], HH_START)
            pool.wait_ge(S["ld_p"], 16)
            half, neg, sig, nrm, al, sg, sn, den, c, idj, keepj = (hs[:, i:i + 1] for i in range(11))
            wide = [CW, KC, RD]

            with pool.Fori(0, RD) as j:
                n = [0]

                def step(ins):
                    n[0] += 1
                    ins.then_inc(S["hh_step"], 1)
                    wait_alone(pool, S["hh_step"], j * HH_FWD + (HH_START + n[0]), S["pool_passed"])

                vj = hV[:, :, bass.ds(j, 1)]
                step(g.tensor_copy(vj, hA[:, :, bass.ds(j, 1)]))
                step(g.tensor_copy(idj, ident[0:CW, bass.ds(j, 1)]))
                step(g.tensor_tensor(hp[:, :, :], hA[:, :, :], vj.to_broadcast(wide), ALU.mult))
                step(g.tensor_tensor(hp[:, 0, :], hp[:, 0, :], hp[:, 1, :], ALU.add))
                step(g.tensor_tensor(hr[:, 0:RD], hp[:, 0, :], hp[:, 2, :], ALU.add))
                step(g.tensor_scalar(hr[:, RD:2 * RD], hA[:, 0, :], idj, 1.0, ALU.mult, ALU.mult))
                step(g.partition_all_reduce(hR[:, :], hr[:, :], CW, RED))
                step(g.tensor_copy(sig, hR[:, bass.ds(j, 1)]))
                step(g.tensor_copy(al, hR[:, bass.ds(j + RD, 1)]))
                step(g.tensor_tensor(nrm, sig, half, ALU.pow))
                step(g.tensor_scalar(sg, al, 0.0, 2.0, ALU.is_ge, ALU.mult))
                step(g.tensor_scalar(sg, sg, 1.0, -1.0, ALU.mult, ALU.add))
                step(g.tensor_tensor(sn, nrm, sg, ALU.mult))
                step(g.tensor_tensor(den, al, sn, ALU.mult))
                step(g.tensor_tensor(den, den, sig, ALU.add))
                step(g.tensor_scalar(den, den, 1e-37, 1e38, ALU.max, ALU.min))
                step(g.tensor_tensor(c, den, neg, ALU.pow))
                step(g.tensor_copy(hC[:, bass.ds(j, 1)], c))
                step(g.tensor_tensor(sig, idj, sn, ALU.mult))
                step(g.tensor_tensor(hV[:, 0, bass.ds(j, 1)], hV[:, 0, bass.ds(j, 1)], sig, ALU.add))
                step(g.tensor_scalar(hr[:, 0:RD], hR[:, RD:2 * RD], sn, 1.0, ALU.mult, ALU.mult))
                step(g.tensor_tensor(hr[:, 0:RD], hr[:, 0:RD], hR[:, 0:RD], ALU.add))
                step(g.tensor_scalar(hr[:, 0:RD], hr[:, 0:RD], c, 1.0, ALU.mult, ALU.mult))
                step(g.tensor_tensor(hp[:, :, :], hr[:, 0:RD].unsqueeze(1).to_broadcast(wide), vj.to_broadcast(wide), ALU.mult))
                step(g.tensor_tensor(hA[:, :, :], hA[:, :, :], hp[:, :, :], ALU.subtract))
                step(g.tensor_scalar(keepj, idj, -1.0, 1.0, ALU.mult, ALU.add))
                step(g.tensor_scalar(hA[:, 0, :], hA[:, 0, :], keepj, 1.0, ALU.mult, ALU.mult))
                assert n[0] == HH_FWD, n
            with pool.Fori(0, RD) as i:
                j = (RD - 1) - i
                n = [0]

                def step(ins):
                    n[0] += 1
                    ins.then_inc(S["hh_step"], 1)
                    wait_alone(pool, S["hh_step"], i * HH_BWD + (HH_START + RD * HH_FWD + n[0]), S["pool_passed"])

                vj = hV[:, :, bass.ds(j, 1)]
                step(g.tensor_tensor(hp[:, :, :], U[:, :, :], vj.to_broadcast(wide), ALU.mult))
                step(g.tensor_tensor(hp[:, 0, :], hp[:, 0, :], hp[:, 1, :], ALU.add))
                step(g.tensor_tensor(hr[:, 0:RD], hp[:, 0, :], hp[:, 2, :], ALU.add))
                step(g.partition_all_reduce(hR[:, 0:RD], hr[:, 0:RD], CW, RED))
                step(g.tensor_tensor(hr[:, 0:RD], hR[:, 0:RD], hC[:, bass.ds(j, 1)].to_broadcast([CW, RD]), ALU.mult))
                step(g.tensor_tensor(hp[:, :, :], hr[:, 0:RD].unsqueeze(1).to_broadcast(wide), vj.to_broadcast(wide), ALU.mult))
                step(g.tensor_tensor(U[:, :, :], U[:, :, :], hp[:, :, :], ALU.subtract))
                assert n[0] == HH_BWD, n

        @block.tensor
        def _(pe):
            mm, tr = nc.tensor.matmul, nc.tensor.transpose
            pe.sem_inc(S["tr2_done"], 2 * KC)
            pe.sem_inc(S["pv_done"], 16)
            pe.sem_inc(S["fc2_mm"], TT)
            pe.sem_inc(S["xt_tr"], KC)
            pe.wait_ge(S["silu_done"], 2)

            for n in range(8):
                if n % 2 == 0:
                    pe.wait_ge(S[f"ld_wf{n // 2 % 2}"], 32 * (n // 4 + 1))
                if n >= 4:
                    pe.wait_ge(S["skew_out"], n - 3)
                for c in range(KC):
                    k = CW + (c == KC - 1)
                    ins = mm(ps[0:B, n % 4, :], silu[0:k, c, :], wf[0:k, (n // 2) % 2, c, (n % 2) * 512:(n % 2) * 512 + 512],
                             start=(c == 0), stop=(c == KC - 1))
                ins.then_inc(S["skew_mm"], 1)
            pe.wait_ge(S["ld_const"], 16 * 7)
            MC = MOD // 4
            for l in range(NL):
                pe.wait_ge(S[f"ld_ada{l % 2}"], 32 * (l // 2 + 1))
                if l:
                    pe.wait_ge(S["mod_cp"], 4 * l)
                for n in range(4):
                    for c in range(KC):
                        k = CW + (c == KC - 1)
                        ins = mm(ps[0:B, 4 + n, 0:MC], silu[0:k, c, :], ada[0:k, l % 2, c, n * MC:(n + 1) * MC],
                                 start=(c == 0), stop=(c == KC - 1))
                    ins.then_inc(S["mod_mm"], 1)
                if l:
                    pe.wait_ge(S["md_step"], 18 * l)
                else:
                    pe.wait_ge(S["skew_out"], 8)
                pe.wait_ge(S["mod_cp"], 4 * (l + 1))
                for s, sec in enumerate((0, 1, 3, 4)):
                    for c in range(KC):
                        q = (s * KC + c) * B
                        ins = tr(ps[0:CW, 0, q:q + B], modsb[:, sec * C + c * CW:sec * C + (c + 1) * CW], ident[0:B, 0:B])
                ins.then_inc(S["mod_tr"], 1)
            pe.wait_ge(S["ld_skew"], 16)
            for b in range(B):
                ins = tr(ps[0:RD, 1, b * RD:(b + 1) * RD], skew[:, b, :], ident[0:RD, 0:RD])
            ins.then_inc(S["sk_tr"], 1)

            def pair_products(to, left, right):
                for h in range(2):
                    for b in range(B):
                        q = (h * B + b) * RD
                        ins = mm(ps[0:RD, to, q:q + RD], left[:, 1 - h, b, :], right[:, h, b, :], start=True, stop=True)
                ins.then_inc(S["ex_mm"], 1)

            for i in range(TAYLOR - 1):
                pe.wait_ge(S["ex_ev"], i + 1)
                pair_products(2 + i % 2, sx, ey[:, i % 2])
            with pe.Fori(0, DOUBLINGS // 2) as i:
                for u in range(2):
                    wait_alone(pe, S["ex_ev"], i * 2 + (TAYLOR + u), S["pe_passed"])
                    e = ey[:, (TAYLOR - 1 + u) % 2]
                    pair_products(2 + (TAYLOR - 1 + u) % 2, e, e)

            def attention_work(l, b, prev, nxt):
                G, it = b * NG + B * NG * l, b + B * l
                reads = {}

                def bank_free(kind, key, sem, value):
                    n = BANK[kind, key]
                    if n in reads:
                        pe.wait_ge(S[reads[n][0]], reads[n][1])
                    reads[n] = (sem, value)
                    return n

                def qk_tile(g, what):
                    n = bank_free(("Pq", "Pk")[what], g % NG, "lo_done", G * 2 + (2 * g + what + 1))
                    o = what * C + (g % NG) * GR
                    if g % NG == 0:
                        pe.wait_ge(S["h1_ready"], (it + g // NG) * KC + KC)
                    for c in range(KC):
                        ins = mm(ps[0:GR, n, :], wqkv[:, c, o:o + GR], hT[:, c, :], start=(c == 0), stop=(c == KC - 1))
                    ins.then_inc(S["qk_mm"], 1)

                def v_tile(t):
                    n = bank_free("V", t, "v_ready", it * TT + (t + 1))
                    for c in range(KC):
                        ins = mm(ps[:, n, 0:C], hT[:, c, t * P:(t + 1) * P], wqkv[:, c, 2 * C:3 * C], start=(c == 0), stop=(c == KC - 1))
                    ins.then_inc(S["v_mm"], 1)

                def turn_maxima(g):
                    n = bank_free("R", g % NG, "nmT_ready", G + (g + 1))
                    pe.wait_ge(S["nm_ready"], G + (g + 1))
                    for qt in range(TT):
                        ins = tr(ps[0:2 * HG, n, qt * P:(qt + 1) * P], nm[:, g % NG, qt, :].bitcast(F32), ident[:, :])
                    ins.then_inc(S["nm_tr"], 1)

                def row_sums(g):
                    n = bank_free("on", g % NG, "rec_done", G + (g + 1))
                    pe.wait_ge(S["oc_done"], G + (g + 2))
                    for qt in range(TT):
                        ins = mm(ps[:, n, qt * HG:(qt + 1) * HG], oc[:, qt * P:(qt + 1) * P], selden[:, :], start=True, stop=True)
                    ins.then_inc(S["on_mm"], 1)

                def turn_reciprocals(g):
                    n = bank_free("ob", g % NG, "oT_ready", G + (g + 2))
                    pe.wait_ge(S["rbc_ready"], G + (g + 1))
                    for qt in range(TT):
                        ins = tr(ps[:, n, qt * P:(qt + 1) * P], rbc[:, qt, :, :].rearrange("p h r -> p (h r)"), ident[:, :])
                    ins.then_inc(S["ob_tr"], 1)

                def turn_layernorm(which, c, i):
                    ready, done, read = (("xn1_ready", "tr1_done", "h1_ready"), ("xn2_ready", "tr2_done", "h2_ready"))[which - 1]
                    n = bank_free(f"T{which}", c, read, i * KC + (c + 1))
                    if c == 0:
                        pe.wait_ge(S[ready], i * TT + TT)
                    for t in range(TT):
                        ins = tr(ps[0:CW, n, t * P:(t + 1) * P], xn[:, t, c * CW:(c + 1) * CW], ident[:, :])
                    ins.then_inc(S[done], 1)

                def projection(t, i):
                    n = bank_free("pj", t, "xa_t", i * TT + (t + 1))
                    if t == 0:
                        pe.wait_ge(S["oT_ready"], i * NG + (NG + 1))
                    for g in range(NG):
                        ins = mm(ps[:, n, 0:C], oT[:, g, t * P:(t + 1) * P], wproj[:, g, :], start=(g == 0), stop=(g == NG - 1))
                    ins.then_inc(S["pj_mm"], 1)

                def gate_logits(i, bb):
                    n = bank_free("lg", 0, "lg_cp", i + 1)
                    pe.wait_ge(S["h2_ready"], i * KC + KC)
                    for c in range(KC):
                        ins = mm(ps[0:NE, n, :], wgate[:, c, :], h2T[:, c, bass.ds(bb * N, N)], start=(c == 0), stop=(c == KC - 1))
                    ins.then_inc(S["lg_mm"], 1)

                def turn_logits(i):
                    n = bank_free("lt", 0, "tk_in", i + 1)
                    wait_alone(pe, S["lg_cp"], i + 1, S["pe_passed"])
                    for t in range(TT):
                        ins = tr(ps[:, n, t * NE:(t + 1) * NE], lgT[:, t * P:(t + 1) * P], ident[0:NE, 0:NE])
                    ins.then_inc(S["lg_tr"], 1)

                def max_tiles(g, qt, which):
                    if qt == 0 and which[0] == 0:
                        pe.wait_ge(S[f"stack_ld{g % NG}"], G * 32 + (128 * (g // NG) + 128))
                    for i in which:
                        u = 16 * g + qt * HG + i
                        if u >= 2 or not isinstance(G, int) or G > 0:
                            pe.wait_ge(S["mx_done"], G * NU + (u - 1))
                        h = (g % NG) * HG + i
                        ins = mm(bank(i % 2), qs[0:4 * HD, h, qt * P:(qt + 1) * P], ks[0:4 * HD, h, :], start=True, stop=True)
                        ins.then_inc(S["max_mm"], 1)

                def score_tiles(g, kt, which):
                    if kt == 0 and which[0] == 0:
                        pe.wait_ge(S[f"nm_ld{g % 2}"], G * 16 + (32 * (g // 2) + 32))
                        pe.wait_ge(S["ones_ld"], 16 * (l + 1))
                    for i in which:
                        h = g * HG + i
                        pe.wait_ge(S["exp_done"], G * NU + (NU * g + kt * HG + i + 1))
                        ins = mm(bank(2 + i % 2), ks[0:4 * HD + 2, h, kt * P:(kt + 1) * P], qs[0:4 * HD + 2, h, :], start=True, stop=True)
                        ins.then_inc(S["st_mm"], 1)

                def value_products(g, kt):
                    pe.wait_ge(S["exp_done"], G * NU + (NU * g + kt * HG + HG + 2))
                    if kt == 0:
                        pe.wait_ge(S["oc_done"], G + (g + 1))
                    if g == 0:
                        pe.wait_ge(S["v_ready"], it * TT + (kt + 1))
                    for i in range(HG):
                        ins = mm(ps[32 * i:32 * i + 32, 4, :], vaug[:, kt, g % NG * HG + i, :], pT[:, kt % 2 * HG + i, :],
                                 start=(kt == 0), stop=(kt == TT - 1), tile_position=(0, 32 * i))
                    ins.then_inc(S["pv_done"], 1)

                def tiles(g, kt, which):
                    for i in which:
                        score_tiles(g, kt, (i,))
                        if g + 2 < NG or nxt:
                            max_tiles(g + 2, kt, (i,))

                def others(g, kt, place):
                    for kind, arg in other_work(g, kt, place, prev, nxt, l == 0):
                        if kind in ("Pq", "Pk"):
                            qk_tile(g + arg, int(kind == "Pk"))
                        elif kind == "R":
                            turn_maxima(g + arg)
                        elif kind == "on":
                            row_sums(g + arg)
                        elif kind == "ob":
                            turn_reciprocals(g + arg)
                        elif kind == "V":
                            v_tile(arg)
                        elif kind == "T1":
                            turn_layernorm(1, arg, it + 1)
                        elif kind == "pj":
                            projection(arg, it - 1)
                        elif kind == "T2":
                            turn_layernorm(2, arg, it - 1)
                        elif kind == "lg":
                            gate_logits(it - 1, b - 1)
                        elif kind == "lt":
                            turn_logits(it - 1)

                def pv(g, kt):
                    if kt:
                        value_products(g, kt - 1)
                    elif g or prev:
                        value_products(g - 1, TT - 1)

                def all_read():
                    for sem, value in reads.values():
                        pe.wait_ge(S[sem], value)

                def start():
                    for c in range(KC):
                        turn_layernorm(1, c, it)
                    for g in range(3):
                        for what in range(2):
                            qk_tile(g, what)
                    for g in range(2):
                        for qt in range(TT):
                            max_tiles(g, qt, range(HG))
                        if g == 0:
                            pass
                    turn_maxima(0)
                    all_read()

                def steps():
                    walk(tiles, others, pv)
                    all_read()

                def end():
                    value_products(NG - 1, TT - 1)
                    row_sums(NG - 1)
                    turn_reciprocals(NG - 1)
                    for t in range(TT):
                        projection(t, it)
                    for c in range(KC):
                        turn_layernorm(2, c, it)
                    if l == 0:
                        gate_logits(it, b)
                        turn_logits(it)
                    all_read()

                return start, steps, end

            def mlp(p, b):
                it = b + B * p
                for j in range(NJ):
                    if j >= 3:
                        pe.wait_ge(S["gelu_done"], it * NJ + (j - 2))
                    for c in range(KC):
                        ins = mm(bank(j % 3), w1[:, c, j * P:(j + 1) * P], h2T[:, c, bass.ds(b * N, N)], start=(c == 0), stop=(c == KC - 1))
                    ins.then_inc(S["fc1_mm"], 1)
                pe.wait_ge(S["evac_done"], it * TT + TT)
                for t in range(TT):
                    for j in range(NJ):
                        if t == 0:
                            pe.wait_ge(S["gelu_done"], it * NJ + (j + 1))
                        ins = mm(ps[:, 4 + t, 0:C], gT[:, j, t * P:(t + 1) * P], w2[:, j, :], start=(j == 0), stop=(j == NJ - 1))
                    ins.then_inc(S["fc2_mm"], 1)

            def rotation():
                pe.wait_ge(S["hh_step"], HH_START + RD * (HH_FWD + HH_BWD))
                for c in range(KC):
                    ins = tr(ps[0:RD, 3, c * CW:(c + 1) * CW], U[:, c, :], ident[0:CW, 0:CW])
                ins.then_inc(S["u_tr"], 1)
                pe.wait_ge(S["u_cp"], 1)
                for b in range(B):
                    pe.wait_ge(S["evac_done"], 16 * (NE + 1) + TT)
                    ins = mm(ps[0:RD, 4 + b, 0:C], GE[:, b, :], hU[:, :], start=True, stop=True)
                ins.then_inc(S["eu_mm"], 1)
                pe.wait_ge(S["eu_cp"], 1)
                with pe.Fori(0, B) as b:
                    pe.wait_ge(S["xc_done"], b * TT + TT)
                    for c in range(KC):
                        for t in range(TT):
                            ins = tr(ps[0:CW, c, t * P:(t + 1) * P], xn[:, t, c * CW:(c + 1) * CW], ident[:, :])
                        ins.then_inc(S["xt_tr"], 1)
                    for c in range(KC):
                        pe.wait_ge(S["xt_cp"], b * KC + (c + 1))
                        ins = mm(ps[0:RD, 3, :], U[:, c, :], hT[:, c, :], start=(c == 0), stop=(c == KC - 1))
                    ins.then_inc(S["z_mm"], 1)
                    pe.wait_ge(S["z_cp"], b + 1)
                    for t in range(TT):
                        ins = mm(ps[:, 4 + t, 0:C], zT[:, t * P:(t + 1) * P], EUt[:, bass.ds(b, 1), :].rearrange("p a n -> p (a n)"), start=True, stop=True)
                        ins.then_inc(S["r_mm"], 1)

            for l in range(NL):
                if l == 2:
                    rotation()
                pe.wait_ge(S["ld_w"], 48 * (l + 1))
                attention_work(l, 0, False, True)[0]()
                attention_work(l, 0, False, True)[1]()
                with pe.Fori(1, B - 1) as b:
                    attention_work(l, b, True, True)[1]()
                attention_work(l, B - 1, True, False)[1]()
                attention_work(l, B - 1, True, False)[2]()
                for e in range(NE if l == 0 else 1):
                    p = e if l == 0 else NE + l - 1
                    pe.wait_ge(S["ld_mlp"], 48 * (p + 1))
                    pe.wait_ge(S["h2_ready"], KC * B * (l + 1))
                    with pe.Fori(0, B) as b:
                        mlp(p, b)

        @block.scalar
        def _(act):
            A = nc.scalar.activation
            act.sem_inc(S["exp_done"], 2)
            act.sem_inc(S["oc_done"], 1)
            act.dma_start(xres[:, :, :], a["x"].rearrange("b (t p) c -> p (b t) c", p=P)).then_inc(S["ld_x"], 16)
            act.wait_ge(S["ld_cond"], 16)
            A(silu[0:CW, :, :], silu[0:CW, :, :], ACT.Silu).then_inc(S["silu_done"], 1)
            for n in range(8):
                act.wait_ge(S["skew_mm"], n + 1)
                if n >= 2:
                    act.wait_ge(S[f"skew_stored{n % 2}"], 16 * (n // 2))
                A(vsb[:, n % 2, :], ps[0:B, n % 4, :], ACT.Copy).then_inc(S["skew_out"], 1)
                act.wait_ge(S["skew_out"], n + 1)
                act.dma_start(vd[:, n * 512:(n + 1) * 512], vsb[:, n % 2, :]).then_inc(S[f"skew_stored{n % 2}"], 16)
            for l in range(NL):
                if l:
                    act.wait_ge(S["mod_stored"], 16 * l)
                    act.wait_ge(S["mod_tr"], l)
                for n in range(4):
                    act.wait_ge(S["mod_mm"], 4 * l + n + 1)
                    A(modsb[:, n * (MOD // 4):(n + 1) * (MOD // 4)], ps[0:B, 4 + n, 0:MOD // 4], ACT.Copy).then_inc(S["mod_cp"], 1)
                act.wait_ge(S["mod_cp"], 4 * l + 4)
                act.dma_start(modd[l], modsb[:, :]).then_inc(S["mod_stored"], 16)

            def attention_work(l, b, prev, nxt):
                G, it = b * NG + B * NG * l, b + B * l

                def high_part(g, what):
                    act.wait_ge(S["qk_mm"], G * 2 + (2 * g + what + 1))
                    if isinstance(G, int) and G + g < 2:
                        pass
                    elif what == 0:
                        act.wait_ge(S["qk_st"], G * 16 + 16 * (g - 1))
                    A(qk[:, g % 2, 2 * what, :], ps[0:GR, BANK[("Pq", "Pk")[what], g % NG], :], ACT.Identity,
                      bias=cols[0:GR, l, NG * what + g % NG:NG * what + g % NG + 1]).then_inc(S["hi_done"], 1)

                def maxima_out(g):
                    act.wait_ge(S["nm_tr"], G + (g + 1))
                    A(nmT[:, g % 2, :], ps[0:2 * HG, BANK["R", g % NG], :], ACT.Copy).then_inc(S["nmT_ready"], 1)

                def layernorm_out(which, c, i, bb):
                    act.wait_ge(S[f"tr{which}_done"], i * KC + (c + 1 + 2 * KC * (which == 2)))
                    if which == 1:
                        act.wait_ge(S["v_mm"], i * TT) if not (isinstance(i, int) and i == 0) else None
                        dst = hT[:, c, :]
                    else:
                        dst = h2T[:, c, bass.ds(bb * N, N)]
                    A(dst, ps[0:CW, BANK[f"T{which}", c], :], ACT.Identity, bias=modcol[:, l, 2 * which - 2, c, bass.ds(bb, 1)],
                      scale=modcol[:, l, 2 * which - 1, c, bass.ds(bb, 1)]).then_inc(S[f"h{which}_ready"], 1)

                def sums_out(g):
                    act.wait_ge(S["pv_done"], G * TT + (TT * (g + 1) + 16))
                    act.wait_ge(S["oT_ready"], G + (g + 1))
                    A(oc[:, :], bank(4), ACT.Copy).then_inc(S["oc_done"], 1)

                def exps(g, kt, which):
                    for i in which:
                        act.wait_ge(S["st_mm"], G * NU + (NU * g + kt * HG + i + 1))
                        act.wait_ge(S["pv_done"], G * TT + (TT * g + kt + 15))
                        A(pT[:, kt % 2 * HG + i, :], bank(2 + i % 2), ACT.Exp, scale=SCALE).then_inc(S["exp_done"], 1)

                def logits_out(i):
                    act.wait_ge(S["lg_mm"], i + 1)
                    A(lgT[:, :], ps[0:NE, BANK["lg", 0], :], ACT.Copy).then_inc(S["lg_cp"], 1)

                def top2_exp(i):
                    act.wait_ge(S["tk_in"], i + 1)
                    A(tk[:, 1, :, :], tk[:, 1, :, :], ACT.Exp).then_inc(S["tk_exp"], 1)

                def others(g, kt, place):
                    for kind, arg in other_work(g, kt, place, prev, nxt, l == 0):
                        if kind in ("Pq", "Pk"):
                            high_part(g + arg, int(kind == "Pk"))
                        elif kind == "R":
                            maxima_out(g + arg)
                        elif kind == "T1":
                            layernorm_out(1, arg, it + 1, b + 1)
                        elif kind == "T2":
                            layernorm_out(2, arg, it - 1, b - 1)
                        elif kind == "lg":
                            logits_out(it - 1)
                        elif kind == "top2":
                            top2_exp(it - 1)

                def pv(g, kt):
                    if kt == 0 and (g or prev):
                        sums_out(g - 1)

                def start():
                    for c in range(KC):
                        layernorm_out(1, c, it, b)
                    for g in range(3):
                        for what in range(2):
                            high_part(g, what)
                    maxima_out(0)

                def steps():
                    walk(exps, others, pv)

                def end():
                    sums_out(NG - 1)
                    for c in range(KC):
                        layernorm_out(2, c, it, b)
                    if l == 0:
                        logits_out(it)
                        top2_exp(it)

                return start, steps, end

            def mlp(l, e, p, b):
                it = b + B * p
                act.wait_ge(S["fc2_mm"], it * TT + TT)
                for j in range(NJ):
                    act.wait_ge(S["fc1_mm"], it * NJ + (j + 1))
                    A(gT[:, j, :], bank(j % 3), ACT.Gelu if l == 2 else ACT.Gelu_apprx_tanh,
                      bias=cols[:, l, COL_FC + NJ * e + j:COL_FC + NJ * e + j + 1]).then_inc(S["gelu_done"], 1)

            for l in range(NL):
                if l == 2:
                    act.wait_ge(S["u_tr"], 1)
                    A(hU[:, :], ps[0:RD, 3, 0:C], ACT.Copy).then_inc(S["u_cp"], 1)
                    act.wait_ge(S["eu_mm"], 1)
                    A(EUt[:, :, :], ps[0:RD, 4:8, 0:C], ACT.Copy).then_inc(S["eu_cp"], 1)
                    with act.Fori(0, B) as b:
                        for c in range(KC):
                            act.wait_ge(S["xt_tr"], b * KC + (KC + c + 1))
                            A(hT[:, c, :], ps[0:CW, c, :], ACT.Copy).then_inc(S["xt_cp"], 1)
                        act.wait_ge(S["z_mm"], b + 1)
                        A(zT[:, :], ps[0:RD, 3, :], ACT.Copy).then_inc(S["z_cp"], 1)
                act.wait_ge(S["md_step"], 18 * (l + 1))
                attention_work(l, 0, False, True)[0]()
                attention_work(l, 0, False, True)[1]()
                with act.Fori(1, B - 1) as b:
                    attention_work(l, b, True, True)[1]()
                attention_work(l, B - 1, True, False)[1]()
                attention_work(l, B - 1, True, False)[2]()
                for e in range(NE if l == 0 else 1):
                    p = e if l == 0 else NE + l - 1
                    with act.Fori(0, B) as b:
                        mlp(l, e, p, b)

        @block.vector
        def _(dve):
            V = nc.vector
            dve.sem_inc(S["evac_done"], TT)
            dve.sem_inc(S["oT_ready"], 1)
            V.memset(silu[CW:CW + 1, :, :], 1.0).then_inc(S["silu_done"], 1)
            V.memset(vaug[:, :, :, :], 1.0)
            dve.wait_ge(S["ld_const"], 16 * 7)
            for l in range(NL):
                dve.wait_ge(S["mod_tr"], l + 1)
                tp = ps[0:CW, 0, 0:4 * KC * B].rearrange("p (s c b) -> p s c b", s=4, c=KC)
                for s in (0, 2):
                    for c in range(KC):
                        lnw = cols[0:CW, l, COL_LN + 3 * s + c:COL_LN + 3 * s + c + 1]
                        lnb = cols[0:CW, l, COL_LN + 3 * s + KC + c:COL_LN + 3 * s + KC + c + 1]
                        V.tensor_scalar(modcol[:, l, s + 1, c, :], tp[:, s + 1, c, :], 1.0, lnw, ALU.add, ALU.mult).then_inc(S["md_step"], 1)
                        V.tensor_scalar(stats[0:CW, 0, 0:B], tp[:, s + 1, c, :], 1.0, lnb, ALU.add, ALU.mult).then_inc(S["md_step"], 1)
                        k = (l * 2 + s // 2) * KC + c
                        dve.wait_ge(S["md_step"], 3 * k + 2)
                        V.tensor_tensor(modcol[:, l, s, c, :], stats[0:CW, 0, 0:B], tp[:, s, c, :], ALU.add).then_inc(S["md_step"], 1)
                        dve.wait_ge(S["md_step"], 3 * k + 3)
            dve.wait_ge(S["ld_skew"], 16)
            dve.wait_ge(S["sk_tr"], 1)
            vt = ps[0:RD, 1, 0:B * RD].rearrange("p (b j) -> p b j", b=B)
            V.tensor_tensor(skew[:, :, :], skew[:, :, :], vt, ALU.subtract).then_inc(S["sk_dve"], 1)
            dve.wait_ge(S["sk_dve"], 1)
            for h in range(2):
                V.tensor_scalar(sx[:, h, :, :], skew[:, :, :], (1 - 2 * h) * 2.0 ** -DOUBLINGS, None, ALU.mult).then_inc(S["sk_dve"], 1)
            dve.wait_ge(S["sk_dve"], 3)

            def flat(t):
                return t.rearrange("p h b j -> p (h b j)")

            V.scalar_tensor_tensor(out=flat(ey[:, 0]), in0=flat(sx[:, :, :, :]), scalar=1.0 / TAYLOR, in1=flat(eye8[:, :, :, :]),
                                   op0=ALU.mult, op1=ALU.add).then_inc(S["ex_ev"], 1)
            for i in range(TAYLOR - 1):
                k = TAYLOR - 1 - i
                dve.wait_ge(S["ex_mm"], i + 1)
                if k > 1:
                    V.scalar_tensor_tensor(out=flat(ey[:, (i + 1) % 2]), in0=ps[0:RD, 2 + i % 2, :], scalar=1.0 / k,
                                           in1=flat(eye8[:, :, :, :]), op0=ALU.mult, op1=ALU.add).then_inc(S["ex_ev"], 1)
                else:
                    V.tensor_copy(flat(ey[:, (i + 1) % 2]), ps[0:RD, 2 + i % 2, :]).then_inc(S["ex_ev"], 1)
            with dve.Fori(0, DOUBLINGS // 2) as i:
                for u in range(2):
                    dve.wait_ge(S["ex_mm"], i * 2 + (TAYLOR + u))
                    dve.wait_ge(S["ex_ev"], i * 2 + (TAYLOR + u))
                    q = (TAYLOR - 1 + u) % 2
                    V.scalar_tensor_tensor(out=flat(ey[:, 1 - q]), in0=flat(ey[:, q]), scalar=2.0, in1=ps[0:RD, 2 + q, :],
                                           op0=ALU.mult, op1=ALU.add).then_inc(S["ex_ev"], 1)
            dve.wait_ge(S["ex_ev"], TAYLOR + DOUBLINGS)
            V.tensor_copy(GE[:, :, :], ey[:, (TAYLOR - 1) % 2, 1, :, :]).then_inc(S["setup_done"], 1)

            def layernorm(which, i, b, eps, parts, xn_free=None):
                ln = S[f"ln{which}_step"]
                k = [{"a": 0, "b": TT, "c": LN_STEPS}[parts[0]]]

                def step(ins, wait=True):
                    k[0] += 1
                    ins.then_inc(ln, 1)
                    if wait:
                        wait_alone(dve, ln, i * LN_STEPS + k[0], S["dve_passed"])

                var, y, u, w = (nwt[:, n, :] for n in range(4))
                if "a" in parts:
                    for t in range(TT):
                        step(V.bn_stats(stats[:, t, :], xrow(b, t)), t == TT - 1)
                if "b" in parts:
                    for t in range(TT):
                        step(V.bn_aggr(mv[:, t, :], stats[:, t, :]), t == TT - 1)
                    step(V.tensor_scalar(var, mv[:, :, 1], eps, None, ALU.add))
                    step(V.tensor_scalar(u.bitcast(I32), var.bitcast(I32), 1, None, ALU.logical_shift_right))
                    step(V.tensor_scalar(y.bitcast(I32), u.bitcast(I32), -1.0, float(RSQRT_MAGIC), ALU.mult, ALU.add))
                    for _ in range(3):
                        step(V.tensor_tensor(u, y, y, ALU.mult))
                        step(V.scalar_tensor_tensor(out=w, in0=u, scalar=-0.5, in1=var, op0=ALU.mult, op1=ALU.mult))
                        step(V.scalar_tensor_tensor(out=y, in0=w, scalar=1.5, in1=y, op0=ALU.add, op1=ALU.mult))
                if "c" in parts:
                    assert k[0] == LN_STEPS, k
                    if xn_free:
                        dve.wait_ge(*xn_free)
                    for t in range(TT):
                        V.tensor_scalar(xn[:, t, :], xrow(b, t), mv[:, t, 0:1], y[:, t:t + 1],
                                        ALU.subtract, ALU.mult).then_inc(S[f"xn{which}_ready"], 1)

            def xrow(b, t):
                return xres[:, bass.ds(b * TT + t, 1), :].rearrange("p a n -> p (a n)")

            def gate_row(b):
                return gates[:, bass.ds(b, 1), :].rearrange("p a n -> p (a n)")

            def attention_work(l, b, prev, nxt):
                G, it = b * NG + B * NG * l, b + B * l

                def low_part(g, what):
                    dve.wait_ge(S["hi_done"], G * 2 + (2 * g + what + 1))
                    V.scalar_tensor_tensor(out=qk[:, g % 2, 2 * what + 1, :], in0=ps[0:GR, BANK[("Pq", "Pk")[what], g % NG], :],
                                           scalar=cols[0:GR, l, NG * what + g % NG:NG * what + g % NG + 1],
                                           in1=qk[:, g % 2, 2 * what, :].bitcast(F32), op0=ALU.add, op1=ALU.subtract).then_inc(S["lo_done"], 1)

                def maxima(g, qt, which):
                    for i in which:
                        dve.wait_ge(S["max_mm"], G * NU + (NU * g + qt * HG + i + 1))
                        V.tensor_reduce(mx[:, g % NG, qt, i:i + 1], bank(i % 2), AX.X, ALU.max).then_inc(S["mx_done"], 1)

                def negate(g):
                    dve.wait_ge(S["mx_done"], G * NU + NU * (g + 1))
                    V.tensor_scalar(nm[:, g % NG, :, 0:HG], mx[:, g % NG, :, :], -1.0, None, ALU.mult).then_inc(S["nh_done"], 1)
                    dve.wait_ge(S["nh_done"], G + (g + 1))
                    V.scalar_tensor_tensor(out=nm[:, g % NG, :, HG:2 * HG], in0=mx[:, g % NG, :, :], scalar=-1.0,
                                           in1=nm[:, g % NG, :, 0:HG].bitcast(F32), op0=ALU.mult, op1=ALU.subtract).then_inc(S["nm_ready"], 1)

                def v_out(t):
                    dve.wait_ge(S["v_mm"], it * TT + (t + 1))
                    dve.wait_ge(S["pv_done"], it * 16 + 16)
                    V.tensor_tensor(vaug[:, t, :, 0:HD], ps[:, BANK["V", t], 0:C].rearrange("p (h d) -> p h d", h=NH),
                                    rows_b[:, 0, :].rearrange("p (h d) -> p h d", h=NH), ALU.add).then_inc(S["v_ready"], 1)

                def reciprocals(g):
                    dve.wait_ge(S["on_mm"], G + (g + 1))
                    V.reciprocal(rsm[:, :, :].rearrange("p t h -> p (t h)"), ps[:, BANK["on", g % NG], 0:NU]).then_inc(S["rec_done"], 1)
                    dve.wait_ge(S["rec_done"], G + (g + 1))
                    V.tensor_copy(rbc[:, :, :, :], rsm[:, :, :].unsqueeze(3).to_broadcast([P, TT, HG, 32])).then_inc(S["rbc_ready"], 1)

                def normalise(g):
                    dve.wait_ge(S["ob_tr"], G + (g + 1))
                    V.tensor_tensor(oT[:, g % NG, :], ps[:, BANK["ob", g % NG], :], oc[:, :], ALU.mult).then_inc(S["oT_ready"], 1)

                def residual(t, i, bb):
                    dve.wait_ge(S["pj_mm"], i * TT + (t + 1))
                    V.tensor_tensor(tmpx[:, :], ps[:, BANK["pj", t], 0:C], rows_b[:, 1, :], ALU.add).then_inc(S["xa_t"], 1)
                    dve.wait_ge(S["xa_t"], i * TT + (t + 1))
                    V.tensor_tensor(tmpx[:, :], tmpx[:, :], gate_row(bb), ALU.mult).then_inc(S["xa_g"], 1)
                    dve.wait_ge(S["xa_g"], i * TT + (t + 1))
                    V.tensor_tensor(xrow(bb, t), xrow(bb, t), tmpx[:, :], ALU.add).then_inc(S["xa_done"], 1)
                    dve.wait_ge(S["xa_done"], i * TT + (t + 1))

                def tiles(g, kt, which):
                    if g + 2 < NG or nxt:
                        maxima(g + 2, kt, which)
                        if kt == TT - 1 and which[-1] == HG - 1:
                            negate(g + 2)

                def others(g, kt, place):
                    for kind, arg in other_work(g, kt, place, prev, nxt, l == 0):
                        if kind in ("Pq", "Pk"):
                            low_part(g + arg, int(kind == "Pk"))
                        elif kind == "on":
                            reciprocals(g + arg)
                        elif kind == "ob":
                            normalise(g + arg)
                        elif kind == "V":
                            v_out(arg)
                        elif kind[:3] == "LN1":
                            layernorm(1, it + 1, b + 1, EPS[l], kind[3], (S["tr2_done"], it * KC + KC))
                        elif kind == "pj":
                            residual(arg, it - 1, b - 1)
                        elif kind[:3] == "LN2":
                            layernorm(2, it - 1, b - 1, EPS[l], kind[3], (S["tr1_done"], it * KC + (2 * KC if nxt else KC)))
                        elif kind == "top2":
                            top2(b - 1, BANK["lt", 0])

                def start():
                    layernorm(1, it, b, EPS[l], "abc")
                    for g in range(3):
                        for what in range(2):
                            low_part(g, what)
                    for g in range(2):
                        for qt in range(TT):
                            maxima(g, qt, range(HG))
                        negate(g)

                def steps():
                    walk(tiles, others, lambda g, kt: None)

                def end():
                    reciprocals(NG - 1)
                    normalise(NG - 1)
                    for t in range(TT):
                        residual(t, it, b)
                    layernorm(2, it, b, EPS[l], "abc", (S["tr1_done"], it * KC + KC))
                    if l == 0:
                        top2(b, BANK["lt", 0])

                return start, steps, end

            def top2(b, lt_bank):
                k = [0]

                def step(ins, wait=True):
                    k[0] += 1
                    ins.then_inc(S["tk_step"], 1)
                    if wait:
                        dve.wait_ge(S["tk_step"], b * 9 + k[0])

                dve.wait_ge(S["lg_tr"], b + 1)
                lg, e1, rank, sel = (tk[:, i, :, :] for i in range(4))
                gt, eq = tkc[:, 0, :, :, :], tkc[:, 1, :, :, :]
                step(V.tensor_copy(lg, ps[:, lt_bank, 0:TT * NE].rearrange("p (t e) -> p t e", t=TT)))
                step(V.tensor_reduce(tkm[:, 0, :], lg, AX.X, ALU.max))
                V.tensor_tensor(e1, lg, tkm[:, 0, :].unsqueeze(2).to_broadcast([P, TT, NE]), ALU.subtract).then_inc(S["tk_in"], 1)
                me = lg.unsqueeze(3).to_broadcast([P, TT, NE, NE])
                other = lg.unsqueeze(2).to_broadcast([P, TT, NE, NE])
                step(V.tensor_tensor(gt, other, me, ALU.is_gt), False)
                step(V.tensor_tensor(eq, other, me, ALU.is_equal))
                step(V.tensor_tensor(eq, eq, lowmask[:, :, :, :], ALU.mult))
                step(V.tensor_tensor(gt, gt, eq, ALU.add))
                step(V.tensor_reduce(rank, gt, AX.X, ALU.add))
                dve.wait_ge(S["tk_exp"], b + 1)
                step(V.scalar_tensor_tensor(out=sel.rearrange("p t e -> p (t e)"), in0=rank.rearrange("p t e -> p (t e)"), scalar=1.5,
                                            in1=e1.rearrange("p t e -> p (t e)"), op0=ALU.is_lt, op1=ALU.mult))
                step(V.tensor_reduce(tkm[:, 1, :], sel, AX.X, ALU.add))
                V.reciprocal(tkm[:, 0, :], tkm[:, 1, :]).then_inc(S["tk_r"], 1)
                dve.wait_ge(S["tk_r"], b + 1)
                V.tensor_tensor(cw[:, bass.ds(b * TT, TT), :], sel, tkm[:, 0, :].unsqueeze(2).to_broadcast([P, TT, NE]),
                                ALU.mult).then_inc(S["cw_ready"], 1)
                assert k[0] == 9, k

            def mlp(l, e, p, b):
                it = b + B * p
                fin = (e == NE - 1) or l > 0
                fi = b + B * l
                for t in range(TT):
                    dve.wait_ge(S["fc2_mm"], it * TT + (TT + t + 1))
                    V.tensor_tensor(tmp[:, t, :], ps[:, 4 + t, 0:C], b2b[:, :], ALU.add).then_inc(S["evac_done"], 1)
                    dve.wait_ge(S["evac_done"], it * TT + (TT + t + 1))
                    src = tmp[:, t, :]
                    if l == 0:
                        row = acc[:, bass.ds(b * TT + t, 1), :].rearrange("p a n -> p (a n)")
                        wgt = cw[:, bass.ds(b * TT + t, 1), e:e + 1].rearrange("p a n -> p (a n)")
                        if e == 0:
                            V.tensor_scalar(row, src, wgt, None, ALU.mult).then_inc(S["acc_done"], 1)
                        else:
                            V.scalar_tensor_tensor(out=row, in0=src, scalar=wgt, in1=row, op0=ALU.mult, op1=ALU.add).then_inc(S["acc_done"], 1)
                        dve.wait_ge(S["acc_done"], it * TT + (t + 1))
                        src = row
                    if fin:
                        V.tensor_tensor(tmp[:, t, :], src, gate_row(b), ALU.mult).then_inc(S["gm_done"], 1)
                        dve.wait_ge(S["gm_done"], fi * TT + (t + 1))
                        V.tensor_tensor(xrow(b, t), xrow(b, t), tmp[:, t, :], ALU.add).then_inc(S["xm_done"], 1)

            dve.wait_ge(S["ld_x"], 16)
            dve.wait_ge(S["mod_stored"], 16 * NL)
            for l in range(NL):
                if l == 1:
                    dve.wait_ge(S["xm_done"], 16)
                if l == 2:
                    with dve.Fori(0, B) as b:
                        for t in range(TT):
                            dve.wait_ge(S["xm_done"], 32)
                            if t == 0:
                                dve.wait_ge(S["xt_tr"], b * KC + KC)
                            V.tensor_copy(xn[:, t, :], xrow(b, t)).then_inc(S["xc_done"], 1)
                        for t in range(TT):
                            dve.wait_ge(S["r_mm"], b * TT + (t + 1))
                            V.tensor_tensor(xrow(b, t), xrow(b, t), ps[:, 4 + t, 0:C], ALU.add).then_inc(S["xr_done"], 1)
                    dve.wait_ge(S["xr_done"], 16)
                dve.wait_ge(S["ld_gate"], 32 * l + 16)
                dve.wait_ge(S["ld_w"], 48 * (l + 1))
                attention_work(l, 0, False, True)[0]()
                attention_work(l, 0, False, True)[1]()
                with dve.Fori(1, B - 1) as b:
                    attention_work(l, b, True, True)[1]()
                attention_work(l, B - 1, True, False)[1]()
                attention_work(l, B - 1, True, False)[2]()
                dve.wait_ge(S["ld_gate"], 32 * l + 32)
                for e in range(NE if l == 0 else 1):
                    p = e if l == 0 else NE + l - 1
                    dve.wait_ge(S["ld_mlp"], 48 * (p + 1))
                    with dve.Fori(0, B) as b:
                        mlp(l, e, p, b)


def kernel(**inputs):
    import concourse.bacc as bacc
    from concourse.bass_utils import run_bass_kernel_spmd

    x = {k: np.asarray(v) for k, v in inputs.items()}
    f = np.float32

    def split_heads(w):
        o = np.zeros((NH, 32, C), f)
        o[:, :HD] = w.reshape(NH, HD, C)
        return o.reshape(NG, P, C)

    qkv_w = [x["L0_cond_w_qkv"], x["L1_cond_W_qkv"], np.concatenate([x["L3_cond_wq"], x["L3_cond_wk"], x["L3_cond_wv"]], 1)]
    qkv_b = [x["L0_cond_b_qkv"], x["L1_cond_b_qkv"], np.zeros(3 * C, f)]
    proj_w = [x["L0_cond_w_proj"], x["L1_cond_W_proj"], x["L3_cond_wo"]]
    proj_b = [x["L0_cond_b_proj"], x["L1_cond_b_proj"], x["L3_cond_wo_b"]]
    ada_w = [x["L0_cond_w_adaln"], x["L1_cond_W_ada"], x["L3_cond_ada_w"]]
    ada_b = [x["L0_cond_b_adaln"], x["L1_cond_b_ada"], x["L3_cond_ada_b"]]
    fc1_b = [x["L0_cond_b1"], x["L1_cond_b_fc1"][None], x["L3_cond_fc1_b"][None]]
    one, zero = np.ones(C, f), np.zeros(C, f)
    ln = [(one, zero, one, zero)] * 2 + [(x["L3_cond_ln1_w"], x["L3_cond_ln1_b"], x["L3_cond_ln2_w"], x["L3_cond_ln2_b"])]
    cols = np.zeros((P, NL, NCOL), f)
    for l in range(NL):
        cols[:GR, l, 0:2 * NG] = qkv_b[l][:2 * C].reshape(2 * NG, GR).T
        for i, v in enumerate(ln[l]):
            cols[:CW, l, COL_LN + KC * i:COL_LN + KC * (i + 1)] = v.reshape(KC, CW).T
        for e, v in enumerate(fc1_b[l]):
            cols[:, l, COL_FC + NJ * e:COL_FC + NJ * (e + 1)] = v.reshape(NJ, P).T
    iu, ju = np.triu_indices(RD, k=1)
    w_skew = np.zeros((C + 1, RD * RD), f)
    w_skew[:C, iu * RD + ju] = x["L2_cond_W"].T
    w_skew[C, iu * RD + ju] = x["L2_cond_b"]
    low = np.zeros((P, TT, NE, NE), f)
    low[:, :] = np.tril(np.ones((NE, NE), f), -1)
    selden = np.zeros((P, HG), f)
    selden[32 * np.arange(HG) + HD, np.arange(HG)] = 1
    eye8 = np.zeros((RD, 2, B, RD), f)
    eye8[np.arange(RD), :, :, np.arange(RD)] = 1
    arrays = {
        "x": x["x"], "condT": x["cond_1152"].T, "w_gate": x["L0_cond_w_gate"],
        "w_ada": np.stack([np.concatenate([w, b[None]], 0) for w, b in zip(ada_w, ada_b)]),
        "w_skew": w_skew, "P": x["L2_cond_P"], "cols": cols,
        "wqkv": np.stack(qkv_w), "wproj": np.stack([split_heads(w) for w in proj_w]),
        "rows_b": np.stack([np.stack([qb[2 * C:], pb]) for qb, pb in zip(qkv_b, proj_b)]),
        "w1": np.concatenate([x["L0_cond_w1"], x["L1_cond_W_fc1"][None], x["L3_cond_fc1_w"][None]]),
        "w2": np.concatenate([x["L0_cond_w2"], x["L1_cond_W_fc2"][None], x["L3_cond_fc2_w"][None]]),
        "b2": np.concatenate([x["L0_cond_b2"], x["L1_cond_b_fc2"][None], x["L3_cond_fc2_b"][None]]),
        "ident": np.eye(P, dtype=f), "lowmask": low, "ones": np.ones((2, P), f), "eye8": eye8, "selden": selden,
    }
    arrays = {k: np.ascontiguousarray(v) for k, v in arrays.items()}
    nc = bacc.Bacc("TRN2", target_bir_lowering=False, num_devices=1)
    aps = {k: nc.dram_tensor(f"in_{k}", v.shape, mybir.dt.from_np(v.dtype), kind="ExternalInput").ap() for k, v in arrays.items()}
    out = nc.dram_tensor("out", (B, N, C), F32, kind="ExternalOutput").ap()
    bass_cond_seq_kernel(nc, aps, out)
    r = run_bass_kernel_spmd(nc, [{f"in_{k}": v for k, v in arrays.items()}], core_ids=[0])
    return r.results[0]["out"]
```

```python
from contextlib import ExitStack

import numpy as np
import concourse.bass as bass
from concourse import mybir

ALU = mybir.AluOpType
ACT = mybir.ActivationFunctionType
AX = mybir.AxisListType
F32 = mybir.dt.float32
F32R = mybir.dt.float32r
I32 = mybir.dt.int32

B, N, C = 4, 512, 288
NH = 16
HD = C // NH
HID = 4 * C
NE = 4
RD = 64
P = 128
TT = N // P
KC = 3
CW = C // KC
REP = 4
CR = C - 2 * P
NJ = HID // P
NQ = 3
NJP = NJ // NQ
AHEAD = 3
HG = 4
NG = NH // HG
HT = P // HD
QT = -(-2 * NH // HT)
QR = [HD * min(HT, 2 * NH - HT * i) for i in range(QT)]
NU = TT * HG
SCALE = float(HD) ** -0.5
DOUBLINGS = 14
TAYLOR = 6
EPS = [1e-6, 1e-6, 1e-5]
NL = 3
MOD = 6 * C
COL_LN = QT
COL_FC = COL_LN + 4 * KC
NCOL = COL_FC + NE * NJ
LN_STEPS = 20
HH_START, HH_FWD, HH_BWD = 4, 27, 7
RSQRT_MAGIC = 0x5F3759DF


def other_work(g, kt, place, prev, nxt, moe):
    work = {(kt_, p): list(w) for kt_, p, w in (
        (0, "A", [("P", (4, None, 2, 3)[g])] if g != 1 else []), (1, "A", [("R", 1)]), (1, "C", [("on", -1)]), (2, "A", [("rb", -1)]), (2, "B", [("ob", -1)]))}
    own = {
        0: [(0, "B", [("LN1a", 0)]), (0, "C", [("V", 0)]), (1, "A", [("LN1b", 0)]), (1, "B", [("V", 1)]), (1, "C", [("LN1c", 0)]),
            (2, "A", [("V", 2), ("LN1d", 0)]), (2, "B", [("LN1e", 0)]), (2, "C", [("V", 3), ("LN1f", 0)]), (3, "A", [("LN1g", 0)]),
            (3, "B", [("LN1h", 0)])],
        1: [(0, "A", [("T1", 0)]), (0, "B", [("T1", 1)]), (0, "C", [("T1", 2)]), (1, "A", [("P", 0)]), (1, "B", [("P", 1), ("pj", 0)]),
            (1, "C", [("pj", 1)]), (2, "A", [("pj", 2), ("pj", 3)]), (2, "C", [("LN2a", 0)]), (3, "A", [("LN2b", 0)]), (3, "B", [("LN2c", 0)]),
            (3, "C", [("LN2d", 0)])],
        2: [(0, "A", [("LN2e", 0)]), (0, "B", [("LN2f", 0)]), (0, "C", [("LN2g", 0)]), (1, "A", [("LN2h", 0)]), (1, "C", [("T2", 0)]),
            (2, "A", [("T2", 1)]), (2, "C", [("T2", 2)]), (3, "B", [("lg", 0)])],
        3: [(1, "B", [("lt", 0)]), (2, "A", [("top2", 0)])],
    }[g]
    for kt_, p, w in own:
        work.setdefault((kt_, p), []).extend(w)
    out = []
    for kind, arg in work.get((kt, place), []):
        if kind == "P" and g and not nxt:
            continue
        if kind == "R" and g + arg >= NG and not nxt:
            continue
        if kind in ("on", "rb", "ob") and g == 0 and not prev:
            continue
        if kind[:3] in ("T1", "LN1") and not nxt:
            continue
        if kind[:3] in ("pj", "T2", "LN2", "lg", "lt", "top") and not prev:
            continue
        if kind in ("lg", "lt", "top2") and not moe:
            continue
        out.append((kind, arg))
    return out


def walk(tile, others, pv):
    for g in range(NG):
        for kt in range(TT):
            tile(g, kt, (0, 1))
            others(g, kt, "A")
            tile(g, kt, (2, 3))
            others(g, kt, "B")
            pv(g, kt)
            others(g, kt, "C")


def banks_of_other_work():
    table = {}
    n = 0
    for g in range(NG):
        for kt in range(TT):
            for place in "ABC":
                for kind, arg in other_work(g, kt, place, True, True, True):
                    if kind[:2] in ("LN", "to", "rb"):
                        continue
                    table[kind, (g + arg) % NG if kind in ("R", "on", "ob") else arg] = 6 + n % 2
                    n += 1
    return table


BANK = banks_of_other_work()
MAX_BANKS = (0, 1, 5)


def weights_at(j, first, last):
    return [k for k, at, when in ((0, 6, last), (1, 0, first), (2, 4, first)) if when and j == at]


def wait_alone(eng, sem, value, passed):
    eng.wait_ge(sem, value)
    eng.sem_inc(passed, 1)


def bass_cond_seq_kernel(nc, a, out):
    modd = nc.dram_tensor("mod_rows", [NL, B, MOD], F32).ap()
    qkd = nc.dram_tensor("qk_rows", [2 * NH, 2, HD, N], F32).ap()
    vd = nc.dram_tensor("skew_rows", [B, RD * RD], F32).ap()

    with ExitStack() as ctx:
        base = [nc.sbuf_base + 31 & ~31]

        def put(name, shape, dt, at):
            size = 4 * int(np.prod(shape[1:]))
            assert at + size <= nc.sbuf_usable_end, (name, at + size)
            return nc.alloc_sbuf_tensor_at(name, shape, dt, offset=at), at + (size + 31 & ~31)

        def keep(name, shape, dt=F32):
            t, base[0] = put(name, shape, dt, base[0])
            return t

        xres = keep("xres", [P, B * TT, C])
        gates = keep("gates", [P, B, C])
        h2T = keep("h2T", [P, KC, B * N])
        wqh = keep("wqh", [P, 2, 3 * C], F32R)
        wqraw, _ = put("wqraw", [P, KC, 3 * C], F32, base[0])
        wql = keep("wql", [P, KC, 3 * C], F32R)
        wproj = keep("wproj", [P, NG, C])
        vbias = keep("vbias", [P, C])
        tmpx = keep("tmpx", [P, C])
        cols = keep("cols", [P, NL, NCOL])
        modcol = keep("modcol", [P, NL, 4, KC, B])
        ident = keep("ident", [P, P])
        lowmask = keep("lowmask", [P, TT, NE, NE])
        onesr = keep("onesr", [2, CR], F32R)
        wgate = keep("wgate", [P, KC, NE])
        masks = keep("masks", [P, 2])
        silu = keep("silu", [CW + 1, KC, B])
        lgT, _ = put("lgT", [NE, N], F32, base[0])
        xn = keep("xn", [P, TT, KC * P])
        hTh = keep("hTh", [P, KC, N], F32R)
        wqt, _ = put("wqt", [P, 3 * C], F32R, base[0])
        hTraw, _ = put("hTraw", [P, KC, N], F32, base[0])
        hTl = keep("hTl", [P, KC, N], F32R)
        stats = keep("stats", [P, TT, 6])
        mv = keep("mv", [P, TT, 2])
        nwt = keep("nwt", [P, 4, TT])
        qk = keep("qk", [P, 2, 2, N], F32R)
        vaug = keep("vaug", [P, TT, NH, 32])
        mx = keep("mx", [P, NG, TT, HG])
        nm = keep("nm", [P, NG, TT, 2 * HG], F32R)
        oc = keep("oc", [P, N])
        rsm = keep("rsm", [P, TT, HG])
        rbc = keep("rbc", [P, TT, HG, 32])
        selden = keep("selden", [P, HG])
        nmT = keep("nmT", [2 * HG, N], F32R)
        cw = keep("cw", [P, B * TT, NE])
        tk = keep("tk", [P, 4, TT, NE])
        tkm = keep("tkm", [P, 2, TT])
        tkc = keep("tkc", [P, 2, TT, NE, NE])
        U = keep("U", [CW, KC, RD])
        GE = keep("GE", [RD, B, RD])
        hA = keep("hA", [CW, KC, RD])
        hV = keep("hV", [CW, KC, RD])
        hp = keep("hp", [CW, KC, RD])
        hr = keep("hr", [CW, 2 * RD])
        hR = keep("hR", [CW, 2 * RD])
        hC = keep("hC", [CW, RD])
        hs = keep("hs", [CW, 16])
        region = base[0]
        qs, at = put("qs", [P, NH, N], F32R, region)
        ks, at = put("ks", [P, NH, N], F32R, at)
        oT, at = put("oT", [P, NG, N], F32, at)
        pT, at = put("pT", [P, 2 * HG, N], F32, at)
        shared = at
        w1h, at = put("w1h", [P, 2, HID], F32R, region)
        w1l, at2 = put("w1l", [P, KC, HID], F32R, at)
        w1raw, at = put("w1raw", [P, KC, HID], F32, at)
        w1t, at = put("w1t", [P, NJP * P], F32R, at)
        hh, at = put("hh", [P, KC, N], F32R, at)
        assert region + 3 * HG * N * 4 <= at <= region + NH * N * 4
        w2h, at = put("w2h", [P, NJ, C], F32R, region + NH * N * 4)
        w2l, at2 = put("w2l", [P, NJ, C], F32R, at)
        w2raw, at = put("w2raw", [P, NJ, C], F32, at)
        assert at <= region + (NH + 3 * HG) * N * 4
        hl, at = put("hl", [P, KC, N], F32R, at)
        gf, at = put("gf", [P, 3, N], F32, at)
        gh, at = put("gh", [P, 3, N], F32R, at)
        gl, at = put("gl", [P, 3, N], F32R, at)
        b2b, at = put("b2b", [P, 2, C], F32, at)
        hU, _ = put("hU", [RD, C], F32, at)
        tmp, at = put("tmp", [P, TT, C], F32, at)
        assert at <= shared
        EUt, at = put("EUt", [RD, B, C], F32, at)
        zT, zat = put("zT", [RD, N], F32, region)
        xT, _ = put("xT", [CW, KC, N], F32, zat)
        assert at <= shared
        ada, at = put("ada", [CW + 1, 2, KC, MOD], F32, region)
        wf, at = put("wf", [CW + 1, 2, KC, 1024], F32, at)
        assert at >= region + 2 * NH * N * 4
        vsb, at = put("vsb", [B, 2, 512], F32, at)
        modsb, at = put("modsb", [B, MOD], F32, at)
        modx, at = put("modx", [B, 6, P], F32, at)
        skew, at = put("skew", [RD, B, RD], F32, at)
        sx, at = put("sx", [RD, 2, B, RD], F32, at)
        ey, at = put("ey", [RD, 2, 2, B, RD], F32, at)
        eye8, at = put("eye8", [RD, 2, B, RD], F32, at)
        assert at <= nc.sbuf_usable_end

        ps = ctx.enter_context(nc.psum_tensor("ps", [P, 8, N], F32))

        def bank(i):
            return ps[:, i, :]

        names = """ld_const ld_x ld_cond ld_wf0 ld_wf1 ld_ada0 ld_ada1 ld_skew ld_gate ld_w ld_p silu_done
            skew_mm skew_out skew_stored0 skew_stored1 sk_tr sk_dve ex_mm ex_ev mod_mm mod_cp mod_rep mod_stored mod_tr md_step
            ln1_step ln2_step xn1_ready xn2_ready xc1_ready xc2_ready tr1_done tr2_done h1_ready h2_ready
            h1r_done h1h_done wq_hi wq_ready qk_mm hi_done lo_done qk_st stack_ld0 stack_ld1 stack_ld2 stack_ld3 ones_ld
            v_mm v_ready max_mm mx_done nh_done nm_ready nm_tr nmT_ready nm_ld0 nm_ld1 st_mm exp_done pv_done
            oc_done on_mm rec_done rbc_ready ob_tr oT_ready pj_mm xa_g xa_done
            lg_mm lg_cp lg_tr tk_step tk_in tk_exp tk_r cw_ready
            ld_wp0 ld_wp1 ld_wp2 ld_b2 hi_w w1_ready w2_ready hh_done hs_done
            fc1_mm gf_done gh_done gl_done fc2_mm evac_done gm_done xm_done
            hh_step u_tr u_cp eu_mm eu_cp xc_done xt_tr xt_cp z_mm z_cp r_mm xr_done
            out_done setup_done sp_passed pool_passed dve_passed pe_passed""".split()
        S = {n: ctx.enter_context(nc.semaphore(n)) for n in names}
        block = ctx.enter_context(nc.Block())

        @block.sync
        def _(sp):
            for dst, src in ((ident[:, :], a["ident"]), (cols[:, :, :], a["cols"]),
                             (lowmask[:, :, :, :], a["lowmask"]),
                             (wgate[:, :, :], a["w_gate"].rearrange("c p e -> p c e")), (masks[:, :], a["masks"]),
                             (onesr[:, :].bitcast(F32), a["ones"]), (selden[:, :], a["selden"]), (eye8[:, :, :, :], a["eye8"])):
                sp.dma_start(dst, src).then_inc(S["ld_const"], 16)
            sp.dma_start(silu[0:CW, :, :], a["condT"].rearrange("(c p) b -> p c b", p=CW)).then_inc(S["ld_cond"], 16)

            def load_wf(k):
                src = a["w_skew"][:, k * 1024:(k + 1) * 1024]
                sp.dma_start(wf[0:CW, k % 2, 0:2, :], src[0:2 * CW].rearrange("(c p) n -> p c n", p=CW)).then_inc(S[f"ld_wf{k % 2}"], 16)
                sp.dma_start(wf[:, k % 2, 2, :], src[2 * CW:C + 1]).then_inc(S[f"ld_wf{k % 2}"], 16)

            def load_ada(l):
                src = a["w_ada"][l]
                sp.dma_start(ada[0:CW, l % 2, 0:2, :], src[0:2 * CW].rearrange("(c p) n -> p c n", p=CW)).then_inc(S[f"ld_ada{l % 2}"], 16)
                sp.dma_start(ada[:, l % 2, 2, :], src[2 * CW:C + 1]).then_inc(S[f"ld_ada{l % 2}"], 16)

            def load_attention_weights(l):
                sp.dma_start(wqraw[:, :, :], a["wqkv"][l].rearrange("c p n -> p c n")).then_inc(S["ld_w"], 16)
                sp.dma_start(wproj[:, :, :], a["wproj"][l].rearrange("g p n -> p g n")).then_inc(S["ld_w"], 16)
                sp.dma_start(vbias[:, :], a["vbias"][l].partition_broadcast(P)).then_inc(S["ld_w"], 16)

            load_wf(0)
            load_wf(1)
            load_ada(0)
            load_ada(1)
            for k in (2, 3):
                sp.wait_ge(S["skew_mm"], 2 * (k - 1))
                load_wf(k)
            load_attention_weights(0)
            sp.wait_ge(S["mod_mm"], 4)
            load_ada(2)
            for u in range(2):
                sp.wait_ge(S[f"skew_stored{u}"], 4 * 16)
            sp.dma_start(skew[:, :, :], vd.rearrange("b (i j) -> i b j", i=RD)).then_inc(S["ld_skew"], 16)

            for l in range(NL):
                if l == 2:
                    sp.wait_ge(S["xr_done"], TT * B)
                sp.wait_ge(S["mod_stored"], 16 * NL)
                if l == 0:
                    sp.wait_ge(S["mod_mm"], 4 * NL)
                else:
                    sp.wait_ge(S["fc2_mm"], NJ * B * (NE + l - 1) + 3)
                if l:
                    sp.wait_ge(S["xm_done"], TT * B * (NE + l - 1))
                sp.dma_start(gates[:, :, :], modd[l, :, 2 * C:3 * C].partition_broadcast(P)).then_inc(S["ld_gate"], 16)
                sp.dma_start(ks[4 * HD:4 * HD + 2, :, :].rearrange("r h (t n) -> r (h t) n", n=CR).bitcast(F32),
                             onesr[:, :].bitcast(F32).unsqueeze(1).to_broadcast([2, NH * N // CR, CR])).then_inc(S["ones_ld"], 16)

                def store_tile(i, tile):
                    o = HT * tile
                    if not (isinstance(i, int) and i == 0):
                        for g in range(o // (2 * HG), (o + QR[tile] // HD - 1) // (2 * HG) + 1):
                            wait_alone(sp, S[f"stack_ld{g}"], i * 80, S["sp_passed"])
                    for part, done in enumerate(("hi_done", "lo_done")):
                        wait_alone(sp, S[done], i * QT + (tile + 1), S["sp_passed"])
                        sp.dma_start(qkd[o:o + QR[tile] // HD, part], qk[0:QR[tile], tile % 2, part, :].bitcast(F32)).then_inc(S["qk_st"], 16)
                    wait_alone(sp, S["qk_st"], i * 32 * QT + 32 * (tile + 1), S["sp_passed"])

                def stack(i, g):
                    if g == 0:
                        store_tile(i, 0)
                    store_tile(i, g + 1)
                    wait_alone(sp, S["pv_done"], i * NU + (TT * g + TT), S["sp_passed"])
                    heads, o = slice(HG * g, HG * g + HG), 2 * HG * g
                    for to, row, src in ((qs, 0, qkd[o:o + HG]), (qs, 2, qkd[o:o + HG]), (ks, 0, qkd[o + HG:o + 2 * HG]),
                                         (ks, 2, qkd[o + HG:o + 2 * HG, 1:2]), (ks, 3, qkd[o + HG:o + 2 * HG, 0:1])):
                        src = src.rearrange("h a d n -> (a d) h n")
                        sp.dma_start(to[HD * row:HD * row + src.shape[0], heads, :].bitcast(F32), src).then_inc(S[f"stack_ld{g}"], 16)

                def maxima(G, g):
                    sp.wait_ge(S["nmT_ready"], G + 1)
                    for row in range(2):
                        sp.dma_start(qs[4 * HD + row:4 * HD + row + 1, HG * g:HG * g + HG, :].bitcast(F32),
                                     nmT[HG * row:HG * row + HG, :].bitcast(F32)).then_inc(S[f"nm_ld{g % 2}"], 16)

                G0 = NG * B * l
                for g in range(3):
                    stack(B * l, g)
                maxima(G0, 0)
                with sp.Fori(0, B - 1) as b:
                    for g in range(NG):
                        if g == 1:
                            maxima(b * NG + (G0 + g + 1), g + 1)
                        stack(b + (B * l + (g > 0)), (g + 3) % NG)
                        if g != 1:
                            maxima(b * NG + (G0 + g + 1), (g + 1) % NG)
                for g in range(NG - 1):
                    if g == 0:
                        stack(B * l + B - 1, NG - 1)
                    maxima(G0 + NG * (B - 1) + g + 1, g + 1)
                def load_piece(p, k):
                    sp.dma_start(w1raw[:, :, NJP * P * k:NJP * P * (k + 1)],
                                 a["w1"][p][:, :, NJP * P * k:NJP * P * (k + 1)].rearrange("c p n -> p c n")).then_inc(S[f"ld_wp{k}"], 16)
                    sp.dma_start(w2raw[:, NJP * k:NJP * (k + 1), :],
                                 a["w2"][p][NJP * P * k:NJP * P * (k + 1)].rearrange("(j p) n -> p j n", p=P)).then_inc(S[f"ld_wp{k}"], 16)

                def load_bias(p):
                    sp.dma_start(b2b[:, p % 2, :], a["b2"][p].partition_broadcast(P)).then_inc(S["ld_b2"], 16)

                p = 0 if l == 0 else NE + l - 1
                sp.wait_ge(S["st_mm"], NU * (NG * B * (l + 1) - 1))
                for k in range(NQ):
                    load_piece(p, k)
                sp.wait_ge(S["h2_ready"], KC * B * (l + 1))
                sp.wait_ge(S["xa_done"], TT * B * (l + 1))
                sp.dma_start(gates[:, :, :], modd[l, :, 5 * C:6 * C].partition_broadcast(P)).then_inc(S["ld_gate"], 16)
                load_bias(p)
                if l + 1 < NL:
                    load_attention_weights(l + 1)
                for p in range(1, NE if l == 0 else 0):
                    for k in range(NQ):
                        sp.wait_ge(S["fc1_mm"], NJ * (B * p - 1) + NJP * (k + 1))
                        sp.wait_ge(S["fc2_mm"], NJ * (B * p - 1) + NJP * (k + 1) + 3)
                        load_piece(p, k)
                        if k == 0:
                            sp.wait_ge(S["evac_done"], TT * B * (p - 1) + TT)
                            load_bias(p)
            with sp.Fori(0, B) as b:
                sp.wait_ge(S["xm_done"], b * TT + (TT * B * (NE + 1) + TT))
                sp.dma_start(out.rearrange("b (t p) c -> p (b t) c", p=P)[:, bass.ds(b * TT, TT), :],
                             xres[:, bass.ds(b * TT, TT), :]).then_inc(S["out_done"], 16)
            sp.wait_ge(S["out_done"], 16 * B)

        @block.gpsimd
        def _(pool):
            g = nc.gpsimd
            RED = bass.bass_isa.ReduceOp.add
            pool.dma_start(hA[:, :, :], a["P"].rearrange("(c p) d -> p c d", p=CW)).then_inc(S["ld_p"], 16)
            pool.wait_ge(S["ld_const"], 16 * 8)
            g.memset(hs[:, :], 0.5).then_inc(S["hh_step"], 1)
            g.memset(U[:, :, :], 0.0).then_inc(S["hh_step"], 1)
            pool.wait_ge(S["hh_step"], 2)
            g.tensor_copy(U[0:RD, 0, :], ident[0:RD, 0:RD]).then_inc(S["hh_step"], 1)
            g.memset(hs[:, 1:2], -1.0).then_inc(S["hh_step"], 1)
            pool.wait_ge(S["hh_step"], HH_START)
            pool.wait_ge(S["ld_p"], 16)
            half, neg, sig, nrm, al, sg, sn, den, c, idj, keepj = (hs[:, i:i + 1] for i in range(11))
            wide = [CW, KC, RD]

            with pool.Fori(0, RD) as j:
                n = [0]

                def step(ins):
                    n[0] += 1
                    ins.then_inc(S["hh_step"], 1)
                    wait_alone(pool, S["hh_step"], j * HH_FWD + (HH_START + n[0]), S["pool_passed"])

                vj = hV[:, :, bass.ds(j, 1)]
                step(g.tensor_copy(vj, hA[:, :, bass.ds(j, 1)]))
                step(g.tensor_copy(idj, ident[0:CW, bass.ds(j, 1)]))
                step(g.tensor_tensor(hp[:, :, :], hA[:, :, :], vj.to_broadcast(wide), ALU.mult))
                step(g.tensor_tensor(hp[:, 0, :], hp[:, 0, :], hp[:, 1, :], ALU.add))
                step(g.tensor_tensor(hr[:, 0:RD], hp[:, 0, :], hp[:, 2, :], ALU.add))
                step(g.tensor_scalar(hr[:, RD:2 * RD], hA[:, 0, :], idj, 1.0, ALU.mult, ALU.mult))
                step(g.partition_all_reduce(hR[:, :], hr[:, :], CW, RED))
                step(g.tensor_copy(sig, hR[:, bass.ds(j, 1)]))
                step(g.tensor_copy(al, hR[:, bass.ds(j + RD, 1)]))
                step(g.tensor_tensor(nrm, sig, half, ALU.pow))
                step(g.tensor_scalar(sg, al, 0.0, 2.0, ALU.is_ge, ALU.mult))
                step(g.tensor_scalar(sg, sg, 1.0, -1.0, ALU.mult, ALU.add))
                step(g.tensor_tensor(sn, nrm, sg, ALU.mult))
                step(g.tensor_tensor(den, al, sn, ALU.mult))
                step(g.tensor_tensor(den, den, sig, ALU.add))
                step(g.tensor_scalar(den, den, 1e-37, 1e38, ALU.max, ALU.min))
                step(g.tensor_tensor(c, den, neg, ALU.pow))
                step(g.tensor_copy(hC[:, bass.ds(j, 1)], c))
                step(g.tensor_tensor(sig, idj, sn, ALU.mult))
                step(g.tensor_tensor(hV[:, 0, bass.ds(j, 1)], hV[:, 0, bass.ds(j, 1)], sig, ALU.add))
                step(g.tensor_scalar(hr[:, 0:RD], hR[:, RD:2 * RD], sn, 1.0, ALU.mult, ALU.mult))
                step(g.tensor_tensor(hr[:, 0:RD], hr[:, 0:RD], hR[:, 0:RD], ALU.add))
                step(g.tensor_scalar(hr[:, 0:RD], hr[:, 0:RD], c, 1.0, ALU.mult, ALU.mult))
                step(g.tensor_tensor(hp[:, :, :], hr[:, 0:RD].unsqueeze(1).to_broadcast(wide), vj.to_broadcast(wide), ALU.mult))
                step(g.tensor_tensor(hA[:, :, :], hA[:, :, :], hp[:, :, :], ALU.subtract))
                step(g.tensor_scalar(keepj, idj, -1.0, 1.0, ALU.mult, ALU.add))
                step(g.tensor_scalar(hA[:, 0, :], hA[:, 0, :], keepj, 1.0, ALU.mult, ALU.mult))
                assert n[0] == HH_FWD, n
            with pool.Fori(0, RD) as i:
                j = (RD - 1) - i
                n = [0]

                def step(ins):
                    n[0] += 1
                    ins.then_inc(S["hh_step"], 1)
                    wait_alone(pool, S["hh_step"], i * HH_BWD + (HH_START + RD * HH_FWD + n[0]), S["pool_passed"])

                vj = hV[:, :, bass.ds(j, 1)]
                step(g.tensor_tensor(hp[:, :, :], U[:, :, :], vj.to_broadcast(wide), ALU.mult))
                step(g.tensor_tensor(hp[:, 0, :], hp[:, 0, :], hp[:, 1, :], ALU.add))
                step(g.tensor_tensor(hr[:, 0:RD], hp[:, 0, :], hp[:, 2, :], ALU.add))
                step(g.partition_all_reduce(hR[:, 0:RD], hr[:, 0:RD], CW, RED))
                step(g.tensor_tensor(hr[:, 0:RD], hR[:, 0:RD], hC[:, bass.ds(j, 1)].to_broadcast([CW, RD]), ALU.mult))
                step(g.tensor_tensor(hp[:, :, :], hr[:, 0:RD].unsqueeze(1).to_broadcast(wide), vj.to_broadcast(wide), ALU.mult))
                step(g.tensor_tensor(U[:, :, :], U[:, :, :], hp[:, :, :], ALU.subtract))
                assert n[0] == HH_BWD, n

        @block.tensor
        def _(pe):
            mm, tr = nc.tensor.matmul, nc.tensor.transpose
            pe.sem_inc(S["tr2_done"], 2 * KC)
            pe.sem_inc(S["pv_done"], 16)
            pe.sem_inc(S["fc2_mm"], 3)
            pe.wait_ge(S["silu_done"], 2)

            for n in range(8):
                if n % 2 == 0:
                    pe.wait_ge(S[f"ld_wf{n // 2 % 2}"], 32 * (n // 4 + 1))
                if n >= 4:
                    pe.wait_ge(S["skew_out"], n - 3)
                for c in range(KC):
                    k = CW + (c == KC - 1)
                    ins = mm(ps[0:B, n % 4, :], silu[0:k, c, :], wf[0:k, (n // 2) % 2, c, (n % 2) * 512:(n % 2) * 512 + 512],
                             start=(c == 0), stop=(c == KC - 1))
                ins.then_inc(S["skew_mm"], 1)
            pe.wait_ge(S["ld_const"], 16 * 8)
            MC = MOD // 4
            for l in range(NL):
                pe.wait_ge(S[f"ld_ada{l % 2}"], 32 * (l // 2 + 1))
                if l:
                    pe.wait_ge(S["mod_cp"], 4 * l)
                for n in range(4):
                    for c in range(KC):
                        k = CW + (c == KC - 1)
                        ins = mm(ps[0:B, 4 + n, 0:MC], silu[0:k, c, :], ada[0:k, l % 2, c, n * MC:(n + 1) * MC],
                                 start=(c == 0), stop=(c == KC - 1))
                    ins.then_inc(S["mod_mm"], 1)
                if l:
                    pe.wait_ge(S["md_step"], 18 * l)
                else:
                    pe.wait_ge(S["skew_out"], 8)
                pe.wait_ge(S["mod_rep"], l + 1)
                for s, sec in enumerate((0, 1, 3, 4)):
                    for c in range(KC):
                        q = (s * KC + c) * B
                        ins = tr(ps[:, 0, q:q + B], modsb[:, sec * C + c * P:sec * C + c * P + P] if c < 2 else modx[:, sec, :],
                                 ident[0:B, 0:B])
                ins.then_inc(S["mod_tr"], 1)
            pe.wait_ge(S["ld_skew"], 16)
            for b in range(B):
                ins = tr(ps[0:RD, 1, b * RD:(b + 1) * RD], skew[:, b, :], ident[0:RD, 0:RD])
            ins.then_inc(S["sk_tr"], 1)

            def pair_products(to, left, right):
                for h in range(2):
                    for b in range(B):
                        q = (h * B + b) * RD
                        ins = mm(ps[0:RD, to, q:q + RD], left[:, 1 - h, b, :], right[:, h, b, :], start=True, stop=True)
                ins.then_inc(S["ex_mm"], 1)

            for i in range(TAYLOR - 1):
                pe.wait_ge(S["ex_ev"], i + 1)
                pair_products(2 + i % 2, sx, ey[:, i % 2])

            def double(n):
                pe.wait_ge(S["ex_ev"], TAYLOR + n)
                e = (TAYLOR - 1 + n) % 2
                pair_products(2 + e, ey[:, e], ey[:, e])

            def products(c, wh, wl, h_high, h_low):
                return ((wh, h_high), (wh, h_low), (wl, h_high)) if c < 2 else ((wl, h_low),)

            def attention_work(l, b, prev, nxt):
                G, it = b * NG + B * NG * l, b + B * l
                reads = {}

                def bank_free(kind, key, sem, value):
                    n = BANK[kind, key]
                    if n in reads:
                        pe.wait_ge(S[reads[n][0]], reads[n][1])
                    reads[n] = (sem, value)
                    return n

                def qk_tile(i, tile):
                    n = bank_free("P", tile, "lo_done", i * QT + (tile + 1))
                    rows, o = QR[tile], HT * HD * tile
                    for c in range(KC):
                        if tile == 0:
                            pe.wait_ge(S["h1_ready"], i * KC + (c + 1))
                        for k, (w, h) in enumerate(products(c, wqh, wql, hTh, hTl)):
                            ins = mm(ps[0:rows, n, :], w[:, c, o:o + rows], h[:, c, :], start=(c == 0 and k == 0), stop=(c == KC - 1))
                    ins.then_inc(S["qk_mm"], 1)

                def v_tile(t):
                    n = bank_free("V", t, "v_ready", it * TT + (t + 1))
                    for c in range(KC):
                        for k, (w, h) in enumerate(products(c, wqh, wql, hTh, hTl)):
                            ins = mm(ps[:, n, 0:C], h[:, c, t * P:(t + 1) * P], w[:, c, 2 * C:3 * C], start=(c == 0 and k == 0), stop=(c == KC - 1))
                    ins.then_inc(S["v_mm"], 1)

                def turn_maxima(g):
                    n = bank_free("R", g % NG, "nmT_ready", G + (g + 1))
                    pe.wait_ge(S["nm_ready"], G + (g + 1))
                    for qt in range(TT):
                        ins = tr(ps[0:2 * HG, n, qt * P:(qt + 1) * P], nm[:, g % NG, qt, :].bitcast(F32), ident[:, :])
                    ins.then_inc(S["nm_tr"], 1)

                def row_sums(g):
                    n = bank_free("on", g % NG, "rec_done", G + (g + 1))
                    pe.wait_ge(S["oc_done"], G + (g + 2))
                    for qt in range(TT):
                        ins = mm(ps[:, n, qt * HG:(qt + 1) * HG], oc[:, qt * P:(qt + 1) * P], selden[:, :], start=True, stop=True)
                    ins.then_inc(S["on_mm"], 1)

                def turn_reciprocals(g):
                    n = bank_free("ob", g % NG, "oT_ready", G + (g + 2))
                    pe.wait_ge(S["rbc_ready"], G + (g + 1))
                    for qt in range(TT):
                        ins = tr(ps[:, n, qt * P:(qt + 1) * P], rbc[:, qt, :, :].rearrange("p h r -> p (h r)"), ident[:, :])
                    ins.then_inc(S["ob_tr"], 1)

                def turn_layernorm(which, c, i):
                    ready, done, read = (("xn1_ready", "tr1_done", "h1r_done"), ("xn2_ready", "tr2_done", "h2_ready"))[which - 1]
                    n = bank_free(f"T{which}", c, read, i * KC + (c + 1))
                    if c == 0:
                        pe.wait_ge(S[ready], i * TT + TT)
                    if c == KC - 1:
                        pe.wait_ge(S[f"xc{which}_ready"], i + 1)
                    for t in range(TT):
                        ins = tr(ps[:, n, t * P:(t + 1) * P], xn[:, t, c * P:(c + 1) * P], ident[:, :])
                    ins.then_inc(S[done], 1)

                def projection(t, i):
                    n = bank_free("pj", t, "xa_g", i * TT + (t + 1))
                    if t == 0:
                        pe.wait_ge(S["oT_ready"], i * NG + (NG + 1))
                    for g in range(NG):
                        ins = mm(ps[:, n, 0:C], oT[:, g, t * P:(t + 1) * P], wproj[:, g, :], start=(g == 0), stop=(g == NG - 1))
                    ins.then_inc(S["pj_mm"], 1)

                def gate_logits(i, bb):
                    n = bank_free("lg", 0, "lg_cp", i + 1)
                    pe.wait_ge(S["h2_ready"], i * KC + KC)
                    for c in range(KC):
                        ins = mm(ps[0:NE, n, :], wgate[:, c, :], h2T[:, c, bass.ds(bb * N, N)], start=(c == 0), stop=(c == KC - 1))
                    ins.then_inc(S["lg_mm"], 1)

                def turn_logits(i):
                    n = bank_free("lt", 0, "tk_in", i + 1)
                    wait_alone(pe, S["lg_cp"], i + 1, S["pe_passed"])
                    for t in range(TT):
                        ins = tr(ps[:, n, t * NE:(t + 1) * NE], lgT[:, t * P:(t + 1) * P], ident[0:NE, 0:NE])
                    ins.then_inc(S["lg_tr"], 1)

                def max_tiles(g, qt, which, first):
                    if qt == 0 and which[0] == 0:
                        pe.wait_ge(S[f"stack_ld{g % NG}"], G * 20 + (80 * (g // NG) + 80))
                    for i in which:
                        u = NU * g + qt * HG + i
                        v = u - first
                        if u >= 3 or not isinstance(G, int) or G > 0:
                            pe.wait_ge(S["mx_done"], G * NU + (u - min(v, 2)))
                        h = (g % NG) * HG + i
                        ins = mm(bank(MAX_BANKS[v % 3]), qs[0:4 * HD, h, qt * P:(qt + 1) * P], ks[0:4 * HD, h, :], start=True, stop=True)
                        ins.then_inc(S["max_mm"], 1)

                def score_tiles(g, kt, which):
                    if kt == 0 and which[0] == 0:
                        pe.wait_ge(S[f"nm_ld{g % 2}"], G * 16 + (32 * (g // 2) + 32))
                        pe.wait_ge(S["ones_ld"], 16 * (l + 1))
                    for i in which:
                        h = g * HG + i
                        pe.wait_ge(S["exp_done"], G * NU + (NU * g + kt * HG + i + 1))
                        ins = mm(bank(2 + i % 2), ks[0:4 * HD + 2, h, kt * P:(kt + 1) * P], qs[0:4 * HD + 2, h, :], start=True, stop=True)
                        ins.then_inc(S["st_mm"], 1)

                def value_products(g, kt):
                    pe.wait_ge(S["exp_done"], G * NU + (NU * g + kt * HG + HG + 2))
                    if kt == 0:
                        pe.wait_ge(S["oc_done"], G + (g + 1))
                    if g == 0:
                        pe.wait_ge(S["v_ready"], it * TT + (kt + 1))
                    for i in range(HG):
                        ins = mm(ps[32 * i:32 * i + 32, 4, :], vaug[:, kt, g % NG * HG + i, :], pT[:, kt % 2 * HG + i, :],
                                 start=(kt == 0), stop=(kt == TT - 1), tile_position=(0, 32 * i))
                    ins.then_inc(S["pv_done"], 1)

                def tiles(g, kt, which):
                    for i in which:
                        score_tiles(g, kt, (i,))
                        if g + 2 < NG or nxt:
                            max_tiles(g + 2, kt, (i,), 2 * NU)

                def others(g, kt, place):
                    for kind, arg in other_work(g, kt, place, prev, nxt, l == 0):
                        if kind == "P":
                            qk_tile(it + (g > 0), arg)
                        elif kind == "R":
                            turn_maxima(g + arg)
                        elif kind == "on":
                            row_sums(g + arg)
                        elif kind == "ob":
                            turn_reciprocals(g + arg)
                        elif kind == "V":
                            v_tile(arg)
                        elif kind == "T1":
                            turn_layernorm(1, arg, it + 1)
                        elif kind == "pj":
                            projection(arg, it - 1)
                        elif kind == "T2":
                            turn_layernorm(2, arg, it - 1)
                        elif kind == "lg":
                            gate_logits(it - 1, b - 1)
                        elif kind == "lt":
                            turn_logits(it - 1)

                def pv(g, kt):
                    if kt:
                        value_products(g, kt - 1)
                    elif g or prev:
                        value_products(g - 1, TT - 1)

                def all_read():
                    for sem, value in reads.values():
                        pe.wait_ge(S[sem], value)

                def start():
                    if l == 1:
                        pe.wait_ge(S["evac_done"], TT * B * NE + TT)
                    if l == 2:
                        pe.wait_ge(S["xr_done"], TT * B)
                    for c in range(KC):
                        turn_layernorm(1, c, it)
                        if l == 0:
                            double(c)
                    pe.wait_ge(S["wq_ready"], l + 1)
                    for tile in range(QT - 1):
                        qk_tile(it, tile)
                        if l == 0:
                            double(KC + tile)
                    for g in range(2):
                        for qt in range(TT):
                            max_tiles(g, qt, range(HG), 0)
                            if l == 0 and TT * g + qt < DOUBLINGS - KC - QT + 1:
                                double(KC + QT - 1 + TT * g + qt)
                    turn_maxima(0)
                    all_read()

                def steps():
                    walk(tiles, others, pv)
                    all_read()

                def end():
                    value_products(NG - 1, TT - 1)
                    row_sums(NG - 1)
                    turn_reciprocals(NG - 1)
                    for t in range(TT):
                        projection(t, it)
                    p = 0 if l == 0 else NE + l - 1
                    for j in range(AHEAD):
                        fc1(p, True, B * p, j)
                    for c in range(KC):
                        turn_layernorm(2, c, it)
                    if l == 0:
                        gate_logits(it, b)
                        turn_logits(it)
                    all_read()

                return start, steps, end

            def fc1(p, first, it, j):
                if first and j % NJP == 0:
                    pe.wait_ge(S["w1_ready"], NQ * p + j // NJP + 1)
                pe.wait_ge(S["gh_done"], it * NJ + (j + 1))
                o = j * P
                for c in range(KC):
                    if j == 0:
                        pe.wait_ge(S["hs_done"], it * KC + (c + 1))
                    for n, (w, h) in enumerate(products(c, w1h, w1l, hh, hl)):
                        ins = mm(bank(j % 3), w[:, c, o:o + P], h[:, c, :], start=(c == 0 and n == 0), stop=(c == KC - 1))
                ins.then_inc(S["fc1_mm"], 1)

            def fc2(p, first, it, j):
                if first and j % NJP == 0:
                    pe.wait_ge(S["w2_ready"], NQ * p + j // NJP + 1)
                pe.wait_ge(S["gl_done"], it * NJ + (j + 4))
                for t in range(TT):
                    if j == 0:
                        pe.wait_ge(S["evac_done"], it * TT + (t + 1))
                    for n, (g, w) in enumerate(((gh, w2h), (gh, w2l), (gl, w2h))):
                        ins = mm(ps[:, 4 + t, 0:C], g[:, j % 3, t * P:(t + 1) * P], w[:, j, :], start=(j == 0 and n == 0),
                                 stop=(j == NJ - 1 and n == 2))
                ins.then_inc(S["fc2_mm"], 1)

            def mlp(p, b, first, prev, done=0):
                it = b + B * p
                for j in range(NJ):
                    if j >= done:
                        fc1(p, first, it, j)
                    if j == 1 and prev:
                        fc2(p - first, False, it - 1, NJ - 1)
                    if j >= 2:
                        fc2(p, first, it, j - 2)
                fc2(p, first, it, NJ - 2)

            def rotation_matrices():
                pe.wait_ge(S["hh_step"], HH_START + RD * (HH_FWD + HH_BWD))
                for c in range(KC):
                    ins = tr(ps[0:RD, 3, c * CW:(c + 1) * CW], U[:, c, :], ident[0:CW, 0:CW])
                ins.then_inc(S["u_tr"], 1)
                pe.wait_ge(S["u_cp"], 1)
                for b in range(B):
                    ins = mm(ps[0:RD, 4 + b, 0:C], GE[:, b, :], hU[:, :], start=True, stop=True)
                ins.then_inc(S["eu_mm"], 1)
                pe.wait_ge(S["eu_cp"], 1)

            def rotation():
                pe.wait_ge(S["evac_done"], TT * B * (NE + 1) + TT)
                for b in range(B):
                    if b in (0, B - 1):
                        pe.wait_ge(S["xm_done"], TT * (B * NE + b + 1))
                    for c in range(KC):
                        if b:
                            pe.wait_ge(S["xt_cp"], (b - 1) * KC + (c + 1))
                        for t in range(TT):
                            ins = tr(ps[0:CW, c, t * P:(t + 1) * P], xres[:, b * TT + t, c * CW:(c + 1) * CW], ident[:, :])
                        ins.then_inc(S["xt_tr"], 1)
                    if b:
                        pe.wait_ge(S["z_cp"], b)
                    for c in range(KC):
                        pe.wait_ge(S["xt_cp"], b * KC + (c + 1))
                        ins = mm(ps[0:RD, 3, :], U[:, c, :], xT[:, c, :], start=(c == 0), stop=(c == KC - 1))
                    ins.then_inc(S["z_mm"], 1)
                    pe.wait_ge(S["z_cp"], b + 1)
                    for t in range(TT):
                        if b:
                            pe.wait_ge(S["xr_done"], (b - 1) * TT + t + 1)
                        ins = mm(ps[:, 4 + t, 0:C], zT[:, t * P:(t + 1) * P], EUt[:, b, :], start=True, stop=True)
                        ins.then_inc(S["r_mm"], 1)

            for l in range(NL):
                if l == 2:
                    rotation()
                pe.wait_ge(S["ld_w"], 48 * (l + 1))
                attention_work(l, 0, False, True)[0]()
                attention_work(l, 0, False, True)[1]()
                with pe.Fori(1, B - 1) as b:
                    attention_work(l, b, True, True)[1]()
                attention_work(l, B - 1, True, False)[1]()
                attention_work(l, B - 1, True, False)[2]()
                if l == 1:
                    rotation_matrices()
                for e in range(NE if l == 0 else 1):
                    p = e if l == 0 else NE + l - 1
                    mlp(p, 0, True, e > 0, 0 if e else AHEAD)
                    with pe.Fori(1, B) as b:
                        mlp(p, b, False, True)
                fc2(p, False, B * p + B - 1, NJ - 1)

        @block.scalar
        def _(act):
            A = nc.scalar.activation
            act.sem_inc(S["exp_done"], 2)
            act.sem_inc(S["oc_done"], 1)
            act.sem_inc(S["gh_done"], 3)
            act.dma_start(xres[:, :, :], a["x"].rearrange("b (t p) c -> p (b t) c", p=P)).then_inc(S["ld_x"], 16)
            act.wait_ge(S["ld_cond"], 16)
            A(silu[0:CW, :, :], silu[0:CW, :, :], ACT.Silu).then_inc(S["silu_done"], 1)
            for n in range(8):
                act.wait_ge(S["skew_mm"], n + 1)
                if n >= 2:
                    act.wait_ge(S[f"skew_stored{n % 2}"], 16 * (n // 2))
                A(vsb[:, n % 2, :], ps[0:B, n % 4, :], ACT.Copy).then_inc(S["skew_out"], 1)
                act.wait_ge(S["skew_out"], n + 1)
                act.dma_start(vd[:, n * 512:(n + 1) * 512], vsb[:, n % 2, :]).then_inc(S[f"skew_stored{n % 2}"], 16)
            def qkv_weights_high(l):
                act.wait_ge(S["ld_w"], 48 * (l + 1))
                A(wqh[:, :, :], wqraw[:, 0:2, :], ACT.Copy).then_inc(S["wq_hi"], 1)
                A(wqt[:, :], wqraw[:, 2, :], ACT.Copy).then_inc(S["wq_hi"], 1)

            for l in range(NL):
                if l == 1:
                    qkv_weights_high(0)
                if l:
                    act.wait_ge(S["mod_stored"], 16 * l)
                    act.wait_ge(S["mod_tr"], l)
                for n in range(4):
                    act.wait_ge(S["mod_mm"], 4 * l + n + 1)
                    A(modsb[:, n * (MOD // 4):(n + 1) * (MOD // 4)], ps[0:B, 4 + n, 0:MOD // 4], ACT.Copy).then_inc(S["mod_cp"], 1)
                act.wait_ge(S["mod_cp"], 4 * l + 4)
                A(modx[:, :, :].rearrange("b s (r c) -> b s r c", c=CR), modsb[:, :].rearrange("b (s c) -> b s c", c=C)[:, :, 2 * P:C].unsqueeze(2)
                  .to_broadcast([B, 6, REP, CR]), ACT.Copy).then_inc(S["mod_rep"], 1)
                act.dma_start(modd[l], modsb[:, :]).then_inc(S["mod_stored"], 16)

            def hidden_tile(l, e, it, j):
                act.wait_ge(S["fc1_mm"], it * NJ + (j + 1))
                act.wait_ge(S["gl_done"], it * NJ + (j + 1))
                act.wait_ge(S["fc2_mm"], it * NJ + (j + 1))
                gelu, bias = ACT.Gelu if l == 2 else ACT.Gelu_apprx_tanh, cols[:, l, COL_FC + NJ * e + j:COL_FC + NJ * e + j + 1]
                A(gf[:, j % 3, :], bank(j % 3), gelu, bias=bias).then_inc(S["gf_done"], 1)
                A(gh[:, j % 3, :], bank(j % 3), gelu, bias=bias).then_inc(S["gh_done"], 1)

            def weights_high(p, k):
                act.wait_ge(S[f"ld_wp{k}"], 32 * (p + 1))
                o = slice(NJP * P * k, NJP * P * (k + 1))
                if NQ * p + k:
                    act.wait_ge(S["w1_ready"], NQ * p + k)
                A(w1h[:, :, o], w1raw[:, 0:2, o], ACT.Copy).then_inc(S["hi_w"], 1)
                A(w1t[:, :], w1raw[:, 2, o], ACT.Copy).then_inc(S["hi_w"], 1)
                A(w2h[:, NJP * k:NJP * (k + 1), :], w2raw[:, NJP * k:NJP * (k + 1), :], ACT.Copy).then_inc(S["hi_w"], 1)

            def attention_work(l, b, prev, nxt):
                G, it = b * NG + B * NG * l, b + B * l

                def high_part(i, tile):
                    act.wait_ge(S["qk_mm"], i * QT + (tile + 1))
                    if not (isinstance(i, int) and i == 0 and tile < 2):
                        act.wait_ge(S["qk_st"], i * 32 * QT + 32 * max(0, tile - 1))
                    rows = QR[tile]
                    A(qk[0:rows, tile % 2, 0, :], ps[0:rows, BANK["P", tile], :], ACT.Identity, bias=cols[0:rows, l, tile:tile + 1]).then_inc(S["hi_done"], 1)

                def maxima_out(g):
                    act.wait_ge(S["nm_tr"], G + (g + 1))
                    if not (isinstance(G, int) and G + g == 0):
                        act.wait_ge(S[f"nm_ld{(g - 1) % 2}"], G * 16 + (32 * ((g - 1) // 2) + 32))
                    A(nmT[:, :], ps[0:2 * HG, BANK["R", g % NG], :], ACT.Copy).then_inc(S["nmT_ready"], 1)

                def layernorm_out(which, c, i, bb):
                    act.wait_ge(S[f"tr{which}_done"], i * KC + (c + 1 + 2 * KC * (which == 2)))
                    if which == 1:
                        act.wait_ge(S["v_mm"], i * TT) if not (isinstance(i, int) and i == 0) else None
                        dst = hTraw[:, c, :]
                    else:
                        dst = h2T[:, c, bass.ds(bb * N, N)]
                    A(dst, ps[:, BANK[f"T{which}", c], :], ACT.Identity, bias=modcol[:, l, 2 * which - 2, c, bass.ds(bb, 1)],
                      scale=modcol[:, l, 2 * which - 1, c, bass.ds(bb, 1)]).then_inc(S[("h1r_done", "h2_ready")[which - 1]], 1)

                def split_high(c, i):
                    act.wait_ge(S["h1r_done"], i * KC + (c + 1))
                    A(hTh[:, c, :], hTraw[:, c, :], ACT.Copy).then_inc(S["h1h_done"], 1)

                def spread_reciprocals(g):
                    act.wait_ge(S["rec_done"], G + (g + 1))
                    A(rbc[:, :, :, :], rsm[:, :, :].unsqueeze(3).to_broadcast([P, TT, HG, 32]), ACT.Copy).then_inc(S["rbc_ready"], 1)

                def sums_out(g):
                    act.wait_ge(S["pv_done"], G * TT + (TT * (g + 1) + 16))
                    act.wait_ge(S["oT_ready"], G + (g + 1))
                    A(oc[:, :], bank(4), ACT.Copy).then_inc(S["oc_done"], 1)

                def exps(g, kt, which):
                    if not nxt and g == NG - 1 and kt == TT - 1 and which[0] == 0:
                        weights_high(0 if l == 0 else NE + l - 1, 0)
                    for i in which:
                        act.wait_ge(S["st_mm"], G * NU + (NU * g + kt * HG + i + 1))
                        act.wait_ge(S["pv_done"], G * TT + (TT * g + kt + 15))
                        A(pT[:, kt % 2 * HG + i, :], bank(2 + i % 2), ACT.Exp, scale=SCALE).then_inc(S["exp_done"], 1)

                def logits_out(i):
                    act.wait_ge(S["lg_mm"], i + 1)
                    A(lgT[:, :], ps[0:NE, BANK["lg", 0], :], ACT.Copy).then_inc(S["lg_cp"], 1)

                def top2_exp(i):
                    act.wait_ge(S["tk_in"], i + 1)
                    A(tk[:, 1, :, :], tk[:, 1, :, :], ACT.Exp).then_inc(S["tk_exp"], 1)

                def others(g, kt, place):
                    for kind, arg in other_work(g, kt, place, prev, nxt, l == 0):
                        if kind == "P":
                            high_part(it + (g > 0), arg)
                        elif kind == "R":
                            maxima_out(g + arg)
                        elif kind == "T1":
                            layernorm_out(1, arg, it + 1, b + 1)
                            split_high(arg, it + 1)
                        elif kind == "rb":
                            spread_reciprocals(g + arg)
                        elif kind == "T2":
                            layernorm_out(2, arg, it - 1, b - 1)
                        elif kind == "lg":
                            logits_out(it - 1)
                        elif kind == "top2":
                            top2_exp(it - 1)

                def pv(g, kt):
                    if kt == 0 and (g or prev):
                        sums_out(g - 1)

                def start():
                    for c in range(KC):
                        layernorm_out(1, c, it, b)
                        split_high(c, it)
                    for tile in range(QT - 1):
                        high_part(it, tile)
                    maxima_out(0)

                def steps():
                    walk(exps, others, pv)

                def end():
                    sums_out(NG - 1)
                    spread_reciprocals(NG - 1)
                    for j in range(AHEAD):
                        hidden_tile(l, 0, B * (0 if l == 0 else NE + l - 1), j)
                    for c in range(KC):
                        layernorm_out(2, c, it, b)
                    if l == 0:
                        logits_out(it)
                        top2_exp(it)

                return start, steps, end

            def mlp(l, e, p, b, first, last, done=0):
                it = b + B * p
                for j in range(NJ):
                    for k in weights_at(j, first, last):
                        weights_high(p + (k == 0), k)
                    if j >= done:
                        hidden_tile(l, e, it, j)

            for l in range(NL):
                if l == 2:
                    for b in range(B):
                        for c in range(KC):
                            act.wait_ge(S["xt_tr"], b * KC + c + 1)
                            if b:
                                act.wait_ge(S["z_mm"], b)
                            A(xT[:, c, :], ps[0:CW, c, :], ACT.Copy).then_inc(S["xt_cp"], 1)
                        act.wait_ge(S["z_mm"], b + 1)
                        if b:
                            act.wait_ge(S["r_mm"], b * TT)
                        A(zT[:, :], ps[0:RD, 3, :], ACT.Copy).then_inc(S["z_cp"], 1)
                act.wait_ge(S["md_step"], 18 * (l + 1))
                act.wait_ge(S["wq_ready"], l + 1)
                attention_work(l, 0, False, True)[0]()
                if l == 0:
                    act.wait_ge(S["setup_done"], 1)
                attention_work(l, 0, False, True)[1]()
                with act.Fori(1, B - 1) as b:
                    attention_work(l, b, True, True)[1]()
                attention_work(l, B - 1, True, False)[1]()
                attention_work(l, B - 1, True, False)[2]()
                if l == 1:
                    act.wait_ge(S["u_tr"], 1)
                    A(hU[:, :], ps[0:RD, 3, 0:C], ACT.Copy).then_inc(S["u_cp"], 1)
                    act.wait_ge(S["eu_mm"], 1)
                    A(EUt[:, :, :], ps[0:RD, 4:8, 0:C], ACT.Copy).then_inc(S["eu_cp"], 1)
                passes = NE if l == 0 else 1
                for e in range(passes):
                    p = e if l == 0 else NE + l - 1
                    mlp(l, e, p, 0, True, False, 0 if e else AHEAD)
                    with act.Fori(1, B - 1) as b:
                        mlp(l, e, p, b, False, False)
                    if e + 1 == passes and l + 1 < NL:
                        qkv_weights_high(l + 1)
                    mlp(l, e, p, B - 1, False, e + 1 < passes)

        @block.vector
        def _(dve):
            V = nc.vector
            dve.sem_inc(S["evac_done"], TT)
            dve.sem_inc(S["oT_ready"], 1)
            dve.sem_inc(S["gl_done"], 3)
            V.memset(silu[CW:CW + 1, :, :], 1.0).then_inc(S["silu_done"], 1)
            V.memset(vaug[:, :, :, :], 1.0)
            dve.wait_ge(S["ld_const"], 16 * 8)
            def layernorm(which, i, b, eps, parts, xn_free=None):
                ln = S[f"ln{which}_step"]
                k = [{"a": 0, "b": 2, "c": TT, "d": TT + 7, "e": TT + 10, "f": TT + 13, "g": LN_STEPS, "h": LN_STEPS}[parts[0]]]

                def step(ins, wait=True):
                    k[0] += 1
                    ins.then_inc(ln, 1)
                    if wait:
                        wait_alone(dve, ln, i * LN_STEPS + k[0], S["dve_passed"])

                var, y, u, w = (nwt[:, n, :] for n in range(4))
                for part in parts:
                    if part in "ab":
                        for t in (0, 1) if part == "a" else (2, 3):
                            step(V.bn_stats(stats[:, t, :], xrow(b, t)), t == TT - 1)
                    if part == "c":
                        for t in range(TT):
                            step(V.bn_aggr(mv[:, t, :], stats[:, t, :]), t == TT - 1)
                        step(V.tensor_scalar(var, mv[:, :, 1], eps, None, ALU.add))
                        step(V.tensor_scalar(u.bitcast(I32), var.bitcast(I32), 1, None, ALU.logical_shift_right))
                        step(V.tensor_scalar(y.bitcast(I32), u.bitcast(I32), -1.0, float(RSQRT_MAGIC), ALU.mult, ALU.add))
                    if part in "def":
                        step(V.tensor_tensor(u, y, y, ALU.mult))
                        step(V.scalar_tensor_tensor(out=w, in0=u, scalar=-0.5, in1=var, op0=ALU.mult, op1=ALU.mult))
                        step(V.scalar_tensor_tensor(out=y, in0=w, scalar=1.5, in1=y, op0=ALU.add, op1=ALU.mult))
                    if part == "g":
                        assert k[0] == LN_STEPS, k
                        if xn_free:
                            dve.wait_ge(*xn_free)
                    if part in "gh":
                        for t in (0, 1) if part == "g" else (2, 3):
                            V.tensor_scalar(xn[:, t, 0:C], xrow(b, t), mv[:, t, 0:1], y[:, t:t + 1],
                                            ALU.subtract, ALU.mult).then_inc(S[f"xn{which}_ready"], 1)
                    if part == "h":
                        dve.wait_ge(S[f"xn{which}_ready"], i * TT + TT)
                        V.tensor_copy(xn[:, :, C:KC * P].rearrange("p t (r c) -> p t r c", c=CR),
                                      xn[:, :, 2 * P:C].unsqueeze(2).to_broadcast([P, TT, REP - 1, CR])).then_inc(S[f"xc{which}_ready"], 1)

            def xrow(b, t):
                return xres[:, bass.ds(b * TT + t, 1), :].rearrange("p a n -> p (a n)")

            dve.wait_ge(S["ld_x"], 16)
            layernorm(1, 0, 0, EPS[0], "abcdefgh")
            for l in range(NL):
                dve.wait_ge(S["mod_tr"], l + 1)
                tp = ps[:, 0, 0:4 * KC * B].rearrange("p (s c b) -> p s c b", s=4, c=KC)
                for s in (0, 2):
                    for c in range(KC):
                        lnw = cols[:, l, COL_LN + 3 * s + c:COL_LN + 3 * s + c + 1]
                        lnb = cols[:, l, COL_LN + 3 * s + KC + c:COL_LN + 3 * s + KC + c + 1]
                        V.tensor_scalar(modcol[:, l, s + 1, c, :], tp[:, s + 1, c, :], 1.0, lnw, ALU.add, ALU.mult).then_inc(S["md_step"], 1)
                        V.tensor_scalar(stats[:, 0, 0:B], tp[:, s + 1, c, :], 1.0, lnb, ALU.add, ALU.mult).then_inc(S["md_step"], 1)
                        k = (l * 2 + s // 2) * KC + c
                        dve.wait_ge(S["md_step"], 3 * k + 2)
                        V.tensor_tensor(modcol[:, l, s, c, :], stats[:, 0, 0:B], tp[:, s, c, :], ALU.add).then_inc(S["md_step"], 1)
                        dve.wait_ge(S["md_step"], 3 * k + 3)
            def qkv_weights_low(l):
                dve.wait_ge(S["wq_hi"], 2 * (l + 1))
                V.tensor_tensor(wql[:, 0:2, :], wqraw[:, 0:2, :], wqh[:, :, :].bitcast(F32), ALU.subtract)
                V.scalar_tensor_tensor(out=wql[:, 2, :], in0=wqt[:, :].bitcast(F32), scalar=masks[:, 1:2], in1=wqraw[:, 2, :],
                                       op0=ALU.mult, op1=ALU.add).then_inc(S["wq_ready"], 1)

            dve.wait_ge(S["ld_skew"], 16)
            dve.wait_ge(S["sk_tr"], 1)
            vt = ps[0:RD, 1, 0:B * RD].rearrange("p (b j) -> p b j", b=B)
            V.tensor_tensor(skew[:, :, :], skew[:, :, :], vt, ALU.subtract).then_inc(S["sk_dve"], 1)
            dve.wait_ge(S["sk_dve"], 1)
            for h in range(2):
                V.tensor_scalar(sx[:, h, :, :], skew[:, :, :], (1 - 2 * h) * 2.0 ** -DOUBLINGS, None, ALU.mult).then_inc(S["sk_dve"], 1)
            dve.wait_ge(S["sk_dve"], 3)

            def flat(t):
                return t.rearrange("p h b j -> p (h b j)")

            V.scalar_tensor_tensor(out=flat(ey[:, 0]), in0=flat(sx[:, :, :, :]), scalar=1.0 / TAYLOR, in1=flat(eye8[:, :, :, :]),
                                   op0=ALU.mult, op1=ALU.add).then_inc(S["ex_ev"], 1)
            for i in range(TAYLOR - 1):
                k = TAYLOR - 1 - i
                dve.wait_ge(S["ex_mm"], i + 1)
                if k > 1:
                    V.scalar_tensor_tensor(out=flat(ey[:, (i + 1) % 2]), in0=ps[0:RD, 2 + i % 2, :], scalar=1.0 / k,
                                           in1=flat(eye8[:, :, :, :]), op0=ALU.mult, op1=ALU.add).then_inc(S["ex_ev"], 1)
                else:
                    V.tensor_copy(flat(ey[:, (i + 1) % 2]), ps[0:RD, 2 + i % 2, :]).then_inc(S["ex_ev"], 1)
            qkv_weights_low(0)

            def double(n):
                dve.wait_ge(S["ex_mm"], TAYLOR + n)
                dve.wait_ge(S["ex_ev"], TAYLOR + n)
                q = (TAYLOR - 1 + n) % 2
                V.scalar_tensor_tensor(out=flat(ey[:, 1 - q]), in0=flat(ey[:, q]), scalar=2.0, in1=ps[0:RD, 2 + q, :],
                                       op0=ALU.mult, op1=ALU.add).then_inc(S["ex_ev"], 1)

            def expm_out():
                dve.wait_ge(S["ex_ev"], TAYLOR + DOUBLINGS)
                V.tensor_copy(GE[:, :, :], ey[:, (TAYLOR - 1 + DOUBLINGS) % 2, 1, :, :]).then_inc(S["setup_done"], 1)

            def gate_row(b):
                return gates[:, bass.ds(b, 1), :].rearrange("p a n -> p (a n)")

            def hidden_low(it, j):
                dve.wait_ge(S["gh_done"], it * NJ + (j + 4))
                V.tensor_tensor(gl[:, j % 3, :], gf[:, j % 3, :], gh[:, j % 3, :].bitcast(F32), ALU.subtract).then_inc(S["gl_done"], 1)

            def split_input(i, b):
                if not (isinstance(i, int) and i == 0):
                    dve.wait_ge(S["fc1_mm"], i * NJ)
                for c in range(KC):
                    V.tensor_copy(hh[:, c, :], h2T[:, c, bass.ds(b * N, N)]).then_inc(S["hh_done"], 1)
                for c in range(KC):
                    dve.wait_ge(S["hh_done"], i * KC + (c + 1))
                    src = h2T[:, c, bass.ds(b * N, N)]
                    if c < 2:
                        V.tensor_tensor(hl[:, c, :], src, hh[:, c, :].bitcast(F32), ALU.subtract).then_inc(S["hs_done"], 1)
                    else:
                        V.scalar_tensor_tensor(out=hl[:, c, :], in0=hh[:, c, :].bitcast(F32), scalar=masks[:, 0:1], in1=src,
                                               op0=ALU.mult, op1=ALU.add).then_inc(S["hs_done"], 1)

            def weights_low(p, k):
                o, q = slice(NJP * P * k, NJP * P * (k + 1)), slice(NJP * k, NJP * (k + 1))
                n = 3 * (NQ * p + k)
                dve.wait_ge(S["hi_w"], n + 2)
                V.tensor_tensor(w1l[:, 0:2, o], w1raw[:, 0:2, o], w1h[:, :, o].bitcast(F32), ALU.subtract)
                V.scalar_tensor_tensor(out=w1l[:, 2, o], in0=w1t[:, :].bitcast(F32), scalar=masks[:, 1:2], in1=w1raw[:, 2, o],
                                       op0=ALU.mult, op1=ALU.add).then_inc(S["w1_ready"], 1)
                dve.wait_ge(S["hi_w"], n + 3)
                V.tensor_tensor(w2l[:, q, :], w2raw[:, q, :], w2h[:, q, :].bitcast(F32), ALU.subtract).then_inc(S["w2_ready"], 1)

            def attention_work(l, b, prev, nxt):
                G, it = b * NG + B * NG * l, b + B * l

                def low_part(i, tile):
                    dve.wait_ge(S["hi_done"], i * QT + (tile + 1))
                    rows, slot = QR[tile], tile % 2
                    V.scalar_tensor_tensor(out=qk[0:rows, slot, 1, :], in0=ps[0:rows, BANK["P", tile], :], scalar=cols[0:rows, l, tile:tile + 1],
                                           in1=qk[0:rows, slot, 0, :].bitcast(F32), op0=ALU.add, op1=ALU.subtract).then_inc(S["lo_done"], 1)

                def split_h1(i, c):
                    dve.wait_ge(S["h1h_done"], i * KC + (c + 1))
                    if c < 2:
                        V.tensor_tensor(hTl[:, c, :], hTraw[:, c, :], hTh[:, c, :].bitcast(F32), ALU.subtract).then_inc(S["h1_ready"], 1)
                    else:
                        V.scalar_tensor_tensor(out=hTl[:, c, :], in0=hTh[:, c, :].bitcast(F32), scalar=masks[:, 0:1], in1=hTraw[:, c, :],
                                               op0=ALU.mult, op1=ALU.add).then_inc(S["h1_ready"], 1)

                def maxima(g, qt, which, first):
                    for i in which:
                        dve.wait_ge(S["max_mm"], G * NU + (NU * g + qt * HG + i + 1))
                        V.tensor_reduce(mx[:, g % NG, qt, i:i + 1], bank(MAX_BANKS[(NU * g + qt * HG + i - first) % 3]), AX.X, ALU.max).then_inc(S["mx_done"], 1)

                def negate(g):
                    dve.wait_ge(S["mx_done"], G * NU + NU * (g + 1))
                    V.tensor_scalar(nm[:, g % NG, :, 0:HG], mx[:, g % NG, :, :], -1.0, None, ALU.mult).then_inc(S["nh_done"], 1)
                    dve.wait_ge(S["nh_done"], G + (g + 1))
                    V.scalar_tensor_tensor(out=nm[:, g % NG, :, HG:2 * HG], in0=mx[:, g % NG, :, :], scalar=-1.0,
                                           in1=nm[:, g % NG, :, 0:HG].bitcast(F32), op0=ALU.mult, op1=ALU.subtract).then_inc(S["nm_ready"], 1)

                def v_out(t):
                    dve.wait_ge(S["v_mm"], it * TT + (t + 1))
                    dve.wait_ge(S["pv_done"], it * 16 + 16)
                    V.tensor_tensor(vaug[:, t, :, 0:HD], ps[:, BANK["V", t], 0:C].rearrange("p (h d) -> p h d", h=NH),
                                    vbias[:, :].rearrange("p (h d) -> p h d", h=NH), ALU.add).then_inc(S["v_ready"], 1)

                def reciprocals(g):
                    dve.wait_ge(S["on_mm"], G + (g + 1))
                    V.reciprocal(rsm[:, :, :].rearrange("p t h -> p (t h)"), ps[:, BANK["on", g % NG], 0:NU]).then_inc(S["rec_done"], 1)

                def normalise(g):
                    dve.wait_ge(S["ob_tr"], G + (g + 1))
                    V.tensor_tensor(oT[:, g % NG, :], ps[:, BANK["ob", g % NG], :], oc[:, :], ALU.mult).then_inc(S["oT_ready"], 1)

                def residual(t, i, bb):
                    dve.wait_ge(S["pj_mm"], i * TT + (t + 1))
                    V.tensor_tensor(tmpx[:, :], ps[:, BANK["pj", t], 0:C], gate_row(bb), ALU.mult).then_inc(S["xa_g"], 1)
                    dve.wait_ge(S["xa_g"], i * TT + (t + 1))
                    V.tensor_tensor(xrow(bb, t), xrow(bb, t), tmpx[:, :], ALU.add).then_inc(S["xa_done"], 1)
                    dve.wait_ge(S["xa_done"], i * TT + (t + 1))

                def tiles(g, kt, which):
                    if not nxt and g == NG - 1 and kt == TT - 1 and which[0] == 0:
                        weights_low(0 if l == 0 else NE + l - 1, 0)
                    if g + 2 < NG or nxt:
                        maxima(g + 2, kt, which, 2 * NU)
                        if kt == TT - 1 and which[-1] == HG - 1:
                            negate(g + 2)

                def others(g, kt, place):
                    for kind, arg in other_work(g, kt, place, prev, nxt, l == 0):
                        if kind == "P":
                            low_part(it + (g > 0), arg)
                        elif kind == "T1":
                            split_h1(it + 1, arg)
                        elif kind == "on":
                            reciprocals(g + arg)
                        elif kind == "ob":
                            normalise(g + arg)
                        elif kind == "V":
                            v_out(arg)
                        elif kind[:3] == "LN1":
                            layernorm(1, it + 1, b + 1, EPS[l], kind[3], (S["tr2_done"], it * KC + KC))
                        elif kind == "pj":
                            residual(arg, it - 1, b - 1)
                        elif kind[:3] == "LN2":
                            layernorm(2, it - 1, b - 1, EPS[l], kind[3], (S["tr1_done"], it * KC + (2 * KC if nxt else KC)))
                        elif kind == "top2":
                            top2(b - 1, BANK["lt", 0])

                def start():
                    for c in range(KC):
                        split_h1(it, c)
                        if l == 0:
                            double(c)
                    for tile in range(QT - 1):
                        low_part(it, tile)
                        if l == 0:
                            double(KC + tile)
                    for g in range(2):
                        for qt in range(TT):
                            maxima(g, qt, range(HG), 0)
                            if l == 0 and TT * g + qt < DOUBLINGS - KC - QT + 1:
                                double(KC + QT - 1 + TT * g + qt)
                        negate(g)
                    if l == 0:
                        expm_out()

                def steps():
                    walk(tiles, others, lambda g, kt: None)

                def end():
                    reciprocals(NG - 1)
                    normalise(NG - 1)
                    dve.wait_ge(S["st_mm"], NU * NG * B * (l + 1))
                    dve.wait_ge(S["h2_ready"], KC * (B * l + 1))
                    split_input(B * (0 if l == 0 else NE + l - 1), 0)
                    for t in range(TT):
                        residual(t, it, b)
                    layernorm(2, it, b, EPS[l], "abcdefgh", (S["tr1_done"], it * KC + KC))
                    for j in range(AHEAD):
                        hidden_low(B * (0 if l == 0 else NE + l - 1), j)
                    if l == 0:
                        top2(b, BANK["lt", 0])

                return start, steps, end

            def top2(b, lt_bank):
                k = [0]

                def step(ins, wait=True):
                    k[0] += 1
                    ins.then_inc(S["tk_step"], 1)
                    if wait:
                        dve.wait_ge(S["tk_step"], b * 9 + k[0])

                dve.wait_ge(S["lg_tr"], b + 1)
                lg, e1, rank, sel = (tk[:, i, :, :] for i in range(4))
                gt, eq = tkc[:, 0, :, :, :], tkc[:, 1, :, :, :]
                step(V.tensor_copy(lg, ps[:, lt_bank, 0:TT * NE].rearrange("p (t e) -> p t e", t=TT)))
                step(V.tensor_reduce(tkm[:, 0, :], lg, AX.X, ALU.max))
                V.tensor_tensor(e1, lg, tkm[:, 0, :].unsqueeze(2).to_broadcast([P, TT, NE]), ALU.subtract).then_inc(S["tk_in"], 1)
                me = lg.unsqueeze(3).to_broadcast([P, TT, NE, NE])
                other = lg.unsqueeze(2).to_broadcast([P, TT, NE, NE])
                step(V.tensor_tensor(gt, other, me, ALU.is_gt), False)
                step(V.tensor_tensor(eq, other, me, ALU.is_equal))
                step(V.tensor_tensor(eq, eq, lowmask[:, :, :, :], ALU.mult))
                step(V.tensor_tensor(gt, gt, eq, ALU.add))
                step(V.tensor_reduce(rank, gt, AX.X, ALU.add))
                dve.wait_ge(S["tk_exp"], b + 1)
                step(V.scalar_tensor_tensor(out=sel.rearrange("p t e -> p (t e)"), in0=rank.rearrange("p t e -> p (t e)"), scalar=1.5,
                                            in1=e1.rearrange("p t e -> p (t e)"), op0=ALU.is_lt, op1=ALU.mult))
                step(V.tensor_reduce(tkm[:, 1, :], sel, AX.X, ALU.add))
                V.reciprocal(tkm[:, 0, :], tkm[:, 1, :]).then_inc(S["tk_r"], 1)
                dve.wait_ge(S["tk_r"], b + 1)
                V.tensor_tensor(cw[:, bass.ds(b * TT, TT), :], sel, tkm[:, 0, :].unsqueeze(2).to_broadcast([P, TT, NE]),
                                ALU.mult).then_inc(S["cw_ready"], 1)
                assert k[0] == 9, k

            def bias_out(p, i):
                dve.wait_ge(S["fc2_mm"], i * NJ + (NJ + 3))
                if not (isinstance(i, int) and i == 0):
                    dve.wait_ge(S["xm_done"], i * TT)
                for t in range(TT):
                    V.tensor_tensor(tmp[:, t, :], ps[:, 4 + t, 0:C], b2b[:, p % 2, :], ALU.add).then_inc(S["evac_done"], 1)

            def add_mlp(l, e, i, b, t):
                dve.wait_ge(S["evac_done"], i * TT + (TT + t + 1))
                src = tmp[:, t, :]
                if l == 0:
                    V.scalar_tensor_tensor(out=src, in0=src, scalar=cw[:, bass.ds(b * TT + t, 1), e:e + 1].rearrange("p a n -> p (a n)"),
                                           in1=gate_row(b), op0=ALU.mult, op1=ALU.mult).then_inc(S["gm_done"], 1)
                else:
                    V.tensor_tensor(src, src, gate_row(b), ALU.mult).then_inc(S["gm_done"], 1)
                dve.wait_ge(S["gm_done"], i * TT + (t + 1))
                V.tensor_tensor(xrow(b, t), xrow(b, t), src, ALU.add).then_inc(S["xm_done"], 1)

            def mlp(l, e, p, b, prev, next_batch, first, last, ahead=False, done=0):
                it = b + B * p
                for j in range(NJ):
                    for k in weights_at(j, first, last):
                        weights_low(p + (k == 0), k)
                    if j == NJ - 1 and next_batch is not None:
                        split_input(it + 1, next_batch)
                    if ahead and j < 8:
                        if j == 0:
                            dve.wait_ge(S["xm_done"], TT * B * (NE - 1) + TT)
                        layernorm(1, B * (l + 1), 0, EPS[l + 1], "abcdefgh"[j])
                    if j >= done:
                        hidden_low(it, j)
                    if prev is not None:
                        if j == 1:
                            bias_out(prev[0], it - 1)
                        if 2 <= j < 2 + TT:
                            add_mlp(l, prev[1], it - 1, prev[2], j - 2)

            dve.wait_ge(S["mod_stored"], 16 * NL)
            for l in range(NL):
                if l == 2:
                    for b in range(B):
                        for t in range(TT):
                            dve.wait_ge(S["r_mm"], b * TT + t + 1)
                            V.tensor_tensor(xres[:, b * TT + t, :], xres[:, b * TT + t, :], ps[:, 4 + t, 0:C], ALU.add).then_inc(S["xr_done"], 1)
                        if b < 2:
                            dve.wait_ge(S["xr_done"], TT)
                            layernorm(1, B * l, 0, EPS[l], ("abcd", "efgh")[b])
                dve.wait_ge(S["ld_gate"], 32 * l + 16)
                dve.wait_ge(S["ld_w"], 48 * (l + 1))
                attention_work(l, 0, False, True)[0]()
                attention_work(l, 0, False, True)[1]()
                with dve.Fori(1, B - 1) as b:
                    attention_work(l, b, True, True)[1]()
                attention_work(l, B - 1, True, False)[1]()
                attention_work(l, B - 1, True, False)[2]()
                dve.wait_ge(S["ld_gate"], 32 * l + 32)
                dve.wait_ge(S["h2_ready"], KC * B * (l + 1))
                passes = NE if l == 0 else 1
                for e in range(passes):
                    p = e if l == 0 else NE + l - 1
                    dve.wait_ge(S["ld_b2"], 16 * (p + 1))
                    mlp(l, e, p, 0, (p - 1, e - 1, B - 1) if e else None, 1, True, False, False, 0 if e else AHEAD)
                    with dve.Fori(1, B - 1) as b:
                        mlp(l, e, p, b, (p, e, b - 1), b + 1, False, False)
                    if e + 1 == passes and l + 1 < NL:
                        qkv_weights_low(l + 1)
                    mlp(l, e, p, B - 1, (p, e, B - 2), 0 if e + 1 < passes else None, False, e + 1 < passes,
                        l == 0 and e + 1 == passes)
                bias_out(p, B * p + B - 1)
                for t in range(TT):
                    add_mlp(l, e, B * p + B - 1, B - 1, t)


def kernel(**inputs):
    import concourse.bacc as bacc
    from concourse.bass_utils import run_bass_kernel_spmd

    x = {k: np.asarray(v) for k, v in inputs.items()}
    f = np.float32

    def split_heads(w, bias):
        o = np.zeros((NH, 32, C), f)
        o[:, :HD] = w.reshape(NH, HD, C)
        o[0, HD] = bias
        return o.reshape(NG, P, C)

    def chunks(w, times):
        o = np.zeros((KC, P, w.shape[1]), f)
        o[0:2] = w[:2 * P].reshape(2, P, -1)
        for i in range(times):
            o[2, CR * i:CR * (i + 1)] = w[2 * P:]
        return o

    def by_group(w):
        qk = w[:, :2 * C].reshape(-1, 2, NG, HG * HD).transpose(0, 2, 1, 3).reshape(-1, 2 * C)
        return np.concatenate([qk, w[:, 2 * C:]], 1)

    qkv_w = [x["L0_cond_w_qkv"], x["L1_cond_W_qkv"], np.concatenate([x["L3_cond_wq"], x["L3_cond_wk"], x["L3_cond_wv"]], 1)]
    qkv_b = [x["L0_cond_b_qkv"], x["L1_cond_b_qkv"], np.zeros(3 * C, f)]
    proj_w = [x["L0_cond_w_proj"], x["L1_cond_W_proj"], x["L3_cond_wo"]]
    proj_b = [x["L0_cond_b_proj"], x["L1_cond_b_proj"], x["L3_cond_wo_b"]]
    ada_w = [x["L0_cond_w_adaln"], x["L1_cond_W_ada"], x["L3_cond_ada_w"]]
    ada_b = [x["L0_cond_b_adaln"], x["L1_cond_b_ada"], x["L3_cond_ada_b"]]
    fc1_b = [x["L0_cond_b1"], x["L1_cond_b_fc1"][None], x["L3_cond_fc1_b"][None]]
    one, zero = np.ones(C, f), np.zeros(C, f)
    ln = [(one, zero, one, zero)] * 2 + [(x["L3_cond_ln1_w"], x["L3_cond_ln1_b"], x["L3_cond_ln2_w"], x["L3_cond_ln2_b"])]
    cols = np.zeros((P, NL, NCOL), f)
    for l in range(NL):
        for i in range(QT):
            cols[:QR[i], l, i] = by_group(qkv_b[l][None])[0, HT * HD * i:HT * HD * i + QR[i]]
        for i, v in enumerate(ln[l]):
            cols[:, l, COL_LN + KC * i:COL_LN + KC * (i + 1)] = chunks(v[:, None], REP)[:, :, 0].T
        for e, v in enumerate(fc1_b[l]):
            cols[:, l, COL_FC + NJ * e:COL_FC + NJ * (e + 1)] = v.reshape(NJ, P).T
    iu, ju = np.triu_indices(RD, k=1)
    w_skew = np.zeros((C + 1, RD * RD), f)
    w_skew[:C, iu * RD + ju] = x["L2_cond_W"].T
    w_skew[C, iu * RD + ju] = x["L2_cond_b"]
    low = np.zeros((P, TT, NE, NE), f)
    low[:, :] = np.tril(np.ones((NE, NE), f), -1)
    selden = np.zeros((P, HG), f)
    selden[32 * np.arange(HG) + HD, np.arange(HG)] = 1
    masks = np.zeros((P, 2), f)
    masks[32:64, 0] = masks[96:, 0] = masks[64:, 1] = -1
    eye8 = np.zeros((RD, 2, B, RD), f)
    eye8[np.arange(RD), :, :, np.arange(RD)] = 1
    arrays = {
        "x": x["x"], "condT": x["cond_1152"].T, "w_gate": chunks(x["L0_cond_w_gate"], 1),
        "w_ada": np.stack([np.concatenate([w, b[None]], 0) for w, b in zip(ada_w, ada_b)]),
        "w_skew": w_skew, "P": x["L2_cond_P"], "cols": cols,
        "wqkv": np.stack([chunks(by_group(w), REP) for w in qkv_w]), "wproj": np.stack([split_heads(w, b) for w, b in zip(proj_w, proj_b)]),
        "vbias": np.stack([qb[2 * C:] for qb in qkv_b]),
        "w1": np.stack([chunks(w, REP) for w in (*x["L0_cond_w1"], x["L1_cond_W_fc1"], x["L3_cond_fc1_w"])]),
        "w2": np.concatenate([x["L0_cond_w2"], x["L1_cond_W_fc2"][None], x["L3_cond_fc2_w"][None]]),
        "b2": np.concatenate([x["L0_cond_b2"], x["L1_cond_b_fc2"][None], x["L3_cond_fc2_b"][None]]),
        "ident": np.eye(P, dtype=f), "lowmask": low, "ones": np.ones((2, CR), f), "eye8": eye8, "selden": selden, "masks": masks,
    }
    arrays = {k: np.ascontiguousarray(v) for k, v in arrays.items()}
    nc = bacc.Bacc("TRN2", target_bir_lowering=False, num_devices=1)
    aps = {k: nc.dram_tensor(f"in_{k}", v.shape, mybir.dt.from_np(v.dtype), kind="ExternalInput").ap() for k, v in arrays.items()}
    out = nc.dram_tensor("out", (B, N, C), F32, kind="ExternalOutput").ap()
    bass_cond_seq_kernel(nc, aps, out)
    r = run_bass_kernel_spmd(nc, [{f"in_{k}": v for k, v in arrays.items()}], core_ids=[0])
    return r.results[0]["out"]
```
